# Optimizing a Trainium2 kernel written in Bass

```python
import numpy as np
import jax
import jax.numpy as jnp

def _softmax(x, axis=-1):
    return jax.nn.softmax(x, axis=axis)

def _gelu(x):
    return jax.nn.gelu(x, approximate=True)

def _silu(x):
    return jax.nn.silu(x)

def _sigmoid(x):
    return jax.nn.sigmoid(x)

def _layernorm(x, axis=-1, eps=1e-05):
    m = jnp.mean(x, axis=axis, keepdims=True)
    v = jnp.var(x, axis=axis, keepdims=True)
    return (x - m) / jnp.sqrt(v + eps)

def _scatter_add(tgt, idx, src, axis=0):
    return tgt.at[idx].add(src)

def _segment_sum(src, seg, n):
    return jax.ops.segment_sum(src, seg, n)
kernel_name = 'mk_seq_preln_d2_jaxref_r4_58330f'

def setup_inputs(seed: int=0):
    np.random.seed(seed)
    _w = jnp.asarray

    def _L0_attn_setup():
        import jax, jax.numpy as jnp
        import numpy as np
        key = jax.random.key(seed)
        k1, k2, k3, k4 = jax.random.split(key, 4)
        B, T, E, H = (4, 512, 256, 16)
        hs = E // H
        x = jax.random.normal(k1, (B, T, E), dtype=jnp.float32)
        s = 1.0 / np.sqrt(E)
        Wq = jax.random.uniform(k2, (H, E, hs), dtype=jnp.float32, minval=-s, maxval=s)
        Wk = jax.random.uniform(k3, (H, E, hs), dtype=jnp.float32, minval=-s, maxval=s)
        Wv = jax.random.uniform(k4, (H, E, hs), dtype=jnp.float32, minval=-s, maxval=s)
        return {'x': x, 'Wq': Wq, 'Wk': Wk, 'Wv': Wv}
    _L0_attn_in = _L0_attn_setup()

    def _L0_ffn_setup():
        import jax, jax.numpy as jnp
        import numpy as np
        B, T, D = (2, 512, 256)
        DCD = 1024
        RET = 128
        NEXP = 1024
        NKEYS = 64
        H = 4
        KPH = 8
        key = jax.random.key(seed)
        ks = jax.random.split(key, 10)
        s = lambda k, shape, scale: jax.random.normal(k, shape, jnp.float32) * scale
        return {'hidden_states': jax.random.normal(ks[0], (B, T, D), jnp.float32), 'Wg': s(ks[1], (D, DCD), 0.02), 'bg': jnp.zeros((DCD,), jnp.float32), 'Wu': s(ks[2], (D, DCD), 0.02), 'bu': jnp.zeros((DCD,), jnp.float32), 'Wd': s(ks[3], (DCD, D), 0.02), 'bd': jnp.zeros((D,), jnp.float32), 'Wq': s(ks[4], (D, RET * H), 0.02), 'keys': s(ks[5], (H, NKEYS, 2, RET // 2), 0.02), 'down_embed': s(ks[6], (NEXP, D), 0.02), 'up_embed': s(ks[7], (NEXP, D), 0.02)}
    _L0_ffn_in = _L0_ffn_setup()

    def _L1_attn_setup():
        import jax, jax.numpy as jnp
        import numpy as np
        B, S, DIM, HD = (64, 200, 256, 128)
        BASE = 10000.0

        def _rope(t, cos, sin):
            tr = t[..., 0::2]
            ti = t[..., 1::2]
            rr = tr * cos - ti * sin
            ri = tr * sin + ti * cos
            return jnp.stack([rr, ri], axis=-1).reshape(t.shape)
        key = jax.random.key(seed)
        ks = jax.random.split(key, 5)
        x = jax.random.normal(ks[0], (B, S, DIM), jnp.float32)
        si = DIM ** (-0.5)
        so = HD ** (-0.5)
        wq = jax.random.normal(ks[1], (HD, DIM), jnp.float32) * si
        wk = jax.random.normal(ks[2], (HD, DIM), jnp.float32) * si
        wv = jax.random.normal(ks[3], (HD, DIM), jnp.float32) * si
        wo = jax.random.normal(ks[4], (DIM, HD), jnp.float32) * so
        return {'x': x, 'wq': wq, 'wk': wk, 'wv': wv, 'wo': wo}
    _L1_attn_in = _L1_attn_setup()

    def _L1_ffn_setup():
        import jax, jax.numpy as jnp
        import numpy as np
        BS, L, D = (4, 512, 256)
        H, E, K = (8, 16, 2)
        HD = D // H
        I = 1024 // H
        key = jax.random.key(seed)
        ks = jax.random.split(key, 10)
        s = lambda k, shp, fan: jax.random.normal(k, shp, jnp.float32) / np.sqrt(fan)
        return {'x': jax.random.normal(ks[0], (BS, L, D), jnp.float32), 'Wm': s(ks[1], (D, D), D), 'bm': jnp.zeros((D,), jnp.float32), 'expert_emb': jax.random.normal(ks[2], (HD, E), jnp.float32), 'W1': s(ks[3], (E, HD, I), HD), 'b1': jnp.zeros((E, I), jnp.float32), 'W2': s(ks[4], (E, I, HD), I), 'b2': jnp.zeros((E, HD), jnp.float32), 'Wo': s(ks[5], (D, D), D), 'bo': jnp.zeros((D,), jnp.float32)}
    _L1_ffn_in = _L1_ffn_setup()
    _d = {'L0_attn_x': _L0_attn_in['x'], 'L0_attn_Wq': _L0_attn_in['Wq'], 'L0_attn_Wk': _L0_attn_in['Wk'], 'L0_attn_Wv': _L0_attn_in['Wv'], 'L0_ffn_Wg': _L0_ffn_in['Wg'], 'L0_ffn_bg': _L0_ffn_in['bg'], 'L0_ffn_Wu': _L0_ffn_in['Wu'], 'L0_ffn_bu': _L0_ffn_in['bu'], 'L0_ffn_Wd': _L0_ffn_in['Wd'], 'L0_ffn_bd': _L0_ffn_in['bd'], 'L0_ffn_Wq': _L0_ffn_in['Wq'], 'L0_ffn_keys': _L0_ffn_in['keys'], 'L0_ffn_down_embed': _L0_ffn_in['down_embed'], 'L0_ffn_up_embed': _L0_ffn_in['up_embed'], 'L1_attn_wq': _L1_attn_in['wq'], 'L1_attn_wk': _L1_attn_in['wk'], 'L1_attn_wv': _L1_attn_in['wv'], 'L1_attn_wo': _L1_attn_in['wo'], 'L1_ffn_Wm': _L1_ffn_in['Wm'], 'L1_ffn_bm': _L1_ffn_in['bm'], 'L1_ffn_expert_emb': _L1_ffn_in['expert_emb'], 'L1_ffn_W1': _L1_ffn_in['W1'], 'L1_ffn_b1': _L1_ffn_in['b1'], 'L1_ffn_W2': _L1_ffn_in['W2'], 'L1_ffn_b2': _L1_ffn_in['b2'], 'L1_ffn_Wo': _L1_ffn_in['Wo'], 'L1_ffn_bo': _L1_ffn_in['bo']}
    _x0 = _d['L0_attn_x']
    _d['L0_attn_x'] = jax.random.normal(jax.random.fold_in(jax.random.key(seed), 1), (8, 1024, 256), dtype=_x0.dtype)
    del _x0
    return _d

def reference(L0_attn_x, L0_attn_Wq, L0_attn_Wk, L0_attn_Wv, L0_ffn_Wg, L0_ffn_bg, L0_ffn_Wu, L0_ffn_bu, L0_ffn_Wd, L0_ffn_bd, L0_ffn_Wq, L0_ffn_keys, L0_ffn_down_embed, L0_ffn_up_embed, L1_attn_wq, L1_attn_wk, L1_attn_wv, L1_attn_wo, L1_ffn_Wm, L1_ffn_bm, L1_ffn_expert_emb, L1_ffn_W1, L1_ffn_b1, L1_ffn_W2, L1_ffn_b2, L1_ffn_Wo, L1_ffn_bo):

    def _L0_attn_ref(x, Wq, Wk, Wv):
        import jax, jax.numpy as jnp
        import numpy as np
        B, T, E = x.shape
        H = Wq.shape[0]
        q = jnp.einsum('bte,hed->bhtd', x, Wq)
        k = jnp.einsum('bte,hed->bhtd', x, Wk)
        v = jnp.einsum('bte,hed->bhtd', x, Wv)
        scores = jnp.einsum('bhtd,bhsd->bhts', q, k)
        causal = jnp.tril(jnp.ones((T, T), dtype=bool))
        scores = jnp.where(causal, scores, -jnp.inf)
        scores = scores / jnp.sqrt(jnp.asarray(E, dtype=scores.dtype))
        w = jax.nn.softmax(scores, axis=-1)
        out = jnp.einsum('bhts,bhsd->bhtd', w, v)
        out = jnp.transpose(out, (0, 2, 1, 3)).reshape(B, T, -1)
        return out

    def _L0_ffn_ref(hidden_states, Wg, bg, Wu, bu, Wd, bd, Wq, keys, down_embed, up_embed):
        import jax, jax.numpy as jnp
        import numpy as np
        B, T, D = (2, 512, 256)
        DCD = 1024
        RET = 128
        NEXP = 1024
        NKEYS = 64
        H = 4
        KPH = 8
        b, t, d = hidden_states.shape
        q = (hidden_states @ Wq).reshape(b, t, 2, H, RET // 2)
        sim = jnp.einsum('btphn,hkpn->pbthk', q, keys)
        sc, ix = jax.lax.top_k(sim, KPH)
        sx, sy = (sc[0], sc[1])
        ixx, ixy = (ix[0], ix[1])
        all_sc = (sx[..., :, None] + sy[..., None, :]).reshape(b, t, H, KPH * KPH)
        all_ix = (ixx[..., :, None] * NKEYS + ixy[..., None, :]).reshape(b, t, H, KPH * KPH)
        scores, pk = jax.lax.top_k(all_sc, KPH)
        idx = jnp.take_along_axis(all_ix, pk, axis=-1)
        de = down_embed[idx]
        ue = up_embed[idx]
        w = jnp.einsum('btd,bthkd->bthk', hidden_states, de)
        w = jax.nn.silu(w) * jax.nn.softmax(scores, axis=-1)
        experts_states = jnp.einsum('bthk,bthkd->btd', w, ue)
        mlp = jax.nn.silu(hidden_states @ Wg + bg) * (hidden_states @ Wu + bu) @ Wd + bd
        return mlp + experts_states

    def _L1_attn_ref(x, wq, wk, wv, wo):
        import jax, jax.numpy as jnp
        import numpy as np
        B, S, DIM, HD = (64, 200, 256, 128)
        BASE = 10000.0

        def _rope(t, cos, sin):
            tr = t[..., 0::2]
            ti = t[..., 1::2]
            rr = tr * cos - ti * sin
            ri = tr * sin + ti * cos
            return jnp.stack([rr, ri], axis=-1).reshape(t.shape)
        hd = wq.shape[0]
        seq = x.shape[1]
        q = jnp.einsum('bsd,hd->bsh', x, wq)
        k = jnp.einsum('bsd,hd->bsh', x, wk)
        v = jnp.einsum('bsd,hd->bsh', x, wv)
        inv_freq = 1.0 / BASE ** (jnp.arange(0, hd, 2, dtype=jnp.float32) / hd)
        t = jnp.arange(seq - 1, dtype=jnp.float32)
        ang = t[:, None] * inv_freq[None, :]
        cos, sin = (jnp.cos(ang), jnp.sin(ang))
        apply_rope = lambda z: jnp.concatenate([z[:, :1], _rope(z[:, 1:], cos, sin)], axis=1)
        q = apply_rope(q)
        k = apply_rope(k)
        scale = float(np.sqrt(hd))
        w = jax.nn.softmax(jnp.einsum('bqh,bkh->bqk', q, k) / scale, axis=-1)
        out = jnp.einsum('bqk,bkh->bqh', w, v)
        return jnp.einsum('bsh,dh->bsd', out, wo)

    def _L1_ffn_ref(x, Wm, bm, expert_emb, W1, b1, W2, b2, Wo, bo):
        import jax, jax.numpy as jnp
        import numpy as np
        BS, L, D = (4, 512, 256)
        H, E, K = (8, 16, 2)
        HD = D // H
        I = 1024 // H
        bs, L_, d = x.shape
        h = x @ Wm + bm
        t = h.reshape(bs * L_ * H, HD)
        logits = t @ expert_emb
        w = jax.nn.softmax(logits, axis=-1)
        topw, topi = jax.lax.top_k(w, K)
        hmid = jax.nn.gelu(jnp.einsum('td,edi->tei', t, W1) + b1, approximate=False)
        eo = jnp.einsum('tei,eio->teo', hmid, W2) + b2
        sel = jnp.take_along_axis(eo, topi[:, :, None], axis=1)
        comb = (sel * topw[:, :, None]).sum(axis=1)
        out = comb.reshape(bs, L_, d)
        return out @ Wo + bo
    x = L0_attn_x
    x = x + _L0_attn_ref(_layernorm(x, axis=-1), L0_attn_Wq, L0_attn_Wk, L0_attn_Wv)
    x = x + _L0_ffn_ref(_layernorm(x, axis=-1), L0_ffn_Wg, L0_ffn_bg, L0_ffn_Wu, L0_ffn_bu, L0_ffn_Wd, L0_ffn_bd, L0_ffn_Wq, L0_ffn_keys, L0_ffn_down_embed, L0_ffn_up_embed)
    x = x + _L1_attn_ref(_layernorm(x, axis=-1), L1_attn_wq, L1_attn_wk, L1_attn_wv, L1_attn_wo)
    x = x + _L1_ffn_ref(_layernorm(x, axis=-1), L1_ffn_Wm, L1_ffn_bm, L1_ffn_expert_emb, L1_ffn_W1, L1_ffn_b1, L1_ffn_W2, L1_ffn_b2, L1_ffn_Wo, L1_ffn_bo)
    return x

_drawn_inputs = setup_inputs


def setup_inputs(seed=0):
    import zlib

    import numpy as np

    out = dict(_drawn_inputs(seed))
    spreads = {'L0_ffn_bg': (0.0, 0.346),
     'L0_ffn_bu': (0.0, 0.339),
     'L0_ffn_bd': (0.0, 0.1),
     'L1_ffn_bm': (0.0, 0.1),
     'L1_ffn_b1': (0.0, 0.1),
     'L1_ffn_b2': (0.0, 0.1),
     'L1_ffn_bo': (0.0, 0.1)}
    factors = {'L0_attn_Wq': 5.656,
     'L0_attn_Wk': 5.411,
     'L0_ffn_Wq': 8.0,
     'L0_ffn_keys': 8.0,
     'L0_ffn_down_embed': 3.227,
     'L0_ffn_up_embed': 3.356}
    for name, (base, spread) in spreads.items():
        noise = np.random.default_rng([zlib.crc32(name.encode()), seed]).standard_normal(out[name].shape)
        drawn = base * np.exp(spread * noise) if base else spread * noise
        out[name] = jnp.asarray(drawn.astype(out[name].dtype))
    for name, factor in factors.items():
        out[name] = (out[name] * factor).astype(out[name].dtype)
    return out
```

```python
from contextlib import ExitStack

import numpy as np

import concourse.bass as bass
from concourse import mybir

F32 = mybir.dt.float32
BF16 = mybir.dt.bfloat16
ALU = mybir.AluOpType
ACT = mybir.ActivationFunctionType
AX = mybir.AxisListType
P = 128
D = 256
DC = D // P
T = 1024
KT = T // P
BANK = 512
EPS = 1e-5
FAR = -1e30


def wait(engine, sem, value):
    if not isinstance(value, int) or value > 0:
        engine.wait_ge(sem, value)


def load_x(nc, ctx, x, X, B):
    loaded = ctx.enter_context(nc.semaphore("x_loaded"))
    with nc.Block() as block:
        @block.sync
        def _(sp):
            for b in range(B):
                sp.dma_start(X[:, KT * b:KT * (b + 1), :],
                             x[b].rearrange("(t p) d -> p t d", p=P)).then_inc(loaded, 16)
            sp.wait_ge(loaded, 16 * B)


def ln_scales(nc, X, MEAN, RS, NT, tag):
    with ExitStack() as ctx:
        def sb(name, shape):
            return ctx.enter_context(nc.sbuf_tensor(f"{name}_{tag}", shape, F32))

        ST = sb("ln_stats", [P, NT, 6])
        VE, SD, R0, R1, DM = (sb(n, [P, NT]) for n in ("ln_var", "ln_sd", "ln_r0", "ln_r1", "ln_dm"))
        var_ready = ctx.enter_context(nc.semaphore(f"var_ready_{tag}"))
        sd_ready = ctx.enter_context(nc.semaphore(f"sd_ready_{tag}"))
        with nc.Block() as block:
            @block.vector
            def _(dve):
                with dve.Fori(0, NT // 8) as i:
                    for t in range(8):
                        nc.vector.bn_stats(ST[:, 8 * i + t, :], X[:, 8 * i + t, :])
                dve.drain()
                nc.vector.tensor_tensor(MEAN[:, :], ST[:, :, 1], ST[:, :, 4], ALU.add)
                nc.vector.tensor_tensor(DM[:, :], ST[:, :, 1], ST[:, :, 4], ALU.subtract)
                nc.vector.tensor_tensor(VE[:, :], ST[:, :, 2], ST[:, :, 5], ALU.add)
                dve.drain()
                nc.vector.tensor_scalar(MEAN[:, :], MEAN[:, :], 0.5, None, ALU.mult)
                nc.vector.tensor_tensor(DM[:, :], DM[:, :], DM[:, :], ALU.mult)
                nc.vector.tensor_scalar(VE[:, :], VE[:, :], 1.0 / D, EPS, ALU.mult, ALU.add)
                dve.drain()
                nc.vector.scalar_tensor_tensor(out=VE[:, :], in0=DM[:, :], scalar=0.25, in1=VE[:, :],
                                               op0=ALU.mult, op1=ALU.add).then_inc(var_ready, 1)
                dve.wait_ge(sd_ready, 1)
                dve.wait_ge(var_ready, 1)
                nc.vector.reciprocal(R0[:, :], SD[:, :])
                dve.drain()
                nc.vector.tensor_tensor(R1[:, :], R0[:, :], R0[:, :], ALU.mult)
                dve.drain()
                nc.vector.tensor_tensor(R1[:, :], R1[:, :], VE[:, :], ALU.mult)
                dve.drain()
                nc.vector.tensor_scalar(R1[:, :], R1[:, :], -0.5, 1.5, ALU.mult, ALU.add)
                dve.drain()
                nc.vector.tensor_tensor(RS[:, :], R0[:, :], R1[:, :], ALU.mult)

            @block.scalar
            def _(act):
                act.wait_ge(var_ready, 1)
                nc.scalar.activation(SD[:, :], VE[:, :], ACT.Sqrt).then_inc(sd_ready, 1)


def causal_attention(nc, X, MEAN, RS, B, Wq, Wk, Wv, ident, identb):
    H, HS = Wq.shape[0], Wq.shape[2]
    HH = H // 2
    G = 4
    PARTS_Q = (0, 0, 1, 1, 0, 2)
    PARTS_K = (0, 1, 0, 1, 2, 0)
    K6 = len(PARTS_Q) * HS
    K9 = K6 + 3
    SCALE = 1.0 / float(np.sqrt(D))
    MAXU = [(h, qt, kc) for h in range(HH) for qt in range(KT) for kc in range(qt // 4 + 1)]
    SLOTS = 2 * KT
    FIRST_MAX_SLOT = 2
    PER_SLOT = -(-len(MAXU) // (SLOTS - FIRST_MAX_SLOT))
    NPT = 8

    with ExitStack() as ctx:
        def sb(name, shape, dt=F32):
            return ctx.enter_context(nc.sbuf_tensor(name, shape, dt))

        def sem(name):
            return ctx.enter_context(nc.semaphore(name))

        wq = sb("wq_sb", [P, DC, H, HS])
        wk = sb("wk_sb", [P, DC, H, HS])
        wv = sb("wv_sb", [P, DC, H, HS])
        maskq = sb("mask_query_major", [P, P], BF16)
        maskk = sb("mask_key_major", [P, P], BF16)
        XN = sb("xn", [P, 2, D])
        XT = sb("xnT", [P, DC, T])
        V = sb("values", [P, 2, KT, HH, 32])
        QS = sb("q_stack", [P, 2, HH, T], BF16)
        KS = sb("k_stack", [P, 2, HH, T], BF16)
        PT = sb("probsT", [P, NPT, T])
        REM = sb("split_rest", [P, BANK])
        PC = sb("split_parts", [P, 2, 3, BANK], BF16)
        M2 = sb("maxima", [P, HH, KT, 2])
        NM = sb("row_max", [P, 2, G * KT])
        MREM = sb("max_rest", [G * KT, P])
        MP = sb("max_parts", [G * KT, 3, P], BF16)
        OS = sb("outT", [P, 2 * BANK])
        RZ = sb("recip_sum", [P, 4, G])
        ON = REM[:, 0:4 * G * HS].rearrange("p (t j d) -> p t j d", t=4, j=G)
        F = [ctx.enter_context(nc.psum_tensor(f"front{i}", [P, BANK], F32)) for i in range(2)]
        ST = [ctx.enter_context(nc.psum_tensor(f"scoresT{i}", [P, 2 * BANK], F32)) for i in range(2)]
        PV = ctx.enter_context(nc.psum_tensor("pv", [P, 2 * BANK], F32))
        part_d = nc.dram_tensor("split_scratch", [2, 2, 3, P, T], BF16).ap()
        max_d = nc.dram_tensor("max_scratch", [2, 2, 3, G * KT, P], BF16).ap()

        weights_in = sem("weights_in")
        consts_ready = sem("consts_ready")
        masks_zeroed = sem("masks_zeroed")
        xn_ready = sem("xn_ready")
        front_done = sem("front_done")
        front_free = sem("front_free")
        parts_ready = sem("parts_ready")
        parts_stored = [sem(f"parts_stored{i}") for i in range(2)]
        stacks_in = sem("stacks_in")
        maxp_ready = sem("maxp_ready")
        maxp_stored = sem("maxp_stored")
        maxrows_in = [sem(f"maxrows_in{g}") for g in range(2)]
        rowmax_ready = sem("rowmax_ready")
        scores_ready = sem("scores_ready")
        probs_ready = sem("probs_ready")
        pv_done = sem("pv_done")
        out_ready = sem("out_ready")
        outs_added = sem("outs_added")

        UPB = KT + 2 * (2 + 4 + len(MAXU) + 2 + 4)
        XPB = 4 * KT * G
        VPB = 4 * KT

        def stack_released(n):
            return 2 + 2 * KT * (n - 1)

        def used_before(n):
            return not isinstance(n, int) or n >= 2

        block = ctx.enter_context(nc.Block())

        @block.sync
        def _(sp):
            for w, dst in ((Wq, wq), (Wk, wk), (Wv, wv)):
                for c in range(DC):
                    sp.dma_start(dst[:, c, :, :], w[:, c * P:(c + 1) * P, :].rearrange("h p d -> p h d"))\
                      .then_inc(weights_in, 16)

            def front(b, hf):
                n = 2 * b + hf
                for side, (parts, stack) in enumerate(((PARTS_Q, QS), (PARTS_K, KS))):
                    for c in range(2):
                        u = 2 * side + c
                        sp.wait_ge(parts_ready, 4 * n + u + 1)
                        sp.dma_start(part_d[hf, side, :, :, c * BANK:(c + 1) * BANK].rearrange("s r t -> r s t"),
                                     PC[:, c, :, :]).then_inc(parts_stored[c], 16)
                    for c in range(2):
                        sp.wait_ge(parts_stored[c], 16 * (2 * n + side + 1))
                    if side == 0 and used_before(n):
                        sp.wait_ge(pv_done, stack_released(n))
                    for s, part in enumerate(parts):
                        sp.dma_start(stack[HS * s:HS * (s + 1), hf, :, :],
                                     part_d[hf, side, part].rearrange("(h d) t -> d h t", d=HS))\
                          .then_inc(stacks_in, 16)
                for g in range(2):
                    m = 2 * n + g
                    sp.wait_ge(maxp_ready, m + 1)
                    sp.dma_start(max_d[hf, g].rearrange("s r t -> r s t"), MP[:, :, :]).then_inc(maxp_stored, 16)
                    sp.wait_ge(maxp_stored, 16 * (m + 1))
                    sp.dma_start(QS[K6:K9, hf, G * g:G * (g + 1), :],
                                 max_d[hf, g].rearrange("s (h t) q -> s h (t q)", h=G)).then_inc(maxrows_in[g], 16)

            front(0, 0)
            if B > 1:
                with sp.Fori(0, B - 1) as b:
                    front(b, 1)
                    front(b + 1, 0)
            front(B - 1, 1)

        @block.gpsimd
        def _(pool):
            nc.gpsimd.memset(maskq[:, :], 0.0).then_inc(masks_zeroed, 1)
            nc.gpsimd.memset(maskk[:, :], 0.0).then_inc(masks_zeroed, 1)
            nc.gpsimd.memset(V[:, :, :, :, HS:32], 0.0).then_inc(masks_zeroed, 1)
            pool.wait_ge(masks_zeroed, 3)
            nc.gpsimd.memset(KS[K6:K9, :, :, :], 1.0).then_inc(consts_ready, 1)
            pool.wait_ge(consts_ready, 1)
            nc.gpsimd.affine_select(out=maskq[:, :], in_=maskq[:, :], compare_op=ALU.is_ge, fill=FAR,
                                    base=0, pattern=[[-1, P]], channel_multiplier=1).then_inc(consts_ready, 1)
            nc.gpsimd.affine_select(out=maskk[:, :], in_=maskk[:, :], compare_op=ALU.is_ge, fill=FAR,
                                    base=0, pattern=[[1, P]], channel_multiplier=-1).then_inc(consts_ready, 1)
            nc.gpsimd.memset(V[:, :, :, :, HS:HS + 1], 1.0).then_inc(consts_ready, 1)

        @block.tensor
        def _(pe):
            pe.sem_inc(pv_done, 2)
            pe.wait_ge(weights_in, 16 * 3 * DC)
            pe.wait_ge(consts_ready, 4)

            def front_head(b, base, k, hf):
                if hf == 0:
                    for t in range(KT):
                        pe.wait_ge(xn_ready, KT * b + t + 1)
                        pe.wait_ge(front_free, base + k + 1)
                        for c in range(DC):
                            mm = nc.tensor.transpose(F[k % 2][:, c * P:(c + 1) * P],
                                                     XN[:, t % 2, c * P:(c + 1) * P], ident[:, :])
                        mm.then_inc(front_done, 1)
                        k += 1
                    pe.wait_ge(front_free, base + k + 2)
                for q in range(2):
                    pe.wait_ge(front_free, base + k + 1)
                    for t in range(4):
                        for c in range(DC):
                            mm = nc.tensor.matmul(F[k % 2][:, t * P:(t + 1) * P],
                                                  XT[:, c, (4 * q + t) * P:(4 * q + t + 1) * P],
                                                  wv[:, c, HH * hf:HH * (hf + 1), :],
                                                  start=(c == 0), stop=(c == DC - 1))
                    mm.then_inc(front_done, 1)
                    k += 1
                for w in (wq, wk):
                    for q in range(2):
                        pe.wait_ge(front_free, base + k + 1)
                        for c in range(DC):
                            mm = nc.tensor.matmul(F[k % 2][:, :], w[:, c, HH * hf:HH * (hf + 1), :],
                                                  XT[:, c, q * BANK:(q + 1) * BANK],
                                                  start=(c == 0), stop=(c == DC - 1))
                        mm.then_inc(front_done, 1)
                        k += 1
                return k

            def max_unit(base, k, hf, u):
                h, qt, kc = u
                n = min(BANK, (qt + 1) * P - kc * BANK)
                diag = kc == qt // 4
                pe.wait_ge(front_free, base + k + 1)
                mm = nc.tensor.matmul(F[k % 2][:, 0:n], QS[0:K6, hf, h, qt * P:(qt + 1) * P],
                                      KS[0:K6, hf, h, kc * BANK:kc * BANK + n], start=True, stop=not diag)
                if diag:
                    mm = nc.tensor.matmul(F[k % 2][:, n - P:n], identb[:, :], maskq[:, :], start=False, stop=True)
                mm.then_inc(front_done, 1)
                return k + 1

            def max_turn(base, k, m, g):
                pe.wait_ge(rowmax_ready, m + 1)
                pe.wait_ge(front_free, base + k + 1)
                nc.tensor.transpose(F[k % 2][0:G * KT, 0:P], NM[:, g, :], ident[:, :]).then_inc(front_done, 1)
                return k + 1

            def scores(b, hf, g, kt):
                for j in range(G):
                    h, x = G * g + j, ((2 * hf + g) * KT + kt) * G + j
                    pe.wait_ge(probs_ready, XPB * b + x + 1)
                    for c in range(kt // 4, 2):
                        q0 = max(kt * P, c * BANK)
                        diag = c == kt // 4
                        mm = nc.tensor.matmul(ST[x % 2][:, q0:(c + 1) * BANK],
                                              KS[0:K9, hf, h, kt * P:(kt + 1) * P],
                                              QS[0:K9, hf, h, q0:(c + 1) * BANK], start=True, stop=not diag)
                        if diag:
                            mm = nc.tensor.matmul(ST[x % 2][:, q0:q0 + P], identb[:, :], maskk[:, :],
                                                  start=False, stop=True)
                    mm.then_inc(scores_ready, 1)

            def values(b, hf, g, kt):
                x = ((2 * hf + g) * KT + kt) * G
                pe.wait_ge(probs_ready, XPB * b + x + G + 2)
                if kt == 0:
                    pe.wait_ge(out_ready, 4 * b + 2 * hf + g + 1)
                for c in range(kt // 4, 2):
                    q0 = max(kt * P, c * BANK)
                    for j in range(G):
                        mm = nc.tensor.matmul(PV[32 * j:32 * (j + 1), q0:(c + 1) * BANK],
                                              V[:, hf, kt, G * g + j, :], PT[:, (x + j) % NPT, q0:(c + 1) * BANK],
                                              start=(kt == 0), stop=(kt == 4 * c + 3), tile_position=(0, 32 * j))
                mm.then_inc(pv_done, 1)

            def turn_out(b, base, k, hf, g):
                pe.wait_ge(out_ready, 4 * b + 2 * hf + g + 2)
                for c in range(2):
                    pe.wait_ge(front_free, base + k + 1)
                    for t in range(4):
                        mm = nc.tensor.transpose(F[k % 2][:, t * P:(t + 1) * P],
                                                 OS[:, (4 * c + t) * P:(4 * c + t + 1) * P], ident[:, :])
                    mm.then_inc(front_done, 1)
                    k += 1
                return k

            def step(b, hf, base, k, nb, nhf, last=False):
                n = 2 * b + hf
                if not last:
                    k = front_head(nb, base, k, nhf)
                for g in range(2):
                    pe.wait_ge(maxrows_in[g], 16 * (n + 1))
                    for kt in range(KT):
                        scores(b, hf, g, kt)
                        if kt:
                            values(b, hf, g, kt - 1)
                        if g and kt == 1:
                            k = turn_out(b, base, k, hf, 0)
                        slot = g * KT + kt - FIRST_MAX_SLOT
                        if slot >= 0 and not last:
                            if slot == 0:
                                pe.wait_ge(stacks_in, 16 * 12 * (n + 2))
                            for u in MAXU[slot * PER_SLOT:(slot + 1) * PER_SLOT]:
                                k = max_unit(base, k, nhf, u)
                                if u == MAXU[len(MAXU) // 2 - 1]:
                                    k = max_turn(base, k, 2 * (n + 1), 0)
                    values(b, hf, g, KT - 1)
                if not last:
                    k = max_turn(base, k, 2 * (n + 1) + 1, 1)
                return turn_out(b, base, k, hf, 1)

            k = front_head(0, 0, 0, 0)
            pe.wait_ge(stacks_in, 16 * 12)
            for u in MAXU:
                k = max_unit(0, k, 0, u)
                if u == MAXU[len(MAXU) // 2 - 1]:
                    k = max_turn(0, k, 0, 0)
            k0 = max_turn(0, k, 1, 1)
            if B > 1:
                with pe.Fori(0, B - 1) as b:
                    k = step(b, 0, UPB * b, k0, b, 1)
                    k = step(b, 1, UPB * b, k, b + 1, 0)
                    assert k == k0 + UPB and UPB % 2 == 0
            k = step(B - 1, 0, UPB * (B - 1), k0, B - 1, 1)
            step(B - 1, 1, UPB * (B - 1), k, 0, 0, last=True)

        @block.scalar
        def _(act):
            act.sem_inc(probs_ready, 2)
            act.sem_inc(out_ready, 1)
            with act.Fori(0, B) as b:
                for g in range(4):
                    for kt in range(KT):
                        for j in range(G):
                            x = (g * KT + kt) * G + j
                            act.wait_ge(scores_ready, XPB * b + x + 1)
                            if j == 0:
                                act.wait_ge(pv_done, VPB * b + x // G + 1)
                            nc.scalar.activation(PT[:, x % NPT, kt * P:T], ST[x % 2][:, kt * P:T], ACT.Exp,
                                                 scale=SCALE).then_inc(probs_ready, 1)
                    act.wait_ge(pv_done, VPB * b + (g + 1) * KT + 2)
                    act.wait_ge(outs_added, 4 * b + g + 1)
                    nc.scalar.activation(OS[:, :], PV[:, :], ACT.Copy).then_inc(out_ready, 1)

        @block.vector
        def _(dve):
            dve.sem_inc(front_free, 2)
            dve.sem_inc(outs_added, 1)
            nc.vector.memset(M2[:, :, :, :], -3e38)

            def front_head(b, base, k, hf):
                n = 2 * b + hf
                if hf == 0:
                    def norm(t):
                        nc.vector.tensor_scalar(XN[:, t % 2, :], X[:, KT * b + t, :], MEAN[:, bass.ds(KT * b + t, 1)],
                                                RS[:, bass.ds(KT * b + t, 1)], ALU.subtract, ALU.mult)\
                          .then_inc(xn_ready, 1)
                    norm(0)
                    norm(1)
                    for t in range(KT):
                        dve.wait_ge(front_done, base + k + 1)
                        nc.vector.tensor_copy(XT[:, :, t * P:(t + 1) * P],
                                              F[k % 2][:, 0:D].rearrange("p (c t) -> p c t", c=DC))\
                          .then_inc(front_free, 1)
                        k += 1
                        if t + 2 < KT:
                            norm(t + 2)
                if used_before(n):
                    dve.wait_ge(pv_done, stack_released(n))
                for q in range(2):
                    dve.wait_ge(front_done, base + k + 1)
                    nc.vector.tensor_copy(V[:, hf, 4 * q:4 * q + 4, :, 0:HS],
                                          F[k % 2][:, :].rearrange("p (t h d) -> p t h d", t=4, h=HH))\
                      .then_inc(front_free, 1)
                    k += 1
                for u in range(4):
                    dve.wait_ge(front_done, base + k + 1)
                    wait(dve, parts_stored[u % 2], 16 * (2 * n + u // 2))
                    pc = PC[:, u % 2, :, :]
                    nc.vector.tensor_copy(pc[:, 0, :], F[k % 2][:, :])
                    dve.drain()
                    nc.vector.tensor_tensor(REM[:, :], F[k % 2][:, :], pc[:, 0, :], ALU.subtract).then_inc(front_free, 1)
                    dve.drain()
                    nc.vector.tensor_copy(pc[:, 1, :], REM[:, :])
                    dve.drain()
                    nc.vector.tensor_tensor(pc[:, 2, :], REM[:, :], pc[:, 1, :], ALU.subtract).then_inc(parts_ready, 1)
                    k += 1
                return k

            def max_unit(base, k, u):
                h, qt, kc = u
                n = min(BANK, (qt + 1) * P - kc * BANK)
                dve.wait_ge(front_done, base + k + 1)
                nc.vector.tensor_reduce(M2[:, h, qt, kc:kc + 1], F[k % 2][:, 0:n], AX.X, ALU.max)\
                  .then_inc(front_free, 1)
                if u == MAXU[len(MAXU) // 2 - 1] or u == MAXU[-1]:
                    g = h // G
                    dve.drain()
                    nc.vector.tensor_tensor(NM[:, g, :].rearrange("p (h t) -> p h t", h=G),
                                            M2[:, G * g:G * (g + 1), :, 0], M2[:, G * g:G * (g + 1), :, 1],
                                            ALU.max).then_inc(rowmax_ready, 1)
                return k + 1

            def max_turn(base, k, m):
                dve.wait_ge(front_done, base + k + 1)
                wait(dve, maxp_stored, 16 * m)
                turned = F[k % 2][0:G * KT, 0:P]
                nc.vector.tensor_scalar(MP[:, 0, :], turned, -1.0, None, ALU.mult)
                dve.drain()
                nc.vector.scalar_tensor_tensor(out=MREM[:, :], in0=turned, scalar=-1.0, in1=MP[:, 0, :],
                                               op0=ALU.mult, op1=ALU.subtract).then_inc(front_free, 1)
                dve.drain()
                nc.vector.tensor_copy(MP[:, 1, :], MREM[:, :])
                dve.drain()
                nc.vector.tensor_tensor(MP[:, 2, :], MREM[:, :], MP[:, 1, :], ALU.subtract).then_inc(maxp_ready, 1)
                return k + 1

            def add_out(b, base, k, hf, g):
                for c in range(2):
                    dve.wait_ge(front_done, base + k + 1)
                    o = F[k % 2][:, :].rearrange("p (t j e) -> p t j e", t=4, j=G)
                    nc.vector.reciprocal(RZ[:, :, :], o[:, :, :, HS])
                    dve.drain()
                    nc.vector.tensor_tensor(ON, o[:, :, :, 0:HS],
                                            RZ[:, :, :].unsqueeze(3).to_broadcast([P, 4, G, HS]),
                                            ALU.mult).then_inc(front_free, 1)
                    dve.drain()
                    cols = slice((hf * HH + g * G) * HS, (hf * HH + (g + 1) * G) * HS)
                    xs = X[:, bass.ds(KT * b + 4 * c, 4), cols]
                    add = nc.vector.tensor_tensor(xs, xs, ON.rearrange("p t j d -> p t (j d)"), ALU.add)
                    k += 1
                add.then_inc(outs_added, 1)
                return k

            def step(b, hf, base, k, nb, nhf, last=False):
                n = 2 * b + hf
                if not last:
                    k = front_head(nb, base, k, nhf)
                for g in range(2):
                    for kt in range(KT):
                        if g and kt == 1:
                            k = add_out(b, base, k, hf, 0)
                        slot = g * KT + kt - FIRST_MAX_SLOT
                        if slot >= 0 and not last:
                            for u in MAXU[slot * PER_SLOT:(slot + 1) * PER_SLOT]:
                                k = max_unit(base, k, u)
                                if u == MAXU[len(MAXU) // 2 - 1]:
                                    k = max_turn(base, k, 2 * (n + 1))
                if not last:
                    k = max_turn(base, k, 2 * (n + 1) + 1)
                return add_out(b, base, k, hf, 1)

            k = front_head(0, 0, 0, 0)
            for u in MAXU:
                k = max_unit(0, k, u)
                if u == MAXU[len(MAXU) // 2 - 1]:
                    k = max_turn(0, k, 0)
            k0 = max_turn(0, k, 1)
            if B > 1:
                with dve.Fori(0, B - 1) as b:
                    k = step(b, 0, UPB * b, k0, b, 1)
                    k = step(b, 1, UPB * b, k, b + 1, 0)
            k = step(B - 1, 0, UPB * (B - 1), k0, B - 1, 1)
            step(B - 1, 1, UPB * (B - 1), k, 0, 0, last=True)


def expert_weights(nc, Wq, keys, down, MT, DT, ident):
    H, NK, _, KD = keys.shape
    NE = down.shape[0]
    NB = NE // P
    with ExitStack() as ctx:
        WQ = ctx.enter_context(nc.sbuf_tensor("peer_wq", [P, DC, 2, H * KD], F32))
        KY = ctx.enter_context(nc.sbuf_tensor("peer_keys", [NK, 2, H, KD], F32))
        DN = ctx.enter_context(nc.sbuf_tensor("peer_down", [P, NB, D], F32))
        WQT = ctx.enter_context(nc.sbuf_tensor("peer_wqT", [P, 2, H // 2, D], F32))
        KB = ctx.enter_context(nc.sbuf_tensor("peer_keysT", [P, 2, H // 2, P], F32))
        PS = [ctx.enter_context(nc.psum_tensor(f"prep{i}", [P, BANK], F32)) for i in range(2)]
        loaded = ctx.enter_context(nc.semaphore("prep_loaded"))
        filled = ctx.enter_context(nc.semaphore("prep_filled"))
        copied = ctx.enter_context(nc.semaphore("prep_copied"))
        zeroed = ctx.enter_context(nc.semaphore("prep_zeroed"))
        PAIRS = [(p, r) for p in range(2) for r in range(H // 2)]
        with nc.Block() as block:
            @block.sync
            def _(sp):
                for c in range(DC):
                    sp.dma_start(WQ[:, c, :, :], Wq[c * P:(c + 1) * P, :].rearrange("p (s n) -> p s n", s=2))\
                      .then_inc(loaded, 16)
                for s in range(2):
                    sp.dma_start(KY[:, s, :, :], keys[:, :, s, :].rearrange("h k n -> k h n")).then_inc(loaded, 16)
                sp.dma_start(DN[:, :, :], down.rearrange("(b p) d -> p b d", p=P)).then_inc(loaded, 16)

            @block.tensor
            def _(pe):
                pe.wait_ge(loaded, 16 * (DC + 3))
                n = 0
                for s, r in PAIRS:
                    wait(pe, copied, n - 1)
                    for c in range(DC):
                        mm = nc.tensor.transpose(PS[n % 2][:, c * P:(c + 1) * P],
                                                 WQ[:, c, s, 2 * r * KD:2 * (r + 1) * KD], ident[:, :])
                    mm.then_inc(filled, 1)
                    n += 1
                for s, r in PAIRS:
                    wait(pe, copied, n - 1)
                    nc.tensor.transpose(PS[n % 2][:, 0:NK],
                                        KY[:, s, 2 * r:2 * (r + 1), :].rearrange("k h n -> k (h n)"),
                                        ident[0:NK, 0:NK]).then_inc(filled, 1)
                    n += 1
                for c in range(DC):
                    wait(pe, copied, n)
                    for i, (s, r) in enumerate(PAIRS):
                        mm = nc.tensor.matmul(PS[n % 2][:, i * P:(i + 1) * P], WQT[:, s, r, c * P:(c + 1) * P],
                                              KB[:, s, r, :], start=True, stop=True)
                    mm.then_inc(filled, 1)
                    n += 1
                for b in range(NB):
                    wait(pe, copied, n - 1)
                    for c in range(DC):
                        mm = nc.tensor.transpose(PS[n % 2][:, c * P:(c + 1) * P],
                                                 DN[:, b, c * P:(c + 1) * P], ident[:, :])
                    mm.then_inc(filled, 1)
                    n += 1

            @block.vector
            def _(dve):
                nc.vector.memset(KB[:, :, :, :], 0.0)
                dve.drain()
                n = 0
                for s, r in PAIRS:
                    dve.wait_ge(filled, n + 1)
                    nc.vector.tensor_copy(WQT[:, s, r, :], PS[n % 2][:, 0:D]).then_inc(copied, 1)
                    n += 1
                for s, r in PAIRS:
                    dve.wait_ge(filled, n + 1)
                    nc.vector.tensor_copy(KB[0:KD, s, r, 0:NK], PS[n % 2][0:KD, 0:NK])
                    nc.vector.tensor_copy(KB[KD:P, s, r, NK:P], PS[n % 2][KD:P, 0:NK]).then_inc(copied, 1)
                    n += 1
                for c in range(DC):
                    dve.wait_ge(filled, n + 1)
                    nc.vector.tensor_copy(MT[:, c, :], PS[n % 2][:, :]).then_inc(copied, 1)
                    n += 1
                for b in range(NB):
                    dve.wait_ge(filled, n + 1)
                    nc.vector.tensor_copy(DT[:, :, b * P:(b + 1) * P],
                                          PS[n % 2][:, 0:D].rearrange("p (c e) -> p c e", c=DC)).then_inc(copied, 1)
                    n += 1


def expert_ffn(nc, X, MEAN, RS, B, Wg, bg, Wu, bu, Wd, bd, Wq, keys, down, up, ident):
    H, NK, _, KD = keys.shape
    NE = down.shape[0]
    NB = NE // P
    NR = NE // NK
    FF = Wg.shape[1]
    FB = FF // P
    TT = 4
    TM = TT * P
    NM = B * KT // TT
    TOPK = 8
    with ExitStack() as outer:
        MT = outer.enter_context(nc.sbuf_tensor("sim_weights", [P, DC, 2 * H * NK], F32))
        DT = outer.enter_context(nc.sbuf_tensor("downT", [P, DC, NE], F32))
        expert_weights(nc, Wq, keys, down, MT, DT, ident)
        ctx = outer

        def sb(name, shape, dt=F32):
            return ctx.enter_context(nc.sbuf_tensor(name, shape, dt))

        def sem(name):
            return ctx.enter_context(nc.semaphore(name))

        UP = sb("up_sb", [P, NB, D])
        wg = sb("wg_sb", [P, DC, FF])
        wu = sb("wu_sb", [P, DC, FF])
        wd = sb("wd_sb", [P, FB, D])
        bgc = sb("bg_col", [P, FB])
        buc = sb("bu_col", [P, FB])
        bdr = sb("bd_row", [1, D])
        ones = sb("ones_row", [1, P])
        XN = sb("xn0", [P, TT, D])
        XT = sb("xnT0", [P, DC, TM])
        SM = sb("sims", [P, TT, 2, H, NK])
        A = sb("pair_sums", [P, 2, NE])
        E = sb("pair_exp", [P, 2, NE])
        S = sb("expert_weight", [P, TT, NE])
        SD = sb("silu_down", [P, NB, TM])
        GS = sb("silu_gate", [P, 2, TM])
        HT = sb("hiddenT", [P, FB, TM])
        TOP = sb("top_sims", [P, 2, H, TOPK])
        C = sb("candidates", [P, H, TOPK, TOPK])
        T8 = sb("top_pairs", [P, 2, H, TOPK])
        TD = sb("top_less_max", [P, H, TOPK])
        E8 = sb("top_exp", [P, H, TOPK])
        NMX = sb("neg_max", [P, 2, H])
        RZ = sb("recip_z", [P, H])
        SUM = sb("weight_sum", [P, 1])
        F = [ctx.enter_context(nc.psum_tensor(f"front0_{i}", [P, BANK], F32)) for i in range(2)]
        DG = [ctx.enter_context(nc.psum_tensor(f"down_gate{i}", [P, BANK], F32)) for i in range(2)]
        UB = ctx.enter_context(nc.psum_tensor("upward", [P, BANK], F32))
        SP = ctx.enter_context(nc.psum_tensor("weightT", [P, NB, P], F32))
        OB = ctx.enter_context(nc.psum_tensor("ffn_out", [P, BANK], F32))

        weights_in = sem("weights0_in")
        ones_set = sem("ones_set")
        xn_ready = sem("xn0_ready")
        front_done = sem("front0_done")
        front_free = sem("front0_free")
        dg_done = sem("dg_done")
        dg_free = sem("dg_free")
        u_done = sem("u_done")
        h_done = sem("h_done")
        t8_ready = sem("t8_ready")
        e8_ready = sem("e8_ready")
        a_ready = sem("a_ready")
        a_free = sem("a_free")
        e_ready = sem("e_ready")
        e_free = sem("e_free")
        tiles_begun = sem("tiles_begun")
        s_ready = sem("s_ready")
        st_done = sem("st_done")
        w_ready = sem("w_ready")
        out_done = sem("out_done")
        out_free = sem("out_free")

        block = ctx.enter_context(nc.Block())

        @block.sync
        def _(sp):
            moves = [(UP[:, :, :], up.rearrange("(b p) d -> p b d", p=P)),
                     (wg[:, :, :], Wg.rearrange("(c p) f -> p c f", p=P)),
                     (wu[:, :, :], Wu.rearrange("(c p) f -> p c f", p=P)),
                     (wd[:, :, :], Wd.rearrange("(b p) d -> p b d", p=P)),
                     (bdr[:, :], bd.rearrange("(a d) -> a d", a=1))]
            for b in range(FB):
                moves.append((bgc[:, b:b + 1], bg[b * P:(b + 1) * P].rearrange("(p a) -> p a", a=1)))
                moves.append((buc[:, b:b + 1], bu[b * P:(b + 1) * P].rearrange("(p a) -> p a", a=1)))
            assert len(moves) == 5 + 2 * FB
            for dst, src in moves:
                sp.dma_start(dst, src).then_inc(weights_in, 16)

        ALL_IN = 16 * (5 + 2 * FB)

        @block.tensor
        def _(pe):
            pe.wait_ge(weights_in, ALL_IN)
            pe.wait_ge(ones_set, 1)

            def front(m):
                for t in range(TT):
                    k = 2 * TT * m + t
                    pe.wait_ge(xn_ready, TT * m + t + 1)
                    pe.wait_ge(front_free, k + 1)
                    for c in range(DC):
                        mm = nc.tensor.transpose(F[t % 2][:, c * P:(c + 1) * P], XN[:, t, c * P:(c + 1) * P],
                                                 ident[:, :])
                    mm.then_inc(front_done, 1)
                pe.wait_ge(front_free, 2 * TT * m + TT + 2)
                for t in range(TT):
                    k = 2 * TT * m + TT + t
                    pe.wait_ge(front_free, k + 1)
                    for c in range(DC):
                        mm = nc.tensor.matmul(F[t % 2][:, :], XT[:, c, t * P:(t + 1) * P], MT[:, c, :],
                                              start=(c == 0), stop=(c == DC - 1))
                    mm.then_inc(front_done, 1)

            def dense(m):
                for e in range(NB):
                    pe.wait_ge(dg_free, (NB + FB) * m + e + 1)
                    for c in range(DC):
                        mm = nc.tensor.matmul(DG[e % 2][:, :], DT[:, c, e * P:(e + 1) * P], XT[:, c, :],
                                              start=(c == 0), stop=(c == DC - 1))
                    mm.then_inc(dg_done, 1)
                for f in range(FB):
                    pe.wait_ge(dg_free, (NB + FB) * m + NB + f + 1)
                    for c in range(DC):
                        mm = nc.tensor.matmul(DG[f % 2][:, :], wg[:, c, f * P:(f + 1) * P], XT[:, c, :],
                                              start=(c == 0), stop=(c == DC - 1))
                    mm.then_inc(dg_done, 1)
                    pe.wait_ge(h_done, FB * m + f + 2)
                    for c in range(DC):
                        mm = nc.tensor.matmul(UB[:, :], wu[:, c, f * P:(f + 1) * P], XT[:, c, :],
                                              start=(c == 0), stop=(c == DC - 1))
                    mm.then_inc(u_done, 1)

            def outputs(m):
                for t in range(TT):
                    n = TT * m + t
                    tok = slice(t * P, (t + 1) * P)
                    pe.wait_ge(s_ready, n + 1)
                    pe.wait_ge(w_ready, n + 1)
                    for e in range(NB):
                        mm = nc.tensor.transpose(SP[:, e, :], S[:, t, e * P:(e + 1) * P], ident[:, :])
                    mm.then_inc(st_done, 1)
                    if t == 0:
                        pe.wait_ge(h_done, FB * (m + 1) + 2)
                    pe.wait_ge(out_free, n + 1)
                    nc.tensor.matmul(OB[:, 0:D], ones[:, :], bdr[:, :], start=True, stop=False)
                    for f in range(FB):
                        nc.tensor.matmul(OB[:, 0:D], HT[:, f, tok], wd[:, f, :], start=False, stop=False)
                    pe.wait_ge(w_ready, n + 2)
                    for e in range(NB):
                        mm = nc.tensor.matmul(OB[:, 0:D], SD[:, e, tok], UP[:, e, :], start=False, stop=(e == NB - 1))
                    mm.then_inc(out_done, 1)

            front(0)
            if NM > 1:
                with pe.Fori(0, NM - 1) as m:
                    dense(m)
                    front(m + 1)
                    outputs(m)
            dense(NM - 1)
            outputs(NM - 1)

        @block.gpsimd
        def _(pool):
            with pool.Fori(0, NM) as m:
                for t in range(TT):
                    pool.wait_ge(front_free, 2 * TT * m + TT + t + 3)
                    for h in range(H):
                        pool.wait_ge(a_free, H * TT * m + H * t + h + 1)
                        nc.gpsimd.tensor_tensor(A[:, h % 2, :].rearrange("p (i j) -> p i j", i=NR),
                                                SM[:, t, 0, h, 0:NR].unsqueeze(2).to_broadcast([P, NR, NK]),
                                                SM[:, t, 1, h, :].unsqueeze(1).to_broadcast([P, NR, NK]),
                                                ALU.add).then_inc(a_ready, 1)

        @block.scalar
        def _(act):
            act.wait_ge(weights_in, ALL_IN)
            act.sem_inc(front_free, 2)
            act.sem_inc(dg_free, 2)

            def front(m):
                for t in range(TT):
                    act.wait_ge(front_done, 2 * TT * m + t + 1)
                    nc.scalar.activation(XT[:, :, t * P:(t + 1) * P],
                                         F[t % 2][:, 0:D].rearrange("p (c t) -> p c t", c=DC), ACT.Copy)\
                      .then_inc(front_free, 1)
                for t in range(TT):
                    act.wait_ge(front_done, 2 * TT * m + TT + t + 1)
                    if not isinstance(m, int):
                        act.wait_ge(a_ready, H * TT * (m - 1) + H * (t + 1))
                    nc.scalar.activation(SM[:, t, :, :, :], F[t % 2][:, :], ACT.Copy).then_inc(front_free, 1)

            def silu_block(m, n):
                act.wait_ge(dg_done, (NB + FB) * m + n + 1)
                if n < NB:
                    nc.scalar.activation(SD[:, n, :], DG[n % 2][:, :], ACT.Silu).then_inc(dg_free, 1)
                else:
                    f = n - NB
                    act.wait_ge(h_done, FB * m + f + 1)
                    nc.scalar.activation(GS[:, f % 2, :], DG[f % 2][:, :], ACT.Silu, bias=bgc[:, f:f + 1])\
                       .then_inc(dg_free, 1)

            def body(m):
                for t in range(TT):
                    for n in range(t * (NB + FB) // TT, (t + 1) * (NB + FB) // TT):
                        silu_block(m, n)
                    act.wait_ge(t8_ready, TT * m + t + 1)
                    nc.scalar.activation(E8[:, :, :], TD[:, :, :], ACT.Exp).then_inc(e8_ready, 1)
                    for h in range(H):
                        k = H * (TT * m + t) + h
                        act.wait_ge(a_ready, k + 1)
                        act.wait_ge(e_free, k + 1)
                        nc.scalar.activation(E[:, h % 2, :], A[:, h % 2, :], ACT.Exp, bias=NMX[:, t % 2, h:h + 1])\
                           .then_inc(e_ready, 1)

            front(0)
            if NM > 1:
                with act.Fori(0, NM - 1) as m:
                    body(m)
                    front(m + 1)
            body(NM - 1)

        @block.vector
        def _(dve):
            dve.wait_ge(weights_in, ALL_IN)
            nc.vector.memset(ones[:, :], 1.0).then_inc(ones_set, 1)
            dve.sem_inc(h_done, 2)
            dve.sem_inc(a_free, 2)
            dve.sem_inc(e_free, 2)
            dve.sem_inc(w_ready, 1)
            dve.sem_inc(out_free, 1)

            def norm(m):
                for t in range(TT):
                    nc.vector.tensor_scalar(XN[:, t, :], X[:, TT * m + t, :], MEAN[:, bass.ds(TT * m + t, 1)],
                                            RS[:, bass.ds(TT * m + t, 1)], ALU.subtract, ALU.mult)\
                      .then_inc(xn_ready, 1)

            def route(m, t):
                n = TT * m + t
                dve.wait_ge(front_free, 2 * TT * m + TT + t + 3)
                dve.sem_inc(tiles_begun, 1)
                for s in range(2):
                    for h in range(H):
                        nc.vector.max(TOP[:, s, h, :], SM[:, t, s, h, :])
                dve.drain()
                nc.vector.tensor_tensor(C[:, :, :, :], TOP[:, 0, :, :].unsqueeze(3).to_broadcast([P, H, TOPK, TOPK]),
                                        TOP[:, 1, :, :].unsqueeze(2).to_broadcast([P, H, TOPK, TOPK]), ALU.add)
                dve.drain()
                top = T8[:, t % 2, :, :]
                for h in range(H):
                    nc.vector.max(top[:, h, :], C[:, h, :, :].rearrange("p a b -> p (a b)"))
                dve.drain()
                nc.vector.tensor_scalar(NMX[:, t % 2, :], top[:, :, 0], -1.0, None, ALU.mult)
                nc.vector.tensor_tensor(TD[:, :, :], top, top[:, :, 0:1].to_broadcast([P, H, TOPK]), ALU.subtract)
                dve.drain()
                dve.sem_inc(t8_ready, 1)
                dve.wait_ge(e8_ready, n + 1)
                nc.vector.tensor_reduce(RZ[:, :], E8[:, :, :], AX.X, ALU.add)
                dve.drain()
                nc.vector.reciprocal(RZ[:, :], RZ[:, :])
                dve.drain()
                for h in range(H):
                    dve.wait_ge(e_ready, H * n + h + 1)
                    nc.vector.scalar_tensor_tensor(out=E[:, h % 2, :], in0=A[:, h % 2, :], scalar=top[:, h, TOPK - 1:TOPK],
                                                   in1=E[:, h % 2, :], op0=ALU.is_ge, op1=ALU.mult).then_inc(a_free, 1)
                    dve.drain()
                    if h == 0:
                        nc.vector.tensor_scalar(S[:, t, :], E[:, 0, :], RZ[:, 0:1], None, ALU.mult).then_inc(e_free, 1)
                    else:
                        nc.vector.scalar_tensor_tensor(out=S[:, t, :], in0=E[:, h % 2, :], scalar=RZ[:, h:h + 1],
                                                       in1=S[:, t, :], op0=ALU.mult, op1=ALU.add,
                                                       accum_out=SUM[:, :] if h == H - 1 else None)\
                          .then_inc(e_free, 1)
                dve.drain()
                nc.vector.tensor_scalar(SUM[:, :], SUM[:, :], -1.0, float(H), ALU.mult, ALU.add)
                dve.drain()
                nc.vector.tensor_tensor(S[:, t, NE - 1:NE], S[:, t, NE - 1:NE], SUM[:, :], ALU.add).then_inc(s_ready, 1)

            def hidden(m, f):
                dve.wait_ge(u_done, FB * m + f + 1)
                dve.wait_ge(dg_free, (NB + FB) * m + NB + f + 3)
                nc.vector.scalar_tensor_tensor(out=HT[:, f, :], in0=UB[:, :], scalar=buc[:, f:f + 1],
                                               in1=GS[:, f % 2, :], op0=ALU.add, op1=ALU.mult).then_inc(h_done, 1)

            def body(m, last):
                for t in range(TT):
                    if t >= 2:
                        for f in range((t - 2) * FB // 2, (t - 1) * FB // 2):
                            hidden(m, f)
                    route(m, t)
                if not last:
                    dve.wait_ge(front_free, 2 * TT * m + TT + 2)
                    norm(m + 1)
                for t in range(TT):
                    n = TT * m + t
                    tok = slice(t * P, (t + 1) * P)
                    dve.wait_ge(st_done, n + 1)
                    nc.vector.tensor_tensor(SD[:, :, tok], SP[:, :, :], SD[:, :, tok], ALU.mult).then_inc(w_ready, 1)
                    dve.wait_ge(out_done, n + 1)
                    nc.vector.tensor_tensor(X[:, TT * m + t, :], X[:, TT * m + t, :], OB[:, 0:D], ALU.add)\
                      .then_inc(out_free, 1)

            norm(0)
            if NM > 1:
                with dve.Fori(0, NM - 1) as m:
                    body(m, False)
            body(NM - 1, True)


def rotation_tables(T, hd):
    inv_freq = (1.0 / np.float32(10000.0) ** (np.arange(0, hd, 2, dtype=np.float32) / np.float32(hd))).astype(np.float32)
    ang = np.maximum(np.arange(T, dtype=np.float32) - 1, 0)[None, :] * inv_freq[:, None]
    cos, sin = np.cos(ang), np.sin(ang)
    return (np.concatenate([cos, cos]).astype(np.float32), np.concatenate([-sin, sin]).astype(np.float32))


def rotary_attention(nc, X, MEAN, RS, B, Wq, Wk, Wv, Wo, cos_d, sin_d, ident):
    HD = Wq.shape[0]
    SCALE = 1.0 / float(np.sqrt(HD))
    UPB = KT + 2 + 8
    with ExitStack() as ctx:
        def sb(name, shape, dt=F32):
            return ctx.enter_context(nc.sbuf_tensor(name, shape, dt))

        def sem(name):
            return ctx.enter_context(nc.semaphore(name))

        RAW = sb("w_raw", [P, 4, D])
        WT = sb("w_turned", [P, 5, DC, HD])
        WOT = sb("woT", [HD, D])
        COS = sb("cos_sb", [HD, T])
        SIN = sb("sin_sb", [HD, T])
        XN = sb("xn1", [P, KT, D])
        XT = sb("xnT1", [P, DC, T])
        QR = sb("q_turned", [HD, T])
        KR = sb("k_turned", [HD, T])
        RC = sb("rot_cos_part", [HD, BANK])
        RSN = sb("rot_sin_part", [HD, BANK])
        V = sb("values1", [P, KT, HD])
        PQ = sb("probs", [P, 2, T])
        PT = sb("probsT1", [P, 2, KT, P])
        OT = sb("outT1", [HD, 2, P])
        MX = sb("row_max1", [P, 2])
        NB = sb("neg_max1", [P, 2])
        ZS = sb("row_sum", [P, 4])
        RZ = sb("recip_sum1", [P, 4])
        F = [ctx.enter_context(nc.psum_tensor(f"front1_{i}", [P, BANK], F32)) for i in range(2)]
        SC = ctx.enter_context(nc.psum_tensor("scores1", [P, T], F32))
        TP = ctx.enter_context(nc.psum_tensor("turned1", [P, KT, P], F32))
        OP = ctx.enter_context(nc.psum_tensor("pv1", [P, BANK], F32))
        YP = ctx.enter_context(nc.psum_tensor("proj1", [P, BANK], F32))

        weights_in = sem("weights1_in")
        front_done = sem("front1_done")
        front_free = sem("front1_free")
        xn_ready = sem("xn1_ready")
        scores_done = sem("scores1_done")
        max_ready = sem("max1_ready")
        exp_done = sem("exp1_done")
        turned_done = sem("turned1_done")
        turned_act = sem("turned1_act")
        turned_dve = sem("turned1_dve")
        pv_done = sem("pv1_done")
        ot_ready = sem("ot1_ready")
        out_done = sem("out1_done")
        x_added = sem("x1_added")

        block = ctx.enter_context(nc.Block())

        @block.sync
        def _(sp):
            for i, w in enumerate((Wq, Wk, Wv)):
                sp.dma_start(RAW[0:HD, i, :], w).then_inc(weights_in, 16)
            sp.dma_start(RAW[:, 3, :].rearrange("p (a h) -> p a h", a=2), Wo.rearrange("(a p) h -> p a h", p=P))\
              .then_inc(weights_in, 16)
            sp.dma_start(COS[:, :], cos_d).then_inc(weights_in, 16)
            sp.dma_start(SIN[:, :], sin_d).then_inc(weights_in, 16)

        @block.tensor
        def _(pe):
            pe.sem_inc(turned_done, 2)
            pe.sem_inc(pv_done, 2)
            pe.sem_inc(out_done, 2)
            pe.wait_ge(weights_in, 16 * 6)
            for i in range(4):
                pe.wait_ge(front_free, i + 1)
                for c in range(DC):
                    mm = nc.tensor.transpose(F[i % 2][:, c * P:(c + 1) * P], RAW[:, i, c * P:(c + 1) * P], ident[:, :])
                mm.then_inc(front_done, 1)
            pe.wait_ge(front_free, 4 + 2)

            def front(b):
                k = UPB * b + 4
                for t in range(KT):
                    pe.wait_ge(xn_ready, KT * b + t + 1)
                    pe.wait_ge(front_free, k + t + 1)
                    for c in range(DC):
                        mm = nc.tensor.transpose(F[t % 2][:, c * P:(c + 1) * P], XN[:, t, c * P:(c + 1) * P], ident[:, :])
                    mm.then_inc(front_done, 1)
                pe.wait_ge(front_free, k + KT + 2)
                k = k + KT
                for i in range(2):
                    pe.wait_ge(front_free, k + i + 1)
                    for t in range(4):
                        for c in range(DC):
                            mm = nc.tensor.matmul(F[i % 2][:, t * P:(t + 1) * P],
                                                  XT[:, c, (4 * i + t) * P:(4 * i + t + 1) * P], WT[:, 4, c, :],
                                                  start=(c == 0), stop=(c == DC - 1))
                    mm.then_inc(front_done, 1)
                k = k + 2
                for i in range(8):
                    side, q, swapped = i // 4, i // 2 % 2, i % 2
                    pe.wait_ge(front_free, k + i + 1)
                    for c in range(DC):
                        mm = nc.tensor.matmul(F[i % 2][:, :], WT[:, 2 * side + swapped, c, :],
                                              XT[:, c, q * BANK:(q + 1) * BANK], start=(c == 0), stop=(c == DC - 1))
                    mm.then_inc(front_done, 1)
                pe.wait_ge(front_free, k + 8 + 2)

            with pe.Fori(0, B) as b:
                front(b)
                for t in range(KT + 2):
                    n = KT * b + t
                    if 1 <= t <= KT:
                        pe.wait_ge(exp_done, n + 1)
                        pe.wait_ge(turned_act, n)
                        pe.wait_ge(turned_dve, n)
                        for k in range(KT):
                            mm = nc.tensor.transpose(TP[:, k, :], PQ[:, (t - 1) % 2, k * P:(k + 1) * P], ident[:, :])
                        mm.then_inc(turned_done, 1)
                    if t < KT:
                        pe.wait_ge(exp_done, n + 1)
                        for q in range(2):
                            mm = nc.tensor.matmul(SC[:, q * BANK:(q + 1) * BANK], QR[:, t * P:(t + 1) * P],
                                                  KR[:, q * BANK:(q + 1) * BANK], start=True, stop=True)
                        mm.then_inc(scores_done, 1)
                    if t >= 2:
                        pe.wait_ge(ot_ready, n)
                        pe.wait_ge(x_added, n - 1)
                        nc.tensor.matmul(YP[:, 0:D], OT[:, t % 2, :], WOT[:, :], start=True, stop=True)\
                          .then_inc(out_done, 1)
                    if 1 <= t <= KT:
                        pe.wait_ge(turned_act, n + 1)
                        pe.wait_ge(turned_dve, n + 1)
                        pe.wait_ge(ot_ready, n)
                        for k in range(KT):
                            mm = nc.tensor.matmul(OP[:, 0:P], V[:, k, :], PT[:, (t - 1) % 2, k, :],
                                                  start=(k == 0), stop=(k == KT - 1))
                        mm.then_inc(pv_done, 1)

        @block.scalar
        def _(act):
            act.sem_inc(exp_done, 1)
            act.sem_inc(turned_act, 1)
            act.sem_inc(ot_ready, 1)
            with act.Fori(0, B) as b:
                for t in range(KT + 1):
                    n = KT * b + t
                    if t >= 1:
                        act.wait_ge(turned_done, n + 2)
                        act.wait_ge(pv_done, n)
                        nc.scalar.activation(PT[:, (t - 1) % 2, 0:KT // 2, :], TP[:, 0:KT // 2, :], ACT.Copy)\
                           .then_inc(turned_act, 1)
                    if t < KT:
                        act.wait_ge(max_ready, n + 1)
                        act.wait_ge(turned_done, n + 1)
                        nc.scalar.activation(PQ[:, t % 2, :], SC[:, :], ACT.Exp, bias=NB[:, t % 2:t % 2 + 1],
                                             scale=SCALE, accum_out=ZS[:, t % 4:t % 4 + 1]).then_inc(exp_done, 1)
                    if t >= 1:
                        act.wait_ge(pv_done, n + 2)
                        act.wait_ge(out_done, n)
                        nc.scalar.activation(OT[:, (t - 1) % 2, :], OP[:, 0:P], ACT.Copy).then_inc(ot_ready, 1)

        @block.vector
        def _(dve):
            dve.sem_inc(front_free, 2)
            dve.sem_inc(turned_dve, 1)
            dve.sem_inc(x_added, 1)
            dve.wait_ge(weights_in, 16 * 6)
            half = HD // 2
            for i in range(4):
                dve.wait_ge(front_done, i + 1)
                if i < 2:
                    src = F[i % 2][:, 0:D].rearrange("p (c h two) -> p c h two", c=DC, two=2)
                    nc.vector.tensor_copy(WT[:, 2 * i, :, 0:half], src[:, :, :, 0])
                    nc.vector.tensor_copy(WT[:, 2 * i, :, half:HD], src[:, :, :, 1])
                    nc.vector.tensor_copy(WT[:, 2 * i + 1, :, 0:half], src[:, :, :, 1])
                    nc.vector.tensor_copy(WT[:, 2 * i + 1, :, half:HD], src[:, :, :, 0]).then_inc(front_free, 1)
                else:
                    dst = WT[:, 4, :, :] if i == 2 else WOT[:, :].rearrange("p (c h) -> p c h", c=2)
                    nc.vector.tensor_copy(dst, F[i % 2][:, 0:D].rearrange("p (c h) -> p c h", c=DC)).then_inc(front_free, 1)

            def norm(b, t):
                nc.vector.tensor_scalar(XN[:, t, :], X[:, KT * b + t, :], MEAN[:, bass.ds(KT * b + t, 1)],
                                        RS[:, bass.ds(KT * b + t, 1)], ALU.subtract, ALU.mult).then_inc(xn_ready, 1)

            def front(b):
                k = UPB * b + 4
                for t in range(KT):
                    dve.wait_ge(front_done, k + t + 1)
                    nc.vector.tensor_copy(XT[:, :, t * P:(t + 1) * P],
                                          F[t % 2][:, 0:D].rearrange("p (c t) -> p c t", c=DC)).then_inc(front_free, 1)
                k = k + KT
                for i in range(2):
                    dve.wait_ge(front_done, k + i + 1)
                    nc.vector.tensor_copy(V[:, 4 * i:4 * i + 4, :], F[i % 2][:, :].rearrange("p (t h) -> p t h", t=4))\
                      .then_inc(front_free, 1)
                k = k + 2
                for i in range(8):
                    side, q, swapped = i // 4, i // 2 % 2, i % 2
                    tok = slice(q * BANK, (q + 1) * BANK)
                    dve.wait_ge(front_done, k + i + 1)
                    if not swapped:
                        nc.vector.tensor_tensor(RC[:, :], F[i % 2][:, :], COS[:, tok], ALU.mult).then_inc(front_free, 1)
                    else:
                        nc.vector.tensor_tensor(RSN[:, :], F[i % 2][:, :], SIN[:, tok], ALU.mult)
                        dve.drain()
                        nc.vector.tensor_tensor((QR, KR)[side][:, tok], RC[:, :], RSN[:, :], ALU.add).then_inc(front_free, 1)
                        dve.drain()

            def tiles(b):
                for t in range(KT + 2):
                    n = KT * b + t
                    if 1 <= t <= KT:
                        dve.wait_ge(turned_done, n + 2)
                        dve.wait_ge(pv_done, n)
                        nc.vector.tensor_copy(PT[:, (t - 1) % 2, KT // 2:KT, :], TP[:, KT // 2:KT, :])\
                          .then_inc(turned_dve, 1)
                    if t < KT:
                        dve.wait_ge(scores_done, n + 1)
                        nc.vector.tensor_reduce(MX[:, t % 2:t % 2 + 1], SC[:, :], AX.X, ALU.max)
                        dve.drain()
                        nc.vector.tensor_scalar(NB[:, t % 2:t % 2 + 1], MX[:, t % 2:t % 2 + 1], -SCALE, None, ALU.mult)\
                          .then_inc(max_ready, 1)
                    if t >= 2:
                        z = slice((t - 2) % 4, (t - 2) % 4 + 1)
                        dve.wait_ge(out_done, n + 1)
                        dve.wait_ge(exp_done, n)
                        nc.vector.reciprocal(RZ[:, z], ZS[:, z])
                        dve.drain()
                        nc.vector.scalar_tensor_tensor(out=X[:, KT * b + (t - 2), :], in0=YP[:, 0:D], scalar=RZ[:, z],
                                                       in1=X[:, KT * b + (t - 2), :], op0=ALU.mult, op1=ALU.add)\
                          .then_inc(x_added, 1)

            for t in range(KT):
                norm(0, t)
            if B > 1:
                with dve.Fori(0, B - 1) as b:
                    front(b)
                    for t in range(KT):
                        norm(b + 1, t)
                    tiles(b)
            front(B - 1)
            tiles(B - 1)


def mixture_ffn(nc, X, MEAN, RS, B, Wm, bm, emb, W1, b1, W2, b2, Wo, bo, ident):
    HD, E = emb.shape
    I = W1.shape[2]
    G = P // HD
    HC = D // P
    H = G * HC
    TT = 4
    TM = TT * P
    NM = B * KT // TT
    NU = HC * E
    UPM = TT + HC + 1 + 1 + TT
    with ExitStack() as ctx:
        def sb(name, shape, dt=F32):
            return ctx.enter_context(nc.sbuf_tensor(name, shape, dt))

        def sem(name):
            return ctx.enter_context(nc.semaphore(name))

        wm = sb("wm_sb", [P, DC, D])
        wo = sb("wo_sb", [P, HC, D])
        w1 = sb("w1_sb", [P, E, I])
        w2 = sb("w2_sb", [I, E, HD])
        embd = sb("emb_diag", [P, G, E])
        bmc = sb("bm_col", [P, HC])
        b1c = sb("b1_col", [I, E])
        b2c = sb("b2_col", [P, E])
        bor = sb("bo_row", [1, D])
        ones = sb("ones_row1", [1, P])
        SEL = sb("gate_spread", [P, HC, E, G, HD])
        XN = sb("xn2", [P, TT, D])
        XT = sb("xnT2", [P, DC, TM])
        HX = sb("slices", [P, 2, HC, TM])
        LS = sb("logits", [P, TT, H, E])
        LM = sb("logits_less_max", [P, TT, H, E])
        EX = sb("gate_exp", [P, TT, H, E])
        MK = sb("gate_mask", [P, TT, H, E])
        M8 = sb("top_logits", [P, TT, H, 8])
        RZ = sb("gate_recip", [P, TT, H])
        GT = sb("gatesT", [P, 2, TM])
        GH = sb("gelu_out", [I, 4, 2, TM])
        GS = sb("gates_spread", [P, 2, TM])
        Y = sb("gated", [P, 2, TM])
        CM = sb("combined", [P, HC, TM])
        HP = [ctx.enter_context(nc.psum_tensor(f"hidden{i}", [P, 2, TM], F32)) for i in range(2)]
        OP = [ctx.enter_context(nc.psum_tensor(f"expert_out{i}", [P, TM], F32)) for i in range(2)]
        GP = ctx.enter_context(nc.psum_tensor("gate_bank", [P, TM], F32))
        MB = ctx.enter_context(nc.psum_tensor("misc_bank", [P, TM], F32))

        weights_in = sem("weights2_in")
        zeroed = sem("zeroed2")
        consts_ready = sem("consts2_ready")
        xn_ready = sem("xn2_ready")
        misc_done = sem("misc_done")
        misc_free = sem("misc_free")
        lm_ready = sem("lm_ready")
        ex_ready = sem("ex_ready")
        gates_ready = sem("gates_ready")
        a_done = sem("a_done")
        gelu_done = sem("gelu_done")
        o_done = sem("o_done")
        g_done = sem("g_done")
        gs_ready = sem("gs_ready")
        y_ready = sem("y_ready")
        y_added = sem("y_added")

        block = ctx.enter_context(nc.Block())
        moves = [(wm[:, :, :], Wm.rearrange("(c p) n -> p c n", p=P)),
                 (wo[:, :, :], Wo.rearrange("(c p) n -> p c n", p=P)),
                 (w2[:, :, :], W2.rearrange("e i o -> i e o")),
                 (bmc[:, :], bm.rearrange("(c p) -> p c", p=P)),
                 (b1c[:, :], b1.rearrange("e i -> i e")),
                 (bor[:, :], bo.rearrange("(a d) -> a d", a=1))]
        for j in range(G):
            row = slice(HD * j, HD * (j + 1))
            moves += [(w1[row, :, :], W1.rearrange("e d i -> d e i")), (b2c[row, :], b2.rearrange("e o -> o e")),
                      (embd[row, j, :], emb)]
        ALL_IN = 16 * len(moves)

        @block.sync
        def _(sp):
            sp.wait_ge(zeroed, 1)
            for dst, src in moves:
                sp.dma_start(dst, src, allow_slow_non_contiguous=True).then_inc(weights_in, 16)

        FRONT_AT = {2: "x", 5: "h", 8: "l", 11: "w", 16: "g"}

        EXP_AT = 9

        def fb(m):
            return 0 if isinstance(m, int) and m == 0 else UPM * m - TT

        @block.tensor
        def _(pe):
            pe.sem_inc(o_done, 2)
            pe.wait_ge(weights_in, ALL_IN)
            pe.wait_ge(consts_ready, 2)

            def turn_x(m, par):
                for t in range(TT):
                    pe.wait_ge(xn_ready, TT * m + t + 1)
                    pe.wait_ge(misc_free, fb(m) + t + 1)
                    for c in range(DC):
                        mm = nc.tensor.transpose(MB[:, c * P:(c + 1) * P], XN[:, t, c * P:(c + 1) * P], ident[:, :])
                    mm.then_inc(misc_done, 1)

            def project(m, par):
                for h in range(HC):
                    pe.wait_ge(misc_free, fb(m) + TT + h + 1)
                    for c in range(DC):
                        mm = nc.tensor.matmul(MB[:, :], wm[:, c, h * P:(h + 1) * P], XT[:, c, :],
                                              start=(c == 0), stop=(c == DC - 1))
                    mm.then_inc(misc_done, 1)

            def logits(m, par):
                pe.wait_ge(misc_free, fb(m) + TT + HC + 1)
                for t in range(TT):
                    for h in range(HC):
                        mm = nc.tensor.matmul(MB[:, t * P + h * G * E:t * P + (h + 1) * G * E],
                                              HX[:, par, h, t * P:(t + 1) * P], embd[:, :, :], start=True, stop=True)
                mm.then_inc(misc_done, 1)

            def turn_gates(m, par):
                pe.wait_ge(gates_ready, m + 1)
                pe.wait_ge(misc_free, fb(m) + TT + HC + 2)
                for t in range(TT):
                    mm = nc.tensor.transpose(MB[:, t * P:(t + 1) * P], EX[:, t, :, :], ident[:, :])
                mm.then_inc(misc_done, 1)

            def outputs(m, base):
                pe.wait_ge(y_added, NU * m + NU + 3)
                for t in range(TT):
                    pe.wait_ge(misc_free, base + t + 1)
                    nc.tensor.matmul(MB[:, 0:D], ones[:, :], bor[:, :], start=True, stop=False)
                    for h in range(HC):
                        mm = nc.tensor.matmul(MB[:, 0:D], CM[:, h, t * P:(t + 1) * P], wo[:, h, :],
                                              start=False, stop=(h == HC - 1))
                    mm.then_inc(misc_done, 1)

            def hidden(m, par, u):
                hc, e = divmod(u, E)
                for p in range(2):
                    pe.wait_ge(gelu_done, 2 * (NU * m + u) + p + 1)
                    for j in range(2):
                        row = slice(HD * (2 * p + j), HD * (2 * p + j + 1))
                        mm = nc.tensor.matmul(HP[p][:, j, :], w1[row, e, :], HX[row, par, hc, :], start=True, stop=True)
                    mm.then_inc(a_done, 1)

            def expert_out(m, par, u):
                hc, e = divmod(u, E)
                n = NU * m + u
                pe.wait_ge(gs_ready, n + 1)
                nc.tensor.matmul(GP[:, :], SEL[:, hc, e, :, :], GT[:, par, :], start=True, stop=True).then_inc(g_done, 1)
                pe.wait_ge(gelu_done, 2 * n + 4)
                pe.wait_ge(y_ready, n + 1)
                for j in range(G):
                    mm = nc.tensor.matmul(OP[u % 2][HD * j:HD * (j + 1), :], w2[:, e, :],
                                          GH[:, (2 * u + j // 2) % 4, j % 2, :], start=True, stop=True,
                                          tile_position=(0, HD * j))
                mm.then_inc(o_done, 1)

            front = {"x": turn_x, "h": project, "l": logits, "g": turn_gates}

            def one_block(m, par, last):
                for u in range(NU + 1):
                    if u < NU:
                        hidden(m, par, u)
                    if u >= 1:
                        expert_out(m, par, u - 1)
                    if u in FRONT_AT and FRONT_AT[u] != "w" and not last:
                        front[FRONT_AT[u]](m + 1, 1 - par)
                outputs(m, UPM * m + 2 * (UPM - TT) if not last else UPM * m + UPM - TT)

            for part in "xhlg":
                front[part](0, 0)
            pe.wait_ge(misc_free, UPM - TT + 1)
            if NM > 2:
                with pe.Fori(0, NM // 2 - 1) as i:
                    one_block(2 * i, 0, False)
                    one_block(2 * i + 1, 1, False)
            one_block(NM - 2, 0, False)
            one_block(NM - 1, 1, True)

        @block.gpsimd
        def _(pool):
            nc.gpsimd.memset(embd[:, :, :], 0.0).then_inc(zeroed, 1)
            pool.wait_ge(zeroed, 1)
            nc.gpsimd.memset(SEL[:, :, :, :, :], 0.0).then_inc(consts_ready, 1)
            pool.wait_ge(consts_ready, 1)
            nc.gpsimd.affine_select(out=SEL[:, :, :, :, :], in_=SEL[:, :, :, :, :], compare_op=ALU.not_equal, fill=1.0,
                                    base=0, pattern=[[-G * E, HC], [-1, E], [-E, G], [0, HD]], channel_multiplier=1)\
              .then_inc(consts_ready, 1)
            pool.wait_ge(consts_ready, 2)
            pool.sem_inc(y_added, 3)

            def sum_up(m):
                for u in range(NU):
                    hc, e = divmod(u, E)
                    n = NU * m + u
                    pool.wait_ge(y_ready, n + 3)
                    pool.wait_ge(y_added, n + 3)
                    if e == 0:
                        pool.sem_inc(y_added, 1)
                    else:
                        nc.gpsimd.tensor_tensor(CM[:, hc, :], CM[:, hc, :], Y[:, u % 2, :], ALU.add).then_inc(y_added, 1)

            with pool.Fori(0, NM) as m:
                sum_up(m)

        @block.scalar
        def _(act):
            act.wait_ge(weights_in, ALL_IN)
            act.sem_inc(gelu_done, 2)

            def gate_exp(m):
                act.wait_ge(lm_ready, m + 1)
                nc.scalar.activation(EX[:, :, :, :], LM[:, :, :, :], ACT.Exp).then_inc(ex_ready, 1)

            def one_block(m, last):
                for u in range(NU):
                    for p in range(2):
                        k = 2 * u + p
                        act.wait_ge(a_done, 2 * NU * m + k + 1)
                        act.wait_ge(o_done, NU * m + u + 1)
                        nc.scalar.activation(GH[:, k % 4, :, :], HP[p][:, :, :], ACT.Gelu, bias=b1c[:, u % E:u % E + 1])\
                           .then_inc(gelu_done, 1)
                    if u == EXP_AT and not last:
                        gate_exp(m + 1)

            gate_exp(0)
            if NM > 1:
                with act.Fori(0, NM - 1) as m:
                    one_block(m, False)
            one_block(NM - 1, True)

        @block.vector
        def _(dve):
            dve.wait_ge(weights_in, ALL_IN)
            nc.vector.memset(ones[:, :], 1.0)
            dve.drain()
            dve.sem_inc(misc_free, 1)
            dve.sem_inc(gs_ready, 1)
            dve.sem_inc(y_ready, 2)

            def norm(m):
                for t in range(TT):
                    nc.vector.tensor_scalar(XN[:, t, :], X[:, TT * m + t, :], MEAN[:, bass.ds(TT * m + t, 1)],
                                            RS[:, bass.ds(TT * m + t, 1)], ALU.subtract, ALU.mult).then_inc(xn_ready, 1)

            def turn_x(m, par):
                for t in range(TT):
                    dve.wait_ge(misc_done, fb(m) + t + 1)
                    nc.vector.tensor_copy(XT[:, :, t * P:(t + 1) * P], MB[:, 0:D].rearrange("p (c t) -> p c t", c=DC))\
                      .then_inc(misc_free, 1)

            def project(m, par):
                for h in range(HC):
                    dve.wait_ge(misc_done, fb(m) + TT + h + 1)
                    nc.vector.tensor_scalar(HX[:, par, h, :], MB[:, :], bmc[:, h:h + 1], None, ALU.add)\
                      .then_inc(misc_free, 1)

            def logits(m, par):
                dve.wait_ge(misc_done, fb(m) + TT + HC + 1)
                nc.vector.tensor_copy(LS[:, :, :, :], MB[:, :]).then_inc(misc_free, 1)
                dve.drain()
                for t in range(TT):
                    for h in range(H):
                        nc.vector.max(M8[:, t, h, :], LS[:, t, h, :])
                dve.drain()
                flat = lambda a: a.rearrange("p t h e -> p (t h) e")
                ls, m8 = flat(LS[:, :, :, :]), flat(M8[:, :, :, :])
                nc.vector.tensor_tensor(flat(LM[:, :, :, :]), ls, m8[:, :, 0:1].to_broadcast([P, TT * H, E]), ALU.subtract)\
                  .then_inc(lm_ready, 1)
                nc.vector.tensor_tensor(flat(MK[:, :, :, :]), ls, m8[:, :, 1:2].to_broadcast([P, TT * H, E]), ALU.is_ge)

            def weigh(m, par):
                flat = lambda a: a.rearrange("p t h e -> p (t h) e")
                dve.wait_ge(ex_ready, m + 1)
                nc.vector.tensor_reduce(RZ[:, :, :], EX[:, :, :, :], AX.X, ALU.add)
                dve.drain()
                nc.vector.reciprocal(RZ[:, :, :], RZ[:, :, :])
                nc.vector.tensor_tensor(EX[:, :, :, :], EX[:, :, :, :], MK[:, :, :, :], ALU.mult)
                dve.drain()
                nc.vector.tensor_tensor(flat(EX[:, :, :, :]), flat(EX[:, :, :, :]),
                                        RZ[:, :, :].rearrange("p t h -> p (t h)").unsqueeze(2).to_broadcast([P, TT * H, E]),
                                        ALU.mult).then_inc(gates_ready, 1)

            def turn_gates(m, par):
                dve.wait_ge(misc_done, fb(m) + TT + HC + 2)
                nc.vector.tensor_copy(GT[:, par, :], MB[:, :]).then_inc(misc_free, 1)

            def outputs(m, base):
                for t in range(TT):
                    dve.wait_ge(misc_done, base + t + 1)
                    nc.vector.tensor_tensor(X[:, TT * m + t, :], X[:, TT * m + t, :], MB[:, 0:D], ALU.add)\
                      .then_inc(misc_free, 1)

            def gate_unit(m, u):
                n = NU * m + u
                dve.wait_ge(g_done, n + 1)
                nc.vector.tensor_copy(GS[:, u % 2, :], GP[:, :]).then_inc(gs_ready, 1)
                dve.drain()
                dve.wait_ge(o_done, n + 3)
                dve.wait_ge(y_added, n + 2)
                hc, e = divmod(u, E)
                nc.vector.scalar_tensor_tensor(out=Y[:, u % 2, :] if e else CM[:, hc, :], in0=OP[u % 2][:, :], scalar=b2c[:, u % E:u % E + 1],
                                               in1=GS[:, u % 2, :], op0=ALU.add, op1=ALU.mult).then_inc(y_ready, 1)

            front = {"x": turn_x, "h": project, "l": logits, "w": weigh, "g": turn_gates}

            def one_block(m, par, last):
                for u in range(NU + 1):
                    if u >= 1:
                        gate_unit(m, u - 1)
                    if u in FRONT_AT and not last:
                        if FRONT_AT[u] == "x":
                            norm(m + 1)
                        front[FRONT_AT[u]](m + 1, 1 - par)
                outputs(m, UPM * m + 2 * (UPM - TT) if not last else UPM * m + UPM - TT)

            norm(0)
            for part in "xhlwg":
                front[part](0, 0)
            if NM > 2:
                with dve.Fori(0, NM // 2 - 1) as i:
                    one_block(2 * i, 0, False)
                    one_block(2 * i + 1, 1, False)
            one_block(NM - 2, 0, False)
            one_block(NM - 1, 1, True)


def make_idents(nc, ident, identb):
    with ExitStack() as ctx:
        zeroed = ctx.enter_context(nc.semaphore("ident_zeroed"))
        made = ctx.enter_context(nc.semaphore("ident_made"))
        with nc.Block() as block:
            @block.gpsimd
            def _(pool):
                for m in (ident, identb):
                    nc.gpsimd.memset(m[:, :], 0.0).then_inc(zeroed, 1)
                pool.wait_ge(zeroed, 2)
                for m in (ident, identb):
                    nc.gpsimd.affine_select(out=m[:, :], in_=m[:, :], compare_op=ALU.not_equal, fill=1.0,
                                            base=0, pattern=[[-1, P]], channel_multiplier=1).then_inc(made, 1)
                pool.wait_ge(made, 2)


def store_x(nc, ctx, out, X, B):
    stored = ctx.enter_context(nc.semaphore("x_stored"))
    with nc.Block() as block:
        @block.sync
        def _(sp):
            for b in range(B):
                sp.dma_start(out[b].rearrange("(t p) d -> p t d", p=P),
                             X[:, KT * b:KT * (b + 1), :]).then_inc(stored, 16)
            sp.wait_ge(stored, 16 * B)


def program(nc, a, out):
    B = a["L0_attn_x"].shape[0]
    NT = B * KT
    with ExitStack() as ctx:
        X = ctx.enter_context(nc.sbuf_tensor("x_tiles", [P, NT, D], F32))
        MEAN = ctx.enter_context(nc.sbuf_tensor("ln_mean", [P, NT], F32))
        RS = ctx.enter_context(nc.sbuf_tensor("ln_rstd", [P, NT], F32))
        ident = ctx.enter_context(nc.sbuf_tensor("ident", [P, P], F32))
        identb = ctx.enter_context(nc.sbuf_tensor("ident_bf16", [P, P], BF16))
        make_idents(nc, ident, identb)
        load_x(nc, ctx, a["L0_attn_x"], X, B)
        ln_scales(nc, X, MEAN, RS, NT, "a0")
        causal_attention(nc, X, MEAN, RS, B, a["L0_attn_Wq"], a["L0_attn_Wk"], a["L0_attn_Wv"], ident, identb)
        ln_scales(nc, X, MEAN, RS, NT, "f0")
        expert_ffn(nc, X, MEAN, RS, B, *(a["L0_ffn_" + n] for n in (
            "Wg", "bg", "Wu", "bu", "Wd", "bd", "Wq", "keys", "down_embed", "up_embed")), ident)
        ln_scales(nc, X, MEAN, RS, NT, "a1")
        rotary_attention(nc, X, MEAN, RS, B, *(a["L1_attn_" + n] for n in ("wq", "wk", "wv", "wo")),
                         a["rotation_cos"], a["rotation_sin"], ident)
        ln_scales(nc, X, MEAN, RS, NT, "f1")
        mixture_ffn(nc, X, MEAN, RS, B, *(a["L1_ffn_" + n] for n in (
            "Wm", "bm", "expert_emb", "W1", "b1", "W2", "b2", "Wo", "bo")), ident)
        store_x(nc, ctx, out, X, B)


_INS = ["L0_attn_x", "L0_attn_Wq", "L0_attn_Wk", "L0_attn_Wv",
        "L0_ffn_Wg", "L0_ffn_bg", "L0_ffn_Wu", "L0_ffn_bu",
        "L0_ffn_Wd", "L0_ffn_bd", "L0_ffn_Wq", "L0_ffn_keys",
        "L0_ffn_down_embed", "L0_ffn_up_embed", "L1_attn_wq", "L1_attn_wk",
        "L1_attn_wv", "L1_attn_wo", "L1_ffn_Wm", "L1_ffn_bm",
        "L1_ffn_expert_emb", "L1_ffn_W1", "L1_ffn_b1", "L1_ffn_W2",
        "L1_ffn_b2", "L1_ffn_Wo", "L1_ffn_bo"]


def kernel(**inputs):
    import numpy as _np
    import concourse.bacc as _bacc
    from concourse import mybir as _mybir
    from concourse.bass_utils import run_bass_kernel_spmd as _run

    nc = _bacc.Bacc("TRN2", target_bir_lowering=False, num_devices=1)
    arrays, args = {}, {}
    for name in _INS:
        x = _np.ascontiguousarray(inputs[name])
        arrays[f"in_{name}"] = x
        args[name] = nc.dram_tensor(f"in_{name}", x.shape, _mybir.dt.from_np(x.dtype), kind="ExternalInput").ap()
    shape = inputs["L0_attn_x"].shape
    for name, x in zip(("rotation_cos", "rotation_sin"), rotation_tables(shape[1], inputs["L1_attn_wq"].shape[0])):
        arrays[name] = x
        args[name] = nc.dram_tensor(name, x.shape, _mybir.dt.float32, kind="ExternalInput").ap()
    out = nc.dram_tensor("out_x", shape, _mybir.dt.float32, kind="ExternalOutput").ap()
    program(nc, args, out)
    r = _run(nc, [arrays], core_ids=[0])
    return r.results[0]["out_x"]
```

```python
from contextlib import ExitStack

import numpy as np

import concourse.bass as bass
from concourse import mybir

F32 = mybir.dt.float32
BF16 = mybir.dt.bfloat16
ALU = mybir.AluOpType
ACT = mybir.ActivationFunctionType
AX = mybir.AxisListType
P = 128
D = 256
DC = D // P
T = 1024
KT = T // P
BANK = 512
EPS = 1e-5
FAR = -1e30


def wait(engine, sem, value):
    if not isinstance(value, int) or value > 0:
        engine.wait_ge(sem, value)


def load_x(nc, ctx, x, X, B):
    loaded = ctx.enter_context(nc.semaphore("x_loaded"))
    with nc.Block() as block:
        @block.sync
        def _(sp):
            for b in range(B):
                sp.dma_start(X[:, KT * b:KT * (b + 1), :],
                             x[b].rearrange("(t p) d -> p t d", p=P)).then_inc(loaded, 16)
            sp.wait_ge(loaded, 16 * B)


def ln_scales(nc, X, MEAN, RS, NT, tag):
    with ExitStack() as ctx:
        def sb(name, shape):
            return ctx.enter_context(nc.sbuf_tensor(f"{name}_{tag}", shape, F32))

        ST = sb("ln_stats", [P, NT, 6])
        VE, SD, R0, R1, DM = (sb(n, [P, NT]) for n in ("ln_var", "ln_sd", "ln_r0", "ln_r1", "ln_dm"))
        var_ready = ctx.enter_context(nc.semaphore(f"var_ready_{tag}"))
        sd_ready = ctx.enter_context(nc.semaphore(f"sd_ready_{tag}"))
        with nc.Block() as block:
            @block.vector
            def _(dve):
                with dve.Fori(0, NT // 8) as i:
                    for t in range(8):
                        nc.vector.bn_stats(ST[:, 8 * i + t, :], X[:, 8 * i + t, :])
                dve.drain()
                nc.vector.tensor_tensor(MEAN[:, :], ST[:, :, 1], ST[:, :, 4], ALU.add)
                nc.vector.tensor_tensor(DM[:, :], ST[:, :, 1], ST[:, :, 4], ALU.subtract)
                nc.vector.tensor_tensor(VE[:, :], ST[:, :, 2], ST[:, :, 5], ALU.add)
                dve.drain()
                nc.vector.tensor_scalar(MEAN[:, :], MEAN[:, :], 0.5, None, ALU.mult)
                nc.vector.tensor_tensor(DM[:, :], DM[:, :], DM[:, :], ALU.mult)
                nc.vector.tensor_scalar(VE[:, :], VE[:, :], 1.0 / D, EPS, ALU.mult, ALU.add)
                dve.drain()
                nc.vector.scalar_tensor_tensor(out=VE[:, :], in0=DM[:, :], scalar=0.25, in1=VE[:, :],
                                               op0=ALU.mult, op1=ALU.add).then_inc(var_ready, 1)
                dve.wait_ge(sd_ready, 1)
                dve.wait_ge(var_ready, 1)
                nc.vector.reciprocal(R0[:, :], SD[:, :])
                dve.drain()
                nc.vector.tensor_tensor(R1[:, :], R0[:, :], R0[:, :], ALU.mult)
                dve.drain()
                nc.vector.tensor_tensor(R1[:, :], R1[:, :], VE[:, :], ALU.mult)
                dve.drain()
                nc.vector.tensor_scalar(R1[:, :], R1[:, :], -0.5, 1.5, ALU.mult, ALU.add)
                dve.drain()
                nc.vector.tensor_tensor(RS[:, :], R0[:, :], R1[:, :], ALU.mult)

            @block.scalar
            def _(act):
                act.wait_ge(var_ready, 1)
                nc.scalar.activation(SD[:, :], VE[:, :], ACT.Sqrt).then_inc(sd_ready, 1)


def causal_attention(nc, X, MEAN, RS, B, Wq, Wk, Wv, ident, identb):
    H, HS = Wq.shape[0], Wq.shape[2]
    HH = H // 2
    G = 4
    PARTS_Q = (0, 0, 1, 1, 0, 2)
    PARTS_K = (0, 1, 0, 1, 2, 0)
    K6 = len(PARTS_Q) * HS
    K9 = K6 + 3
    SCALE = 1.0 / float(np.sqrt(D))
    MAXU = [(h, qt, kc) for h in range(HH) for qt in range(KT) for kc in range(qt // 4 + 1)]

    def back_pieces():
        out = []
        for g in range(2):
            for kt in range(KT + 1):
                out += [("s", g, kt, j) for j in range(G) if kt < KT]
                out += [("v", g, kt - 1, c, j) for c in range((kt - 1) // 4, 2) for j in range(G) if kt > 0]
        return out

    def front_units(hf):
        out = [("x", t) for t in range(KT) if hf == 0]
        out += [("v", q) for q in range(2)] + [("p", u) for u in range(4)]
        for i, u in enumerate(MAXU):
            out.append(("m", *u))
            if (i + 1) % (len(MAXU) // 2) == 0:
                out.append(("t", u[0] // G))
        return out

    BACK = back_pieces()
    HEAD_EVERY = 1
    FIRST_MAX = 70
    OUT_AT = len(BACK) // 2 + 8

    def filling(nhf):
        after = [[] for _ in BACK]
        if nhf is not None:
            units = front_units(nhf)
            head = [u for u in units if u[0] in "xvp"]
            rest = units[len(head):]
            for i, u in enumerate(head):
                after[i * HEAD_EVERY].append(u)
            room = len(BACK) - FIRST_MAX
            for i, u in enumerate(rest):
                after[FIRST_MAX + i * room // len(rest)].append(u)
        after[OUT_AT].append(("o", 0))
        after[-1].append(("o", 1))
        return after

    NPT = 8

    with ExitStack() as ctx:
        def sb(name, shape, dt=F32):
            return ctx.enter_context(nc.sbuf_tensor(name, shape, dt))

        def sem(name):
            return ctx.enter_context(nc.semaphore(name))

        wq = sb("wq_sb", [P, DC, H, HS])
        wk = sb("wk_sb", [P, DC, H, HS])
        wv = sb("wv_sb", [P, DC, H, HS])
        maskq = sb("mask_query_major", [P, P], BF16)
        maskk = sb("mask_key_major", [P, P], BF16)
        XN = sb("xn", [P, 2, D])
        XT = sb("xnT", [P, DC, T])
        V = sb("values", [P, 2, KT, HH, 32])
        QS = sb("q_stack", [P, 2, HH, T], BF16)
        KS = sb("k_stack", [P, 2, HH, T], BF16)
        PT = sb("probsT", [P, NPT, T])
        REM = sb("split_rest", [P, BANK])
        PC = sb("split_parts", [P, 2, 3, BANK], BF16)
        M2 = sb("maxima", [P, HH, KT, 2])
        NM = sb("row_max", [P, 2, G * KT])
        MREM = sb("max_rest", [G * KT, P])
        MP = sb("max_parts", [G * KT, 3, P], BF16)
        OS = sb("outT", [P, 2 * BANK])
        RZ = sb("recip_sum", [P, 4, G])
        ON = REM[:, 0:4 * G * HS].rearrange("p (t j d) -> p t j d", t=4, j=G)
        F = [ctx.enter_context(nc.psum_tensor(f"front{i}", [P, BANK], F32)) for i in range(2)]
        ST = [ctx.enter_context(nc.psum_tensor(f"scoresT{i}", [P, 2 * BANK], F32)) for i in range(2)]
        PV = ctx.enter_context(nc.psum_tensor("pv", [P, 2 * BANK], F32))
        part_d = nc.dram_tensor("split_scratch", [2, 2, 3, P, T], BF16).ap()
        max_d = nc.dram_tensor("max_scratch", [2, 2, 3, G * KT, P], BF16).ap()

        weights_in = sem("weights_in")
        consts_ready = sem("consts_ready")
        masks_zeroed = sem("masks_zeroed")
        xn_ready = sem("xn_ready")
        front_done = sem("front_done")
        front_free = sem("front_free")
        parts_ready = sem("parts_ready")
        parts_stored = [sem(f"parts_stored{i}") for i in range(2)]
        stacks_in = sem("stacks_in")
        maxp_ready = sem("maxp_ready")
        maxp_stored = sem("maxp_stored")
        maxrows_in = [sem(f"maxrows_in{g}") for g in range(2)]
        rowmax_ready = sem("rowmax_ready")
        scores_ready = sem("scores_ready")
        probs_ready = sem("probs_ready")
        pv_done = sem("pv_done")
        out_ready = sem("out_ready")
        outs_added = sem("outs_added")

        UPB = KT + 2 * (2 + 4 + len(MAXU) + 2 + 4)
        XPB = 4 * KT * G
        VPB = 4 * KT

        def stack_released(n):
            return 2 + 2 * KT * (n - 1)

        def used_before(n):
            return not isinstance(n, int) or n >= 2

        block = ctx.enter_context(nc.Block())

        @block.sync
        def _(sp):
            for w, dst in ((Wq, wq), (Wk, wk), (Wv, wv)):
                for c in range(DC):
                    sp.dma_start(dst[:, c, :, :], w[:, c * P:(c + 1) * P, :].rearrange("h p d -> p h d"))\
                      .then_inc(weights_in, 16)

            def front(b, hf):
                n = 2 * b + hf
                for side, (parts, stack) in enumerate(((PARTS_Q, QS), (PARTS_K, KS))):
                    for c in range(2):
                        u = 2 * side + c
                        sp.wait_ge(parts_ready, 4 * n + u + 1)
                        sp.dma_start(part_d[hf, side, :, :, c * BANK:(c + 1) * BANK].rearrange("s r t -> r s t"),
                                     PC[:, c, :, :]).then_inc(parts_stored[c], 16)
                    for c in range(2):
                        sp.wait_ge(parts_stored[c], 16 * (2 * n + side + 1))
                    if side == 0 and used_before(n):
                        sp.wait_ge(pv_done, stack_released(n))
                    for s, part in enumerate(parts):
                        sp.dma_start(stack[HS * s:HS * (s + 1), hf, :, :],
                                     part_d[hf, side, part].rearrange("(h d) t -> d h t", d=HS))\
                          .then_inc(stacks_in, 16)
                for g in range(2):
                    m = 2 * n + g
                    sp.wait_ge(maxp_ready, m + 1)
                    sp.dma_start(max_d[hf, g].rearrange("s r t -> r s t"), MP[:, :, :]).then_inc(maxp_stored, 16)
                    sp.wait_ge(maxp_stored, 16 * (m + 1))
                    sp.dma_start(QS[K6:K9, hf, G * g:G * (g + 1), :],
                                 max_d[hf, g].rearrange("s (h t) q -> s h (t q)", h=G)).then_inc(maxrows_in[g], 16)

            front(0, 0)
            if B > 1:
                with sp.Fori(0, B - 1) as b:
                    front(b, 1)
                    front(b + 1, 0)
            front(B - 1, 1)

        @block.gpsimd
        def _(pool):
            nc.gpsimd.memset(maskq[:, :], 0.0).then_inc(masks_zeroed, 1)
            nc.gpsimd.memset(maskk[:, :], 0.0).then_inc(masks_zeroed, 1)
            nc.gpsimd.memset(V[:, :, :, :, HS:32], 0.0).then_inc(masks_zeroed, 1)
            pool.wait_ge(masks_zeroed, 3)
            nc.gpsimd.memset(KS[K6:K9, :, :, :], 1.0).then_inc(consts_ready, 1)
            pool.wait_ge(consts_ready, 1)
            nc.gpsimd.affine_select(out=maskq[:, :], in_=maskq[:, :], compare_op=ALU.is_ge, fill=FAR,
                                    base=0, pattern=[[-1, P]], channel_multiplier=1).then_inc(consts_ready, 1)
            nc.gpsimd.affine_select(out=maskk[:, :], in_=maskk[:, :], compare_op=ALU.is_ge, fill=FAR,
                                    base=0, pattern=[[1, P]], channel_multiplier=-1).then_inc(consts_ready, 1)
            nc.gpsimd.memset(V[:, :, :, :, HS:HS + 1], 1.0).then_inc(consts_ready, 1)

        @block.tensor
        def _(pe):
            pe.sem_inc(pv_done, 2)
            pe.wait_ge(weights_in, 16 * 3 * DC)
            pe.wait_ge(consts_ready, 4)

            def fill(unit, base, k, b, hf):
                kind = unit[0]
                n = 2 * b + hf
                if kind == "o":
                    return turn_out(b, base, k, hf, unit[1])
                if kind == "x":
                    pe.wait_ge(xn_ready, KT * b + unit[1] + 1)
                elif kind == "v" and hf == 0 and unit[1] == 0:
                    pe.wait_ge(front_free, base + k + 2)
                elif kind == "m" and unit[1:] == MAXU[0]:
                    pe.wait_ge(stacks_in, 16 * 12 * (n + 1))
                elif kind == "t":
                    pe.wait_ge(rowmax_ready, 2 * n + unit[1] + 1)
                pe.wait_ge(front_free, base + k + 1)
                bank = F[k % 2]
                if kind == "x":
                    t = unit[1]
                    for c in range(DC):
                        mm = nc.tensor.transpose(bank[:, c * P:(c + 1) * P], XN[:, t % 2, c * P:(c + 1) * P], ident[:, :])
                elif kind == "v":
                    for t in range(4):
                        for c in range(DC):
                            tok = slice((4 * unit[1] + t) * P, (4 * unit[1] + t + 1) * P)
                            mm = nc.tensor.matmul(bank[:, t * P:(t + 1) * P], XT[:, c, tok],
                                                  wv[:, c, HH * hf:HH * (hf + 1), :], start=(c == 0), stop=(c == DC - 1))
                elif kind == "p":
                    side, q = divmod(unit[1], 2)
                    for c in range(DC):
                        mm = nc.tensor.matmul(bank[:, :], (wq, wk)[side][:, c, HH * hf:HH * (hf + 1), :],
                                              XT[:, c, q * BANK:(q + 1) * BANK], start=(c == 0), stop=(c == DC - 1))
                elif kind == "m":
                    _, h, qt, kc = unit
                    w = min(BANK, (qt + 1) * P - kc * BANK)
                    diag = kc == qt // 4
                    mm = nc.tensor.matmul(bank[:, 0:w], QS[0:K6, hf, h, qt * P:(qt + 1) * P],
                                          KS[0:K6, hf, h, kc * BANK:kc * BANK + w], start=True, stop=not diag)
                    if diag:
                        mm = nc.tensor.matmul(bank[:, w - P:w], identb[:, :], maskq[:, :], start=False, stop=True)
                elif kind == "t":
                    mm = nc.tensor.transpose(bank[0:G * KT, 0:P], NM[:, unit[1], :], ident[:, :])
                mm.then_inc(front_done, 1)
                return k + 1

            def turn_out(b, base, k, hf, g):
                pe.wait_ge(out_ready, 4 * b + 2 * hf + g + 2)
                for c in range(2):
                    pe.wait_ge(front_free, base + k + 1)
                    for t in range(4):
                        mm = nc.tensor.transpose(F[k % 2][:, t * P:(t + 1) * P],
                                                 OS[:, (4 * c + t) * P:(4 * c + t + 1) * P], ident[:, :])
                    mm.then_inc(front_done, 1)
                    k += 1
                return k

            def scores(b, hf, g, kt, j):
                h, x = G * g + j, ((2 * hf + g) * KT + kt) * G + j
                if kt == 0 and j == 0:
                    pe.wait_ge(maxrows_in[g], 16 * (2 * b + hf + 1))
                pe.wait_ge(probs_ready, XPB * b + x + 1)
                for c in range(kt // 4, 2):
                    q0 = max(kt * P, c * BANK)
                    diag = c == kt // 4
                    mm = nc.tensor.matmul(ST[x % 2][:, q0:(c + 1) * BANK], KS[0:K9, hf, h, kt * P:(kt + 1) * P],
                                          QS[0:K9, hf, h, q0:(c + 1) * BANK], start=True, stop=not diag)
                    if diag:
                        mm = nc.tensor.matmul(ST[x % 2][:, q0:q0 + P], identb[:, :], maskk[:, :], start=False, stop=True)
                mm.then_inc(scores_ready, 1)

            def values(b, hf, g, kt, c, j):
                x = ((2 * hf + g) * KT + kt) * G
                if c == kt // 4 and j == 0:
                    pe.wait_ge(probs_ready, XPB * b + x + G + 2)
                    if kt == 0:
                        pe.wait_ge(out_ready, 4 * b + 2 * hf + g + 1)
                q0 = max(kt * P, c * BANK)
                mm = nc.tensor.matmul(PV[32 * j:32 * (j + 1), q0:(c + 1) * BANK], V[:, hf, kt, G * g + j, :],
                                      PT[:, (x + j) % NPT, q0:(c + 1) * BANK],
                                      start=(kt == 0), stop=(kt == 4 * c + 3), tile_position=(0, 32 * j))
                if c == 1 and j == G - 1:
                    mm.then_inc(pv_done, 1)

            def step(b, hf, base, k, nb, nhf):
                for piece, after in zip(BACK, filling(nhf)):
                    if piece[0] == "s":
                        scores(b, hf, *piece[1:])
                    else:
                        values(b, hf, *piece[1:])
                    for unit in after:
                        k = fill(unit, base, k, b, hf) if unit[0] == "o" else fill(unit, base, k, nb, nhf)
                return k

            k0 = 0
            for unit in front_units(0):
                k0 = fill(unit, 0, k0, 0, 0)
            if B > 1:
                with pe.Fori(0, B - 1) as b:
                    k = step(b, 0, UPB * b, k0, b, 1)
                    k = step(b, 1, UPB * b, k, b + 1, 0)
                    assert k == k0 + UPB and UPB % 2 == 0
            k = step(B - 1, 0, UPB * (B - 1), k0, B - 1, 1)
            step(B - 1, 1, UPB * (B - 1), k, None, None)

        @block.scalar
        def _(act):
            act.sem_inc(probs_ready, 2)
            act.sem_inc(out_ready, 1)
            with act.Fori(0, B) as b:
                for g in range(4):
                    for kt in range(KT):
                        for j in range(G):
                            x = (g * KT + kt) * G + j
                            act.wait_ge(scores_ready, XPB * b + x + 1)
                            if j == 0:
                                act.wait_ge(pv_done, VPB * b + x // G + 1)
                            nc.scalar.activation(PT[:, x % NPT, kt * P:T], ST[x % 2][:, kt * P:T], ACT.Exp,
                                                 scale=SCALE).then_inc(probs_ready, 1)
                    act.wait_ge(pv_done, VPB * b + (g + 1) * KT + 2)
                    act.wait_ge(outs_added, 4 * b + g + 1)
                    nc.scalar.activation(OS[:, :], PV[:, :], ACT.Copy).then_inc(out_ready, 1)

        @block.vector
        def _(dve):
            dve.sem_inc(front_free, 2)
            dve.sem_inc(outs_added, 1)
            nc.vector.memset(M2[:, :, :, :], -3e38)

            def norm(b, t):
                nc.vector.tensor_scalar(XN[:, t % 2, :], X[:, KT * b + t, :], MEAN[:, bass.ds(KT * b + t, 1)],
                                        RS[:, bass.ds(KT * b + t, 1)], ALU.subtract, ALU.mult).then_inc(xn_ready, 1)

            def empty(unit, base, k, b, hf):
                kind = unit[0]
                n = 2 * b + hf
                if kind == "o":
                    return add_out(b, base, k, hf, unit[1])
                bank = F[k % 2]
                if kind == "x" and unit[1] == 0:
                    norm(b, 0)
                    norm(b, 1)
                if kind == "v" and unit[1] == 0 and used_before(n):
                    dve.wait_ge(pv_done, stack_released(n))
                dve.wait_ge(front_done, base + k + 1)
                if kind == "x":
                    t = unit[1]
                    nc.vector.tensor_copy(XT[:, :, t * P:(t + 1) * P], bank[:, 0:D].rearrange("p (c t) -> p c t", c=DC))\
                      .then_inc(front_free, 1)
                    if t + 2 < KT:
                        norm(b, t + 2)
                elif kind == "v":
                    nc.vector.tensor_copy(V[:, hf, 4 * unit[1]:4 * unit[1] + 4, :, 0:HS],
                                          bank[:, :].rearrange("p (t h d) -> p t h d", t=4, h=HH)).then_inc(front_free, 1)
                elif kind == "p":
                    u = unit[1]
                    pc = PC[:, u % 2, :, :]
                    wait(dve, parts_stored[u % 2], 16 * (2 * n + u // 2))
                    nc.vector.tensor_copy(pc[:, 0, :], bank[:, :])
                    dve.drain()
                    nc.vector.tensor_tensor(REM[:, :], bank[:, :], pc[:, 0, :], ALU.subtract).then_inc(front_free, 1)
                    dve.drain()
                    nc.vector.tensor_copy(pc[:, 1, :], REM[:, :])
                    dve.drain()
                    nc.vector.tensor_tensor(pc[:, 2, :], REM[:, :], pc[:, 1, :], ALU.subtract).then_inc(parts_ready, 1)
                elif kind == "m":
                    _, h, qt, kc = unit
                    w = min(BANK, (qt + 1) * P - kc * BANK)
                    nc.vector.tensor_reduce(M2[:, h, qt, kc:kc + 1], bank[:, 0:w], AX.X, ALU.max).then_inc(front_free, 1)
                    if unit[1:] == MAXU[-1] or unit[1:] == MAXU[len(MAXU) // 2 - 1]:
                        g = h // G
                        dve.drain()
                        nc.vector.tensor_tensor(NM[:, g, :].rearrange("p (h t) -> p h t", h=G),
                                                M2[:, G * g:G * (g + 1), :, 0], M2[:, G * g:G * (g + 1), :, 1],
                                                ALU.max).then_inc(rowmax_ready, 1)
                elif kind == "t":
                    wait(dve, maxp_stored, 16 * (2 * n + unit[1]))
                    turned = bank[0:G * KT, 0:P]
                    nc.vector.tensor_scalar(MP[:, 0, :], turned, -1.0, None, ALU.mult)
                    dve.drain()
                    nc.vector.scalar_tensor_tensor(out=MREM[:, :], in0=turned, scalar=-1.0, in1=MP[:, 0, :],
                                                   op0=ALU.mult, op1=ALU.subtract).then_inc(front_free, 1)
                    dve.drain()
                    nc.vector.tensor_copy(MP[:, 1, :], MREM[:, :])
                    dve.drain()
                    nc.vector.tensor_tensor(MP[:, 2, :], MREM[:, :], MP[:, 1, :], ALU.subtract).then_inc(maxp_ready, 1)
                return k + 1

            def add_out(b, base, k, hf, g):
                for c in range(2):
                    dve.wait_ge(front_done, base + k + 1)
                    o = F[k % 2][:, :].rearrange("p (t j e) -> p t j e", t=4, j=G)
                    nc.vector.reciprocal(RZ[:, :, :], o[:, :, :, HS])
                    dve.drain()
                    nc.vector.tensor_tensor(ON, o[:, :, :, 0:HS], RZ[:, :, :].unsqueeze(3).to_broadcast([P, 4, G, HS]),
                                            ALU.mult).then_inc(front_free, 1)
                    dve.drain()
                    cols = slice((hf * HH + g * G) * HS, (hf * HH + (g + 1) * G) * HS)
                    xs = X[:, bass.ds(KT * b + 4 * c, 4), cols]
                    add = nc.vector.tensor_tensor(xs, xs, ON.rearrange("p t j d -> p t (j d)"), ALU.add)
                    k += 1
                add.then_inc(outs_added, 1)
                return k

            def step(b, hf, base, k, nb, nhf):
                for after in filling(nhf):
                    for unit in after:
                        k = empty(unit, base, k, b, hf) if unit[0] == "o" else empty(unit, base, k, nb, nhf)
                return k

            k0 = 0
            for unit in front_units(0):
                k0 = empty(unit, 0, k0, 0, 0)
            if B > 1:
                with dve.Fori(0, B - 1) as b:
                    k = step(b, 0, UPB * b, k0, b, 1)
                    k = step(b, 1, UPB * b, k, b + 1, 0)
            k = step(B - 1, 0, UPB * (B - 1), k0, B - 1, 1)
            step(B - 1, 1, UPB * (B - 1), k, None, None)


def expert_weights(nc, Wq, keys, down, MT, DT, ident):
    H, NK, _, KD = keys.shape
    NE = down.shape[0]
    NB = NE // P
    with ExitStack() as ctx:
        WQ = ctx.enter_context(nc.sbuf_tensor("peer_wq", [P, DC, 2, H * KD], F32))
        KY = ctx.enter_context(nc.sbuf_tensor("peer_keys", [NK, 2, H, KD], F32))
        DN = ctx.enter_context(nc.sbuf_tensor("peer_down", [P, NB, D], F32))
        WQT = ctx.enter_context(nc.sbuf_tensor("peer_wqT", [P, 2, H // 2, D], F32))
        KB = ctx.enter_context(nc.sbuf_tensor("peer_keysT", [P, 2, H // 2, P], F32))
        PS = [ctx.enter_context(nc.psum_tensor(f"prep{i}", [P, BANK], F32)) for i in range(2)]
        loaded = ctx.enter_context(nc.semaphore("prep_loaded"))
        filled = ctx.enter_context(nc.semaphore("prep_filled"))
        copied = ctx.enter_context(nc.semaphore("prep_copied"))
        zeroed = ctx.enter_context(nc.semaphore("prep_zeroed"))
        PAIRS = [(p, r) for p in range(2) for r in range(H // 2)]
        with nc.Block() as block:
            @block.sync
            def _(sp):
                for c in range(DC):
                    sp.dma_start(WQ[:, c, :, :], Wq[c * P:(c + 1) * P, :].rearrange("p (s n) -> p s n", s=2))\
                      .then_inc(loaded, 16)
                for s in range(2):
                    sp.dma_start(KY[:, s, :, :], keys[:, :, s, :].rearrange("h k n -> k h n")).then_inc(loaded, 16)
                sp.dma_start(DN[:, :, :], down.rearrange("(b p) d -> p b d", p=P)).then_inc(loaded, 16)

            @block.tensor
            def _(pe):
                pe.wait_ge(loaded, 16 * (DC + 3))
                n = 0
                for s, r in PAIRS:
                    wait(pe, copied, n - 1)
                    for c in range(DC):
                        mm = nc.tensor.transpose(PS[n % 2][:, c * P:(c + 1) * P],
                                                 WQ[:, c, s, 2 * r * KD:2 * (r + 1) * KD], ident[:, :])
                    mm.then_inc(filled, 1)
                    n += 1
                for s, r in PAIRS:
                    wait(pe, copied, n - 1)
                    nc.tensor.transpose(PS[n % 2][:, 0:NK],
                                        KY[:, s, 2 * r:2 * (r + 1), :].rearrange("k h n -> k (h n)"),
                                        ident[0:NK, 0:NK]).then_inc(filled, 1)
                    n += 1
                for c in range(DC):
                    wait(pe, copied, n)
                    for i, (s, r) in enumerate(PAIRS):
                        mm = nc.tensor.matmul(PS[n % 2][:, i * P:(i + 1) * P], WQT[:, s, r, c * P:(c + 1) * P],
                                              KB[:, s, r, :], start=True, stop=True)
                    mm.then_inc(filled, 1)
                    n += 1
                for b in range(NB):
                    wait(pe, copied, n - 1)
                    for c in range(DC):
                        mm = nc.tensor.transpose(PS[n % 2][:, c * P:(c + 1) * P],
                                                 DN[:, b, c * P:(c + 1) * P], ident[:, :])
                    mm.then_inc(filled, 1)
                    n += 1

            @block.vector
            def _(dve):
                nc.vector.memset(KB[:, :, :, :], 0.0)
                dve.drain()
                n = 0
                for s, r in PAIRS:
                    dve.wait_ge(filled, n + 1)
                    nc.vector.tensor_copy(WQT[:, s, r, :], PS[n % 2][:, 0:D]).then_inc(copied, 1)
                    n += 1
                for s, r in PAIRS:
                    dve.wait_ge(filled, n + 1)
                    nc.vector.tensor_copy(KB[0:KD, s, r, 0:NK], PS[n % 2][0:KD, 0:NK])
                    nc.vector.tensor_copy(KB[KD:P, s, r, NK:P], PS[n % 2][KD:P, 0:NK]).then_inc(copied, 1)
                    n += 1
                for c in range(DC):
                    dve.wait_ge(filled, n + 1)
                    nc.vector.tensor_copy(MT[:, c, :], PS[n % 2][:, :]).then_inc(copied, 1)
                    n += 1
                for b in range(NB):
                    dve.wait_ge(filled, n + 1)
                    nc.vector.tensor_copy(DT[:, :, b * P:(b + 1) * P],
                                          PS[n % 2][:, 0:D].rearrange("p (c e) -> p c e", c=DC)).then_inc(copied, 1)
                    n += 1


def expert_ffn(nc, X, MEAN, RS, B, Wg, bg, Wu, bu, Wd, bd, Wq, keys, down, up, ident):
    H, NK, _, KD = keys.shape
    NE = down.shape[0]
    NB = NE // P
    NR = NE // NK
    FF = Wg.shape[1]
    FB = FF // P
    TT = 4
    TM = TT * P
    NM = B * KT // TT
    TOPK = 8
    with ExitStack() as outer:
        MT = outer.enter_context(nc.sbuf_tensor("sim_weights", [P, DC, 2 * H * NK], F32))
        DT = outer.enter_context(nc.sbuf_tensor("downT", [P, DC, NE], F32))
        expert_weights(nc, Wq, keys, down, MT, DT, ident)
        ctx = outer

        def sb(name, shape, dt=F32):
            return ctx.enter_context(nc.sbuf_tensor(name, shape, dt))

        def sem(name):
            return ctx.enter_context(nc.semaphore(name))

        UP = sb("up_sb", [P, NB, D])
        wg = sb("wg_sb", [P, DC, FF])
        wu = sb("wu_sb", [P, DC, FF])
        wd = sb("wd_sb", [P, FB, D])
        bgc = sb("bg_col", [P, FB])
        buc = sb("bu_col", [P, FB])
        bdr = sb("bd_row", [1, D])
        ones = sb("ones_row", [1, P])
        XN = sb("xn0", [P, TT, D])
        XT = sb("xnT0", [P, DC, TM])
        SM = sb("sims", [P, TT, 2, H, NK])
        A = sb("pair_sums", [P, 2, NE])
        E = sb("pair_exp", [P, 2, NE])
        S = sb("expert_weight", [P, TT, NE])
        SD = sb("silu_down", [P, NB, TM])
        GS = sb("silu_gate", [P, 2, TM])
        HT = sb("hiddenT", [P, FB, TM])
        TOP = sb("top_sims", [P, 2, H, TOPK])
        C = sb("candidates", [P, H, TOPK, TOPK])
        T8 = sb("top_pairs", [P, 2, H, TOPK])
        TD = sb("top_less_max", [P, H, TOPK])
        E8 = sb("top_exp", [P, H, TOPK])
        NMX = sb("neg_max", [P, 2, H])
        RZ = sb("recip_z", [P, H])
        SUM = sb("weight_sum", [P, 1])
        F = [ctx.enter_context(nc.psum_tensor(f"front0_{i}", [P, BANK], F32)) for i in range(2)]
        DG = [ctx.enter_context(nc.psum_tensor(f"down_gate{i}", [P, BANK], F32)) for i in range(2)]
        UB = ctx.enter_context(nc.psum_tensor("upward", [P, BANK], F32))
        SP = ctx.enter_context(nc.psum_tensor("weightT", [P, NB, P], F32))
        OB = ctx.enter_context(nc.psum_tensor("ffn_out", [P, BANK], F32))

        weights_in = sem("weights0_in")
        ones_set = sem("ones_set")
        xn_ready = sem("xn0_ready")
        front_done = sem("front0_done")
        front_free = sem("front0_free")
        dg_done = sem("dg_done")
        dg_free = sem("dg_free")
        u_done = sem("u_done")
        h_done = sem("h_done")
        t8_ready = sem("t8_ready")
        e8_ready = sem("e8_ready")
        a_ready = sem("a_ready")
        a_free = sem("a_free")
        e_ready = sem("e_ready")
        e_free = sem("e_free")
        tiles_begun = sem("tiles_begun")
        s_ready = sem("s_ready")
        st_done = sem("st_done")
        w_ready = sem("w_ready")
        out_done = sem("out_done")
        out_free = sem("out_free")

        block = ctx.enter_context(nc.Block())

        @block.sync
        def _(sp):
            moves = [(UP[:, :, :], up.rearrange("(b p) d -> p b d", p=P)),
                     (wg[:, :, :], Wg.rearrange("(c p) f -> p c f", p=P)),
                     (wu[:, :, :], Wu.rearrange("(c p) f -> p c f", p=P)),
                     (wd[:, :, :], Wd.rearrange("(b p) d -> p b d", p=P)),
                     (bdr[:, :], bd.rearrange("(a d) -> a d", a=1))]
            for b in range(FB):
                moves.append((bgc[:, b:b + 1], bg[b * P:(b + 1) * P].rearrange("(p a) -> p a", a=1)))
                moves.append((buc[:, b:b + 1], bu[b * P:(b + 1) * P].rearrange("(p a) -> p a", a=1)))
            assert len(moves) == 5 + 2 * FB
            for dst, src in moves:
                sp.dma_start(dst, src).then_inc(weights_in, 16)

        ALL_IN = 16 * (5 + 2 * FB)

        @block.tensor
        def _(pe):
            pe.wait_ge(weights_in, ALL_IN)
            pe.wait_ge(ones_set, 1)

            def front(m):
                for t in range(TT):
                    k = 2 * TT * m + t
                    pe.wait_ge(xn_ready, TT * m + t + 1)
                    pe.wait_ge(front_free, k + 1)
                    for c in range(DC):
                        mm = nc.tensor.transpose(F[t % 2][:, c * P:(c + 1) * P], XN[:, t, c * P:(c + 1) * P],
                                                 ident[:, :])
                    mm.then_inc(front_done, 1)
                pe.wait_ge(front_free, 2 * TT * m + TT + 2)
                for t in range(TT):
                    k = 2 * TT * m + TT + t
                    pe.wait_ge(front_free, k + 1)
                    for c in range(DC):
                        mm = nc.tensor.matmul(F[t % 2][:, :], XT[:, c, t * P:(t + 1) * P], MT[:, c, :],
                                              start=(c == 0), stop=(c == DC - 1))
                    mm.then_inc(front_done, 1)

            def dense(m):
                for e in range(NB):
                    pe.wait_ge(dg_free, (NB + FB) * m + e + 1)
                    for c in range(DC):
                        mm = nc.tensor.matmul(DG[e % 2][:, :], DT[:, c, e * P:(e + 1) * P], XT[:, c, :],
                                              start=(c == 0), stop=(c == DC - 1))
                    mm.then_inc(dg_done, 1)
                for f in range(FB):
                    pe.wait_ge(dg_free, (NB + FB) * m + NB + f + 1)
                    for c in range(DC):
                        mm = nc.tensor.matmul(DG[f % 2][:, :], wg[:, c, f * P:(f + 1) * P], XT[:, c, :],
                                              start=(c == 0), stop=(c == DC - 1))
                    mm.then_inc(dg_done, 1)
                    pe.wait_ge(h_done, FB * m + f + 2)
                    for c in range(DC):
                        mm = nc.tensor.matmul(UB[:, :], wu[:, c, f * P:(f + 1) * P], XT[:, c, :],
                                              start=(c == 0), stop=(c == DC - 1))
                    mm.then_inc(u_done, 1)

            def outputs(m):
                for t in range(TT):
                    n = TT * m + t
                    tok = slice(t * P, (t + 1) * P)
                    pe.wait_ge(s_ready, n + 1)
                    pe.wait_ge(w_ready, n + 1)
                    for e in range(NB):
                        mm = nc.tensor.transpose(SP[:, e, :], S[:, t, e * P:(e + 1) * P], ident[:, :])
                    mm.then_inc(st_done, 1)
                    if t == 0:
                        pe.wait_ge(h_done, FB * (m + 1) + 2)
                    pe.wait_ge(out_free, n + 1)
                    nc.tensor.matmul(OB[:, 0:D], ones[:, :], bdr[:, :], start=True, stop=False)
                    for f in range(FB):
                        nc.tensor.matmul(OB[:, 0:D], HT[:, f, tok], wd[:, f, :], start=False, stop=False)
                    pe.wait_ge(w_ready, n + 2)
                    for e in range(NB):
                        mm = nc.tensor.matmul(OB[:, 0:D], SD[:, e, tok], UP[:, e, :], start=False, stop=(e == NB - 1))
                    mm.then_inc(out_done, 1)

            front(0)
            if NM > 1:
                with pe.Fori(0, NM - 1) as m:
                    dense(m)
                    front(m + 1)
                    outputs(m)
            dense(NM - 1)
            outputs(NM - 1)

        @block.gpsimd
        def _(pool):
            with pool.Fori(0, NM) as m:
                for t in range(TT):
                    pool.wait_ge(front_free, 2 * TT * m + TT + t + 3)
                    for h in range(H):
                        pool.wait_ge(a_free, H * TT * m + H * t + h + 1)
                        nc.gpsimd.tensor_tensor(A[:, h % 2, :].rearrange("p (i j) -> p i j", i=NR),
                                                SM[:, t, 0, h, 0:NR].unsqueeze(2).to_broadcast([P, NR, NK]),
                                                SM[:, t, 1, h, :].unsqueeze(1).to_broadcast([P, NR, NK]),
                                                ALU.add).then_inc(a_ready, 1)

        @block.scalar
        def _(act):
            act.wait_ge(weights_in, ALL_IN)
            act.sem_inc(front_free, 2)
            act.sem_inc(dg_free, 2)

            def front(m):
                for t in range(TT):
                    act.wait_ge(front_done, 2 * TT * m + t + 1)
                    nc.scalar.activation(XT[:, :, t * P:(t + 1) * P],
                                         F[t % 2][:, 0:D].rearrange("p (c t) -> p c t", c=DC), ACT.Copy)\
                      .then_inc(front_free, 1)
                for t in range(TT):
                    act.wait_ge(front_done, 2 * TT * m + TT + t + 1)
                    if not isinstance(m, int):
                        act.wait_ge(a_ready, H * TT * (m - 1) + H * (t + 1))
                    nc.scalar.activation(SM[:, t, :, :, :], F[t % 2][:, :], ACT.Copy).then_inc(front_free, 1)

            def silu_block(m, n):
                act.wait_ge(dg_done, (NB + FB) * m + n + 1)
                if n < NB:
                    nc.scalar.activation(SD[:, n, :], DG[n % 2][:, :], ACT.Silu).then_inc(dg_free, 1)
                else:
                    f = n - NB
                    act.wait_ge(h_done, FB * m + f + 1)
                    nc.scalar.activation(GS[:, f % 2, :], DG[f % 2][:, :], ACT.Silu, bias=bgc[:, f:f + 1])\
                       .then_inc(dg_free, 1)

            def body(m):
                for t in range(TT):
                    for n in range(t * (NB + FB) // TT, (t + 1) * (NB + FB) // TT):
                        silu_block(m, n)
                    act.wait_ge(t8_ready, TT * m + t + 1)
                    nc.scalar.activation(E8[:, :, :], TD[:, :, :], ACT.Exp).then_inc(e8_ready, 1)
                    for h in range(H):
                        k = H * (TT * m + t) + h
                        act.wait_ge(a_ready, k + 1)
                        act.wait_ge(e_free, k + 1)
                        nc.scalar.activation(E[:, h % 2, :], A[:, h % 2, :], ACT.Exp, bias=NMX[:, t % 2, h:h + 1])\
                           .then_inc(e_ready, 1)

            front(0)
            if NM > 1:
                with act.Fori(0, NM - 1) as m:
                    body(m)
                    front(m + 1)
            body(NM - 1)

        @block.vector
        def _(dve):
            dve.wait_ge(weights_in, ALL_IN)
            nc.vector.memset(ones[:, :], 1.0).then_inc(ones_set, 1)
            dve.sem_inc(h_done, 2)
            dve.sem_inc(a_free, 2)
            dve.sem_inc(e_free, 2)
            dve.sem_inc(w_ready, 1)
            dve.sem_inc(out_free, 1)

            def norm(m):
                for t in range(TT):
                    nc.vector.tensor_scalar(XN[:, t, :], X[:, TT * m + t, :], MEAN[:, bass.ds(TT * m + t, 1)],
                                            RS[:, bass.ds(TT * m + t, 1)], ALU.subtract, ALU.mult)\
                      .then_inc(xn_ready, 1)

            def route(m, t):
                n = TT * m + t
                dve.wait_ge(front_free, 2 * TT * m + TT + t + 3)
                dve.sem_inc(tiles_begun, 1)
                for s in range(2):
                    for h in range(H):
                        nc.vector.max(TOP[:, s, h, :], SM[:, t, s, h, :])
                dve.drain()
                nc.vector.tensor_tensor(C[:, :, :, :], TOP[:, 0, :, :].unsqueeze(3).to_broadcast([P, H, TOPK, TOPK]),
                                        TOP[:, 1, :, :].unsqueeze(2).to_broadcast([P, H, TOPK, TOPK]), ALU.add)
                dve.drain()
                top = T8[:, t % 2, :, :]
                for h in range(H):
                    nc.vector.max(top[:, h, :], C[:, h, :, :].rearrange("p a b -> p (a b)"))
                dve.drain()
                nc.vector.tensor_scalar(NMX[:, t % 2, :], top[:, :, 0], -1.0, None, ALU.mult)
                nc.vector.tensor_tensor(TD[:, :, :], top, top[:, :, 0:1].to_broadcast([P, H, TOPK]), ALU.subtract)
                dve.drain()
                dve.sem_inc(t8_ready, 1)
                dve.wait_ge(e8_ready, n + 1)
                nc.vector.tensor_reduce(RZ[:, :], E8[:, :, :], AX.X, ALU.add)
                dve.drain()
                nc.vector.reciprocal(RZ[:, :], RZ[:, :])
                dve.drain()
                for h in range(H):
                    dve.wait_ge(e_ready, H * n + h + 1)
                    nc.vector.scalar_tensor_tensor(out=E[:, h % 2, :], in0=A[:, h % 2, :], scalar=top[:, h, TOPK - 1:TOPK],
                                                   in1=E[:, h % 2, :], op0=ALU.is_ge, op1=ALU.mult).then_inc(a_free, 1)
                    dve.drain()
                    if h == 0:
                        nc.vector.tensor_scalar(S[:, t, :], E[:, 0, :], RZ[:, 0:1], None, ALU.mult).then_inc(e_free, 1)
                    else:
                        nc.vector.scalar_tensor_tensor(out=S[:, t, :], in0=E[:, h % 2, :], scalar=RZ[:, h:h + 1],
                                                       in1=S[:, t, :], op0=ALU.mult, op1=ALU.add,
                                                       accum_out=SUM[:, :] if h == H - 1 else None)\
                          .then_inc(e_free, 1)
                dve.drain()
                nc.vector.tensor_scalar(SUM[:, :], SUM[:, :], -1.0, float(H), ALU.mult, ALU.add)
                dve.drain()
                nc.vector.tensor_tensor(S[:, t, NE - 1:NE], S[:, t, NE - 1:NE], SUM[:, :], ALU.add).then_inc(s_ready, 1)

            def hidden(m, f):
                dve.wait_ge(u_done, FB * m + f + 1)
                dve.wait_ge(dg_free, (NB + FB) * m + NB + f + 3)
                nc.vector.scalar_tensor_tensor(out=HT[:, f, :], in0=UB[:, :], scalar=buc[:, f:f + 1],
                                               in1=GS[:, f % 2, :], op0=ALU.add, op1=ALU.mult).then_inc(h_done, 1)

            def body(m, last):
                for t in range(TT):
                    if t >= 2:
                        for f in range((t - 2) * FB // 2, (t - 1) * FB // 2):
                            hidden(m, f)
                    route(m, t)
                if not last:
                    dve.wait_ge(front_free, 2 * TT * m + TT + 2)
                    norm(m + 1)
                for t in range(TT):
                    n = TT * m + t
                    tok = slice(t * P, (t + 1) * P)
                    dve.wait_ge(st_done, n + 1)
                    nc.vector.tensor_tensor(SD[:, :, tok], SP[:, :, :], SD[:, :, tok], ALU.mult).then_inc(w_ready, 1)
                    dve.wait_ge(out_done, n + 1)
                    nc.vector.tensor_tensor(X[:, TT * m + t, :], X[:, TT * m + t, :], OB[:, 0:D], ALU.add)\
                      .then_inc(out_free, 1)

            norm(0)
            if NM > 1:
                with dve.Fori(0, NM - 1) as m:
                    body(m, False)
            body(NM - 1, True)


def rotation_tables(T, hd):
    inv_freq = (1.0 / np.float32(10000.0) ** (np.arange(0, hd, 2, dtype=np.float32) / np.float32(hd))).astype(np.float32)
    ang = np.maximum(np.arange(T, dtype=np.float32) - 1, 0)[None, :] * inv_freq[:, None]
    cos, sin = np.cos(ang), np.sin(ang)
    return (np.concatenate([cos, cos]).astype(np.float32), np.concatenate([-sin, sin]).astype(np.float32))


def rotary_attention(nc, X, MEAN, RS, B, Wq, Wk, Wv, Wo, cos_d, sin_d, ident):
    HD = Wq.shape[0]
    SCALE = 1.0 / float(np.sqrt(HD))
    UPB = KT + 2 + 8
    with ExitStack() as ctx:
        def sb(name, shape, dt=F32):
            return ctx.enter_context(nc.sbuf_tensor(name, shape, dt))

        def sem(name):
            return ctx.enter_context(nc.semaphore(name))

        RAW = sb("w_raw", [P, 4, D])
        WT = sb("w_turned", [P, 5, DC, HD])
        WOT = sb("woT", [HD, D])
        COS = sb("cos_sb", [HD, T])
        SIN = sb("sin_sb", [HD, T])
        XN = sb("xn1", [P, KT, D])
        XT = sb("xnT1", [P, DC, T])
        QR = sb("q_turned", [HD, T])
        KR = sb("k_turned", [HD, T])
        RC = sb("rot_cos_part", [HD, BANK])
        RSN = sb("rot_sin_part", [HD, BANK])
        V = sb("values1", [P, KT, HD])
        PQ = sb("probs", [P, 2, T])
        PT = sb("probsT1", [P, 2, KT, P])
        OT = sb("outT1", [HD, 2, P])
        MX = sb("row_max1", [P, 2])
        NB = sb("neg_max1", [P, 2])
        ZS = sb("row_sum", [P, 4])
        RZ = sb("recip_sum1", [P, 4])
        F = [ctx.enter_context(nc.psum_tensor(f"front1_{i}", [P, BANK], F32)) for i in range(2)]
        SC = ctx.enter_context(nc.psum_tensor("scores1", [P, T], F32))
        TP = ctx.enter_context(nc.psum_tensor("turned1", [P, KT, P], F32))
        OP = ctx.enter_context(nc.psum_tensor("pv1", [P, BANK], F32))
        YP = ctx.enter_context(nc.psum_tensor("proj1", [P, BANK], F32))

        weights_in = sem("weights1_in")
        front_done = sem("front1_done")
        front_free = sem("front1_free")
        xn_ready = sem("xn1_ready")
        scores_done = sem("scores1_done")
        max_ready = sem("max1_ready")
        exp_done = sem("exp1_done")
        turned_done = sem("turned1_done")
        turned_act = sem("turned1_act")
        turned_dve = sem("turned1_dve")
        pv_done = sem("pv1_done")
        ot_ready = sem("ot1_ready")
        out_done = sem("out1_done")
        x_added = sem("x1_added")

        block = ctx.enter_context(nc.Block())

        @block.sync
        def _(sp):
            for i, w in enumerate((Wq, Wk, Wv)):
                sp.dma_start(RAW[0:HD, i, :], w).then_inc(weights_in, 16)
            sp.dma_start(RAW[:, 3, :].rearrange("p (a h) -> p a h", a=2), Wo.rearrange("(a p) h -> p a h", p=P))\
              .then_inc(weights_in, 16)
            sp.dma_start(COS[:, :], cos_d).then_inc(weights_in, 16)
            sp.dma_start(SIN[:, :], sin_d).then_inc(weights_in, 16)

        @block.tensor
        def _(pe):
            pe.sem_inc(turned_done, 2)
            pe.sem_inc(pv_done, 2)
            pe.sem_inc(out_done, 2)
            pe.wait_ge(weights_in, 16 * 6)
            for i in range(4):
                pe.wait_ge(front_free, i + 1)
                for c in range(DC):
                    mm = nc.tensor.transpose(F[i % 2][:, c * P:(c + 1) * P], RAW[:, i, c * P:(c + 1) * P], ident[:, :])
                mm.then_inc(front_done, 1)
            pe.wait_ge(front_free, 4 + 2)

            def front(b):
                k = UPB * b + 4
                for t in range(KT):
                    pe.wait_ge(xn_ready, KT * b + t + 1)
                    pe.wait_ge(front_free, k + t + 1)
                    for c in range(DC):
                        mm = nc.tensor.transpose(F[t % 2][:, c * P:(c + 1) * P], XN[:, t, c * P:(c + 1) * P], ident[:, :])
                    mm.then_inc(front_done, 1)
                pe.wait_ge(front_free, k + KT + 2)
                k = k + KT
                for i in range(2):
                    pe.wait_ge(front_free, k + i + 1)
                    for t in range(4):
                        for c in range(DC):
                            mm = nc.tensor.matmul(F[i % 2][:, t * P:(t + 1) * P],
                                                  XT[:, c, (4 * i + t) * P:(4 * i + t + 1) * P], WT[:, 4, c, :],
                                                  start=(c == 0), stop=(c == DC - 1))
                    mm.then_inc(front_done, 1)
                k = k + 2
                for i in range(8):
                    side, q, swapped = i // 4, i // 2 % 2, i % 2
                    pe.wait_ge(front_free, k + i + 1)
                    for c in range(DC):
                        mm = nc.tensor.matmul(F[i % 2][:, :], WT[:, 2 * side + swapped, c, :],
                                              XT[:, c, q * BANK:(q + 1) * BANK], start=(c == 0), stop=(c == DC - 1))
                    mm.then_inc(front_done, 1)
                pe.wait_ge(front_free, k + 8 + 2)

            with pe.Fori(0, B) as b:
                front(b)
                for t in range(KT + 2):
                    n = KT * b + t
                    if 1 <= t <= KT:
                        pe.wait_ge(exp_done, n + 1)
                        pe.wait_ge(turned_act, n)
                        pe.wait_ge(turned_dve, n)
                        for k in range(KT):
                            mm = nc.tensor.transpose(TP[:, k, :], PQ[:, (t - 1) % 2, k * P:(k + 1) * P], ident[:, :])
                        mm.then_inc(turned_done, 1)
                    if t < KT:
                        pe.wait_ge(exp_done, n + 1)
                        for q in range(2):
                            mm = nc.tensor.matmul(SC[:, q * BANK:(q + 1) * BANK], QR[:, t * P:(t + 1) * P],
                                                  KR[:, q * BANK:(q + 1) * BANK], start=True, stop=True)
                        mm.then_inc(scores_done, 1)
                    if t >= 2:
                        pe.wait_ge(ot_ready, n)
                        pe.wait_ge(x_added, n - 1)
                        nc.tensor.matmul(YP[:, 0:D], OT[:, t % 2, :], WOT[:, :], start=True, stop=True)\
                          .then_inc(out_done, 1)
                    if 1 <= t <= KT:
                        pe.wait_ge(turned_act, n + 1)
                        pe.wait_ge(turned_dve, n + 1)
                        pe.wait_ge(ot_ready, n)
                        for k in range(KT):
                            mm = nc.tensor.matmul(OP[:, 0:P], V[:, k, :], PT[:, (t - 1) % 2, k, :],
                                                  start=(k == 0), stop=(k == KT - 1))
                        mm.then_inc(pv_done, 1)

        @block.scalar
        def _(act):
            act.sem_inc(exp_done, 1)
            act.sem_inc(turned_act, 1)
            act.sem_inc(ot_ready, 1)
            with act.Fori(0, B) as b:
                for t in range(KT + 1):
                    n = KT * b + t
                    if t >= 1:
                        act.wait_ge(turned_done, n + 2)
                        act.wait_ge(pv_done, n)
                        nc.scalar.activation(PT[:, (t - 1) % 2, 0:KT // 2, :], TP[:, 0:KT // 2, :], ACT.Copy)\
                           .then_inc(turned_act, 1)
                    if t < KT:
                        act.wait_ge(max_ready, n + 1)
                        act.wait_ge(turned_done, n + 1)
                        nc.scalar.activation(PQ[:, t % 2, :], SC[:, :], ACT.Exp, bias=NB[:, t % 2:t % 2 + 1],
                                             scale=SCALE, accum_out=ZS[:, t % 4:t % 4 + 1]).then_inc(exp_done, 1)
                    if t >= 1:
                        act.wait_ge(pv_done, n + 2)
                        act.wait_ge(out_done, n)
                        nc.scalar.activation(OT[:, (t - 1) % 2, :], OP[:, 0:P], ACT.Copy).then_inc(ot_ready, 1)

        @block.vector
        def _(dve):
            dve.sem_inc(front_free, 2)
            dve.sem_inc(turned_dve, 1)
            dve.sem_inc(x_added, 1)
            dve.wait_ge(weights_in, 16 * 6)
            half = HD // 2
            for i in range(4):
                dve.wait_ge(front_done, i + 1)
                if i < 2:
                    src = F[i % 2][:, 0:D].rearrange("p (c h two) -> p c h two", c=DC, two=2)
                    nc.vector.tensor_copy(WT[:, 2 * i, :, 0:half], src[:, :, :, 0])
                    nc.vector.tensor_copy(WT[:, 2 * i, :, half:HD], src[:, :, :, 1])
                    nc.vector.tensor_copy(WT[:, 2 * i + 1, :, 0:half], src[:, :, :, 1])
                    nc.vector.tensor_copy(WT[:, 2 * i + 1, :, half:HD], src[:, :, :, 0]).then_inc(front_free, 1)
                else:
                    dst = WT[:, 4, :, :] if i == 2 else WOT[:, :].rearrange("p (c h) -> p c h", c=2)
                    nc.vector.tensor_copy(dst, F[i % 2][:, 0:D].rearrange("p (c h) -> p c h", c=DC)).then_inc(front_free, 1)

            def norm(b, t):
                nc.vector.tensor_scalar(XN[:, t, :], X[:, KT * b + t, :], MEAN[:, bass.ds(KT * b + t, 1)],
                                        RS[:, bass.ds(KT * b + t, 1)], ALU.subtract, ALU.mult).then_inc(xn_ready, 1)

            def front(b):
                k = UPB * b + 4
                for t in range(KT):
                    dve.wait_ge(front_done, k + t + 1)
                    nc.vector.tensor_copy(XT[:, :, t * P:(t + 1) * P],
                                          F[t % 2][:, 0:D].rearrange("p (c t) -> p c t", c=DC)).then_inc(front_free, 1)
                k = k + KT
                for i in range(2):
                    dve.wait_ge(front_done, k + i + 1)
                    nc.vector.tensor_copy(V[:, 4 * i:4 * i + 4, :], F[i % 2][:, :].rearrange("p (t h) -> p t h", t=4))\
                      .then_inc(front_free, 1)
                k = k + 2
                for i in range(8):
                    side, q, swapped = i // 4, i // 2 % 2, i % 2
                    tok = slice(q * BANK, (q + 1) * BANK)
                    dve.wait_ge(front_done, k + i + 1)
                    if not swapped:
                        nc.vector.tensor_tensor(RC[:, :], F[i % 2][:, :], COS[:, tok], ALU.mult).then_inc(front_free, 1)
                    else:
                        nc.vector.tensor_tensor(RSN[:, :], F[i % 2][:, :], SIN[:, tok], ALU.mult)
                        dve.drain()
                        nc.vector.tensor_tensor((QR, KR)[side][:, tok], RC[:, :], RSN[:, :], ALU.add).then_inc(front_free, 1)
                        dve.drain()

            def tiles(b):
                for t in range(KT + 2):
                    n = KT * b + t
                    if 1 <= t <= KT:
                        dve.wait_ge(turned_done, n + 2)
                        dve.wait_ge(pv_done, n)
                        nc.vector.tensor_copy(PT[:, (t - 1) % 2, KT // 2:KT, :], TP[:, KT // 2:KT, :])\
                          .then_inc(turned_dve, 1)
                    if t < KT:
                        dve.wait_ge(scores_done, n + 1)
                        nc.vector.tensor_reduce(MX[:, t % 2:t % 2 + 1], SC[:, :], AX.X, ALU.max)
                        dve.drain()
                        nc.vector.tensor_scalar(NB[:, t % 2:t % 2 + 1], MX[:, t % 2:t % 2 + 1], -SCALE, None, ALU.mult)\
                          .then_inc(max_ready, 1)
                    if t >= 2:
                        z = slice((t - 2) % 4, (t - 2) % 4 + 1)
                        dve.wait_ge(out_done, n + 1)
                        dve.wait_ge(exp_done, n)
                        nc.vector.reciprocal(RZ[:, z], ZS[:, z])
                        dve.drain()
                        nc.vector.scalar_tensor_tensor(out=X[:, KT * b + (t - 2), :], in0=YP[:, 0:D], scalar=RZ[:, z],
                                                       in1=X[:, KT * b + (t - 2), :], op0=ALU.mult, op1=ALU.add)\
                          .then_inc(x_added, 1)

            for t in range(KT):
                norm(0, t)
            if B > 1:
                with dve.Fori(0, B - 1) as b:
                    front(b)
                    for t in range(KT):
                        norm(b + 1, t)
                    tiles(b)
            front(B - 1)
            tiles(B - 1)


def mixture_ffn(nc, X, MEAN, RS, B, Wm, bm, emb, W1, b1, W2, b2, Wo, bo, ident):
    HD, E = emb.shape
    I = W1.shape[2]
    G = P // HD
    HC = D // P
    H = G * HC
    TT = 4
    TM = TT * P
    NM = B * KT // TT
    NU = HC * E
    UPM = TT + HC + 1 + 1 + TT
    with ExitStack() as ctx:
        def sb(name, shape, dt=F32):
            return ctx.enter_context(nc.sbuf_tensor(name, shape, dt))

        def sem(name):
            return ctx.enter_context(nc.semaphore(name))

        wm = sb("wm_sb", [P, DC, D])
        wo = sb("wo_sb", [P, HC, D])
        w1 = sb("w1_sb", [P, E, I])
        w1s = sb("w1_stack", [P, 2, E, I], BF16)
        wpart = sb("w1_part", [P, E, I], BF16)
        w2 = sb("w2_sb", [I, E, HD])
        embd = sb("emb_diag", [P, G, E])
        bmc = sb("bm_col", [P, HC])
        b1c = sb("b1_col", [I, E])
        b2c = sb("b2_col", [P, E])
        bor = sb("bo_row", [1, D])
        ones = sb("ones_row1", [1, P])
        SEL = sb("gate_spread", [3 * HD, E // 2, G, HD], BF16)
        XN = sb("xn2", [P, TT, D])
        XT = sb("xnT2", [P, DC, TM])
        HX = sb("slices", [P, HC, TM])
        REM = sb("split_rest2", [P, TM])
        PCH = sb("slice_parts", [P, HC, 3, TM], BF16)
        PCG = sb("gate_parts", [P, 3, TM], BF16)
        HS = sb("slice_stack", [P, 2, H, TM], BF16)
        GT = sb("gate_stack", [3 * HD, 2, 2 * HC, TM], BF16)
        EXP = sb("gates", [P, TT, P])
        LS = sb("logits", [P, TT, H, E])
        LM = sb("logits_less_max", [P, TT, H, E])
        EX = sb("gate_exp", [P, TT, H, E])
        MK = sb("gate_mask", [P, TT, H, E])
        M8 = sb("top_logits", [P, TT, H, 8])
        RZ = sb("gate_recip", [P, TT, H])
        GH = sb("gelu_out", [I, 4, 2, TM])
        GS = sb("gates_spread", [P, 2, TM])
        Y = sb("gated", [P, 2, TM])
        CM = sb("combined", [P, HC, TM])
        HP = [ctx.enter_context(nc.psum_tensor(f"hidden{i}", [P, 2, TM], F32)) for i in range(2)]
        OP = [ctx.enter_context(nc.psum_tensor(f"expert_out{i}", [P, TM], F32)) for i in range(2)]
        GP = ctx.enter_context(nc.psum_tensor("gate_bank", [P, TM], F32))
        MB = ctx.enter_context(nc.psum_tensor("misc_bank", [P, TM], F32))

        slice_d = nc.dram_tensor("slice_scratch", [2, 3, D, TM], BF16).ap()
        gate_d = nc.dram_tensor("gate_scratch", [2, 3, P, TM], BF16).ap()

        slices_ready = sem("slices_ready")
        slices_stored = [sem(f"slices_stored{c}") for c in range(HC)]
        slices_in = sem("slices_in")
        gparts_ready = sem("gparts_ready")
        gates_stored = sem("gates_stored")
        gates_in = sem("gates_in")
        w1_ready = sem("w1_ready")
        weights_in = sem("weights2_in")
        zeroed = sem("zeroed2")
        consts_ready = sem("consts2_ready")
        xn_ready = sem("xn2_ready")
        misc_done = sem("misc_done")
        misc_free = sem("misc_free")
        lm_ready = sem("lm_ready")
        ex_ready = sem("ex_ready")
        gates_ready = sem("gates_ready")
        a_done = sem("a_done")
        gelu_done = sem("gelu_done")
        o_done = sem("o_done")
        g_done = sem("g_done")
        gs_ready = sem("gs_ready")
        y_ready = sem("y_ready")
        y_added = sem("y_added")

        block = ctx.enter_context(nc.Block())
        moves = [(wm[:, :, :], Wm.rearrange("(c p) n -> p c n", p=P)),
                 (wo[:, :, :], Wo.rearrange("(c p) n -> p c n", p=P)),
                 (w2[:, :, :], W2.rearrange("e i o -> i e o")),
                 (bmc[:, :], bm.rearrange("(c p) -> p c", p=P)),
                 (b1c[:, :], b1.rearrange("e i -> i e")),
                 (bor[:, :], bo.rearrange("(a d) -> a d", a=1))]
        for j in range(G):
            row = slice(HD * j, HD * (j + 1))
            moves += [(w1[row, :, :], W1.rearrange("e d i -> d e i")), (b2c[row, :], b2.rearrange("e o -> o e")),
                      (embd[row, j, :], emb)]
        ALL_IN = 16 * len(moves)

        @block.sync
        def _(sp):
            sp.wait_ge(zeroed, 1)
            for dst, src in moves:
                sp.dma_start(dst, src, allow_slow_non_contiguous=True).then_inc(weights_in, 16)

            def front_io(m, par):
                for c in range(HC):
                    sp.wait_ge(slices_ready, HC * m + c + 1)
                    sp.dma_start(slice_d[par, :, c * P:(c + 1) * P, :].rearrange("s r t -> r s t"), PCH[:, c, :, :])\
                      .then_inc(slices_stored[c], 16)
                for c in range(HC):
                    sp.wait_ge(slices_stored[c], 16 * (m + 1))
                for s, part in enumerate((0, 1, 2, 0)):
                    sp.dma_start(HS[HD * s:HD * (s + 1), par, :, :],
                                 slice_d[par, part].rearrange("(h d) t -> d h t", d=HD)).then_inc(slices_in, 16)
                sp.wait_ge(gparts_ready, m + 1)
                sp.dma_start(gate_d[par].rearrange("s r t -> r s t"), PCG[:, :, :]).then_inc(gates_stored, 16)
                sp.wait_ge(gates_stored, 16 * (m + 1))
                for s in range(3):
                    sp.dma_start(GT[HD * s:HD * (s + 1), par, :, :],
                                 gate_d[par, s].rearrange("(g r) t -> r g t", r=HD)).then_inc(gates_in, 16)

            with sp.Fori(0, NM // 2) as i:
                front_io(2 * i, 0)
                front_io(2 * i + 1, 1)

        FRONT_AT = {2: "x", 5: "h", 8: "l", 11: "w", 16: "g"}

        EXP_AT = 9

        def fb(m):
            return 0 if isinstance(m, int) and m == 0 else UPM * m - TT

        @block.tensor
        def _(pe):
            pe.sem_inc(o_done, 2)
            pe.wait_ge(weights_in, ALL_IN)
            pe.wait_ge(consts_ready, 4)
            pe.wait_ge(w1_ready, 1)

            def turn_x(m, par):
                for t in range(TT):
                    pe.wait_ge(xn_ready, TT * m + t + 1)
                    pe.wait_ge(misc_free, fb(m) + t + 1)
                    for c in range(DC):
                        mm = nc.tensor.transpose(MB[:, c * P:(c + 1) * P], XN[:, t, c * P:(c + 1) * P], ident[:, :])
                    mm.then_inc(misc_done, 1)

            def project(m, par):
                for h in range(HC):
                    pe.wait_ge(misc_free, fb(m) + TT + h + 1)
                    for c in range(DC):
                        mm = nc.tensor.matmul(MB[:, :], wm[:, c, h * P:(h + 1) * P], XT[:, c, :],
                                              start=(c == 0), stop=(c == DC - 1))
                    mm.then_inc(misc_done, 1)

            def logits(m, par):
                pe.wait_ge(misc_free, fb(m) + TT + HC + 1)
                for t in range(TT):
                    for h in range(HC):
                        mm = nc.tensor.matmul(MB[:, t * P + h * G * E:t * P + (h + 1) * G * E],
                                              HX[:, h, t * P:(t + 1) * P], embd[:, :, :], start=True, stop=True)
                mm.then_inc(misc_done, 1)

            def turn_gates(m, par):
                pe.wait_ge(gates_ready, m + 1)
                pe.wait_ge(misc_free, fb(m) + TT + HC + 2)
                for t in range(TT):
                    mm = nc.tensor.transpose(MB[:, t * P:(t + 1) * P], EXP[:, t, :], ident[:, :])
                mm.then_inc(misc_done, 1)

            def outputs(m, base):
                pe.wait_ge(y_added, NU * m + NU + 3)
                for t in range(TT):
                    pe.wait_ge(misc_free, base + t + 1)
                    nc.tensor.matmul(MB[:, 0:D], ones[:, :], bor[:, :], start=True, stop=False)
                    for h in range(HC):
                        mm = nc.tensor.matmul(MB[:, 0:D], CM[:, h, t * P:(t + 1) * P], wo[:, h, :],
                                              start=False, stop=(h == HC - 1))
                    mm.then_inc(misc_done, 1)

            def hidden(m, par, u):
                hc, e = divmod(u, E)
                for p in range(2):
                    pe.wait_ge(gelu_done, 2 * (NU * m + u) + p + 1)
                    for j in range(2):
                        h = G * hc + 2 * p + j
                        nc.tensor.matmul(HP[p][:, j, :], w1s[:, 0, e, :], HS[:, par, h, :], start=True, stop=False)
                        mm = nc.tensor.matmul(HP[p][:, j, :], w1s[0:3 * HD, 1, e, :], HS[0:3 * HD, par, h, :],
                                              start=False, stop=True)
                    mm.then_inc(a_done, 1)

            def expert_out(m, par, u):
                hc, e = divmod(u, E)
                n = NU * m + u
                pe.wait_ge(gs_ready, n + 1)
                nc.tensor.matmul(GP[:, :], SEL[:, e % (E // 2), :, :], GT[:, par, 2 * hc + e // (E // 2), :],
                                 start=True, stop=True).then_inc(g_done, 1)
                pe.wait_ge(gelu_done, 2 * n + 4)
                pe.wait_ge(y_ready, n + 1)
                for j in range(G):
                    mm = nc.tensor.matmul(OP[u % 2][HD * j:HD * (j + 1), :], w2[:, e, :],
                                          GH[:, (2 * u + j // 2) % 4, j % 2, :], start=True, stop=True,
                                          tile_position=(0, HD * j))
                mm.then_inc(o_done, 1)

            front = {"x": turn_x, "h": project, "l": logits, "g": turn_gates}

            def one_block(m, par, last):
                pe.wait_ge(slices_in, 16 * 4 * (m + 1))
                pe.wait_ge(gates_in, 16 * 3 * (m + 1))
                for u in range(NU + 1):
                    if u < NU:
                        hidden(m, par, u)
                    if u >= 1:
                        expert_out(m, par, u - 1)
                    if u in FRONT_AT and FRONT_AT[u] != "w" and not last:
                        front[FRONT_AT[u]](m + 1, 1 - par)
                outputs(m, UPM * m + 2 * (UPM - TT) if not last else UPM * m + UPM - TT)

            for part in "xhlg":
                front[part](0, 0)
            pe.wait_ge(misc_free, UPM - TT + 1)
            if NM > 2:
                with pe.Fori(0, NM // 2 - 1) as i:
                    one_block(2 * i, 0, False)
                    one_block(2 * i + 1, 1, False)
            one_block(NM - 2, 0, False)
            one_block(NM - 1, 1, True)

        @block.gpsimd
        def _(pool):
            nc.gpsimd.memset(embd[:, :, :], 0.0).then_inc(zeroed, 1)
            pool.wait_ge(zeroed, 1)
            nc.gpsimd.memset(SEL[:, :, :, :], 0.0).then_inc(consts_ready, 1)
            pool.wait_ge(consts_ready, 1)
            for s in range(3):
                nc.gpsimd.affine_select(out=SEL[:, :, :, :], in_=SEL[:, :, :, :], compare_op=ALU.not_equal, fill=1.0,
                                        base=-HD * s, pattern=[[-1, E // 2], [-(E // 2), G], [0, HD]],
                                        channel_multiplier=1).then_inc(consts_ready, 1)
                pool.wait_ge(consts_ready, s + 2)
            pool.sem_inc(y_added, 3)

            def sum_up(m):
                for u in range(NU):
                    hc, e = divmod(u, E)
                    n = NU * m + u
                    pool.wait_ge(y_ready, n + 3)
                    pool.wait_ge(y_added, n + 3)
                    if e == 0:
                        pool.sem_inc(y_added, 1)
                    else:
                        nc.gpsimd.tensor_tensor(CM[:, hc, :], CM[:, hc, :], Y[:, u % 2, :], ALU.add).then_inc(y_added, 1)

            with pool.Fori(0, NM) as m:
                sum_up(m)

        @block.scalar
        def _(act):
            act.wait_ge(weights_in, ALL_IN)
            act.sem_inc(gelu_done, 2)

            def gate_exp(m):
                act.wait_ge(lm_ready, m + 1)
                nc.scalar.activation(EX[:, :, :, :], LM[:, :, :, :], ACT.Exp).then_inc(ex_ready, 1)

            def one_block(m, last):
                for u in range(NU):
                    for p in range(2):
                        k = 2 * u + p
                        act.wait_ge(a_done, 2 * NU * m + k + 1)
                        act.wait_ge(o_done, NU * m + u + 1)
                        nc.scalar.activation(GH[:, k % 4, :, :], HP[p][:, :, :], ACT.Gelu, bias=b1c[:, u % E:u % E + 1])\
                           .then_inc(gelu_done, 1)
                    if u == EXP_AT and not last:
                        gate_exp(m + 1)

            gate_exp(0)
            if NM > 1:
                with act.Fori(0, NM - 1) as m:
                    one_block(m, False)
            one_block(NM - 1, True)

        @block.vector
        def _(dve):
            dve.wait_ge(weights_in, ALL_IN)
            nc.vector.memset(ones[:, :], 1.0)
            TAKES = (((0, 0), (0, 1), (0, 2), (1, 3)), ((2, 0), (1, 1), (1, 2)))
            for part in range(3):
                nc.vector.tensor_copy(wpart[:, :, :], w1[:, :, :])
                dve.drain()
                for i in range(2):
                    for takes, block_row in TAKES[i]:
                        if takes == part:
                            row = slice(HD * block_row, HD * (block_row + 1))
                            nc.vector.tensor_copy(w1s[row, i, :, :], wpart[row, :, :])
                nc.vector.tensor_tensor(w1[:, :, :], w1[:, :, :], wpart[:, :, :], ALU.subtract)
                dve.drain()
            dve.sem_inc(w1_ready, 1)
            dve.sem_inc(misc_free, 1)
            dve.sem_inc(gs_ready, 1)
            dve.sem_inc(y_ready, 2)

            def norm(m):
                for t in range(TT):
                    nc.vector.tensor_scalar(XN[:, t, :], X[:, TT * m + t, :], MEAN[:, bass.ds(TT * m + t, 1)],
                                            RS[:, bass.ds(TT * m + t, 1)], ALU.subtract, ALU.mult).then_inc(xn_ready, 1)

            def turn_x(m, par):
                for t in range(TT):
                    dve.wait_ge(misc_done, fb(m) + t + 1)
                    nc.vector.tensor_copy(XT[:, :, t * P:(t + 1) * P], MB[:, 0:D].rearrange("p (c t) -> p c t", c=DC))\
                      .then_inc(misc_free, 1)

            def project(m, par):
                for h in range(HC):
                    dve.wait_ge(misc_done, fb(m) + TT + h + 1)
                    nc.vector.tensor_scalar(HX[:, h, :], MB[:, :], bmc[:, h:h + 1], None, ALU.add)\
                      .then_inc(misc_free, 1)
                    dve.drain()
                    wait(dve, slices_stored[h], 16 * m)
                    nc.vector.tensor_copy(PCH[:, h, 0, :], HX[:, h, :])
                    dve.drain()
                    nc.vector.tensor_tensor(REM[:, :], HX[:, h, :], PCH[:, h, 0, :], ALU.subtract)
                    dve.drain()
                    nc.vector.tensor_copy(PCH[:, h, 1, :], REM[:, :])
                    dve.drain()
                    nc.vector.tensor_tensor(PCH[:, h, 2, :], REM[:, :], PCH[:, h, 1, :], ALU.subtract)\
                      .then_inc(slices_ready, 1)
                    dve.drain()

            def logits(m, par):
                dve.wait_ge(misc_done, fb(m) + TT + HC + 1)
                nc.vector.tensor_copy(LS[:, :, :, :], MB[:, :]).then_inc(misc_free, 1)
                dve.drain()
                for t in range(TT):
                    for h in range(H):
                        nc.vector.max(M8[:, t, h, :], LS[:, t, h, :])
                dve.drain()
                flat = lambda a: a.rearrange("p t h e -> p (t h) e")
                ls, m8 = flat(LS[:, :, :, :]), flat(M8[:, :, :, :])
                nc.vector.tensor_tensor(flat(LM[:, :, :, :]), ls, m8[:, :, 0:1].to_broadcast([P, TT * H, E]), ALU.subtract)\
                  .then_inc(lm_ready, 1)
                nc.vector.tensor_tensor(flat(MK[:, :, :, :]), ls, m8[:, :, 1:2].to_broadcast([P, TT * H, E]), ALU.is_ge)

            def weigh(m, par):
                flat = lambda a: a.rearrange("p t h e -> p (t h) e")
                dve.wait_ge(ex_ready, m + 1)
                nc.vector.tensor_reduce(RZ[:, :, :], EX[:, :, :, :], AX.X, ALU.add)
                dve.drain()
                nc.vector.reciprocal(RZ[:, :, :], RZ[:, :, :])
                nc.vector.tensor_tensor(EX[:, :, :, :], EX[:, :, :, :], MK[:, :, :, :], ALU.mult)
                dve.drain()
                for g in range(2):
                    src = EX[:, :, :, :].rearrange("p t (c j) (g e) -> p g (t c) j e", c=HC, g=2)
                    dst = EXP[:, :, :].rearrange("p t (c g j e) -> p g (t c) j e", c=HC, g=2, j=G)
                    rz = RZ[:, :, :].rearrange("p t (c j) -> p (t c) j", c=HC).unsqueeze(3)
                    mult = nc.vector.tensor_tensor(dst[:, g], src[:, g], rz.to_broadcast([P, TT * HC, G, E // 2]), ALU.mult)
                mult.then_inc(gates_ready, 1)

            def turn_gates(m, par):
                dve.wait_ge(misc_done, fb(m) + TT + HC + 2)
                wait(dve, gates_stored, 16 * m)
                nc.vector.tensor_copy(PCG[:, 0, :], MB[:, :])
                dve.drain()
                nc.vector.tensor_tensor(REM[:, :], MB[:, :], PCG[:, 0, :], ALU.subtract).then_inc(misc_free, 1)
                dve.drain()
                nc.vector.tensor_copy(PCG[:, 1, :], REM[:, :])
                dve.drain()
                nc.vector.tensor_tensor(PCG[:, 2, :], REM[:, :], PCG[:, 1, :], ALU.subtract).then_inc(gparts_ready, 1)

            def outputs(m, base):
                for t in range(TT):
                    dve.wait_ge(misc_done, base + t + 1)
                    nc.vector.tensor_tensor(X[:, TT * m + t, :], X[:, TT * m + t, :], MB[:, 0:D], ALU.add)\
                      .then_inc(misc_free, 1)

            def gate_unit(m, u):
                n = NU * m + u
                dve.wait_ge(g_done, n + 1)
                nc.vector.tensor_copy(GS[:, u % 2, :], GP[:, :]).then_inc(gs_ready, 1)
                dve.drain()
                dve.wait_ge(o_done, n + 3)
                dve.wait_ge(y_added, n + 2)
                hc, e = divmod(u, E)
                nc.vector.scalar_tensor_tensor(out=Y[:, u % 2, :] if e else CM[:, hc, :], in0=OP[u % 2][:, :], scalar=b2c[:, u % E:u % E + 1],
                                               in1=GS[:, u % 2, :], op0=ALU.add, op1=ALU.mult).then_inc(y_ready, 1)

            front = {"x": turn_x, "h": project, "l": logits, "w": weigh, "g": turn_gates}

            def one_block(m, par, last):
                for u in range(NU + 1):
                    if u >= 1:
                        gate_unit(m, u - 1)
                    if u in FRONT_AT and not last:
                        if FRONT_AT[u] == "x":
                            norm(m + 1)
                        front[FRONT_AT[u]](m + 1, 1 - par)
                outputs(m, UPM * m + 2 * (UPM - TT) if not last else UPM * m + UPM - TT)

            norm(0)
            for part in "xhlwg":
                front[part](0, 0)
            if NM > 2:
                with dve.Fori(0, NM // 2 - 1) as i:
                    one_block(2 * i, 0, False)
                    one_block(2 * i + 1, 1, False)
            one_block(NM - 2, 0, False)
            one_block(NM - 1, 1, True)


def make_idents(nc, ident, identb):
    with ExitStack() as ctx:
        zeroed = ctx.enter_context(nc.semaphore("ident_zeroed"))
        made = ctx.enter_context(nc.semaphore("ident_made"))
        with nc.Block() as block:
            @block.gpsimd
            def _(pool):
                for m in (ident, identb):
                    nc.gpsimd.memset(m[:, :], 0.0).then_inc(zeroed, 1)
                pool.wait_ge(zeroed, 2)
                for m in (ident, identb):
                    nc.gpsimd.affine_select(out=m[:, :], in_=m[:, :], compare_op=ALU.not_equal, fill=1.0,
                                            base=0, pattern=[[-1, P]], channel_multiplier=1).then_inc(made, 1)
                pool.wait_ge(made, 2)


def store_x(nc, ctx, out, X, B):
    stored = ctx.enter_context(nc.semaphore("x_stored"))
    with nc.Block() as block:
        @block.sync
        def _(sp):
            for b in range(B):
                sp.dma_start(out[b].rearrange("(t p) d -> p t d", p=P),
                             X[:, KT * b:KT * (b + 1), :]).then_inc(stored, 16)
            sp.wait_ge(stored, 16 * B)


def program(nc, a, out):
    B = a["L0_attn_x"].shape[0]
    NT = B * KT
    with ExitStack() as ctx:
        X = ctx.enter_context(nc.sbuf_tensor("x_tiles", [P, NT, D], F32))
        MEAN = ctx.enter_context(nc.sbuf_tensor("ln_mean", [P, NT], F32))
        RS = ctx.enter_context(nc.sbuf_tensor("ln_rstd", [P, NT], F32))
        ident = ctx.enter_context(nc.sbuf_tensor("ident", [P, P], F32))
        identb = ctx.enter_context(nc.sbuf_tensor("ident_bf16", [P, P], BF16))
        make_idents(nc, ident, identb)
        load_x(nc, ctx, a["L0_attn_x"], X, B)
        ln_scales(nc, X, MEAN, RS, NT, "a0")
        causal_attention(nc, X, MEAN, RS, B, a["L0_attn_Wq"], a["L0_attn_Wk"], a["L0_attn_Wv"], ident, identb)
        ln_scales(nc, X, MEAN, RS, NT, "f0")
        expert_ffn(nc, X, MEAN, RS, B, *(a["L0_ffn_" + n] for n in (
            "Wg", "bg", "Wu", "bu", "Wd", "bd", "Wq", "keys", "down_embed", "up_embed")), ident)
        ln_scales(nc, X, MEAN, RS, NT, "a1")
        rotary_attention(nc, X, MEAN, RS, B, *(a["L1_attn_" + n] for n in ("wq", "wk", "wv", "wo")),
                         a["rotation_cos"], a["rotation_sin"], ident)
        ln_scales(nc, X, MEAN, RS, NT, "f1")
        mixture_ffn(nc, X, MEAN, RS, B, *(a["L1_ffn_" + n] for n in (
            "Wm", "bm", "expert_emb", "W1", "b1", "W2", "b2", "Wo", "bo")), ident)
        store_x(nc, ctx, out, X, B)


_INS = ["L0_attn_x", "L0_attn_Wq", "L0_attn_Wk", "L0_attn_Wv",
        "L0_ffn_Wg", "L0_ffn_bg", "L0_ffn_Wu", "L0_ffn_bu",
        "L0_ffn_Wd", "L0_ffn_bd", "L0_ffn_Wq", "L0_ffn_keys",
        "L0_ffn_down_embed", "L0_ffn_up_embed", "L1_attn_wq", "L1_attn_wk",
        "L1_attn_wv", "L1_attn_wo", "L1_ffn_Wm", "L1_ffn_bm",
        "L1_ffn_expert_emb", "L1_ffn_W1", "L1_ffn_b1", "L1_ffn_W2",
        "L1_ffn_b2", "L1_ffn_Wo", "L1_ffn_bo"]


def kernel(**inputs):
    import numpy as _np
    import concourse.bacc as _bacc
    from concourse import mybir as _mybir
    from concourse.bass_utils import run_bass_kernel_spmd as _run

    nc = _bacc.Bacc("TRN2", target_bir_lowering=False, num_devices=1)
    arrays, args = {}, {}
    for name in _INS:
        x = _np.ascontiguousarray(inputs[name])
        arrays[f"in_{name}"] = x
        args[name] = nc.dram_tensor(f"in_{name}", x.shape, _mybir.dt.from_np(x.dtype), kind="ExternalInput").ap()
    shape = inputs["L0_attn_x"].shape
    for name, x in zip(("rotation_cos", "rotation_sin"), rotation_tables(shape[1], inputs["L1_attn_wq"].shape[0])):
        arrays[name] = x
        args[name] = nc.dram_tensor(name, x.shape, _mybir.dt.float32, kind="ExternalInput").ap()
    out = nc.dram_tensor("out_x", shape, _mybir.dt.float32, kind="ExternalOutput").ap()
    program(nc, args, out)
    r = _run(nc, [arrays], core_ids=[0])
    return r.results[0]["out_x"]
```

```python
from contextlib import ExitStack

import numpy as np

import concourse.bass as bass
from concourse import mybir

F32 = mybir.dt.float32
BF16 = mybir.dt.bfloat16
ALU = mybir.AluOpType
ACT = mybir.ActivationFunctionType
AX = mybir.AxisListType
P = 128
D = 256
DC = D // P
T = 1024
KT = T // P
BANK = 512
EPS = 1e-5
FAR = -1e30


def wait(engine, sem, value):
    if not isinstance(value, int) or value > 0:
        engine.wait_ge(sem, value)


def load_x(nc, x, X, STATS, B, loads, consts):
    with ExitStack() as ctx:
        loaded = [ctx.enter_context(nc.semaphore(f"x_loaded{b}")) for b in range(B)]
        with nc.Block() as block:
            @block.sync
            def _(sp):
                for b in range(B):
                    sp.dma_start(X[:, KT * b:KT * (b + 1), :],
                                 x[b].rearrange("(t p) d -> p t d", p=P)).then_inc(loaded[b], 16)
                loads(sp)

            @block.gpsimd
            def _(pool):
                consts(pool)

            @block.vector
            def _(dve):
                for b in range(B):
                    dve.wait_ge(loaded[b], 16)
                    for t in range(KT):
                        tile_stats(nc, X, STATS, KT * b + t)


def tile_stats(nc, X, STATS, t):
    nc.vector.bn_stats(STATS[:, t, :], X[:, t, :])


def ln_scales(nc, STATS, MEAN, RS, tag, loads=None, consts=None):
    with ExitStack() as ctx:
        VE, DM, SD, R0, R1 = (STATS[:, :, i] for i in (0, 3, 1, 4, 2))
        var_ready = ctx.enter_context(nc.semaphore(f"var_ready_{tag}"))
        sd_ready = ctx.enter_context(nc.semaphore(f"sd_ready_{tag}"))
        with nc.Block() as block:
            if loads is not None:
                @block.sync
                def _(sp):
                    loads(sp)

            if consts is not None:
                @block.gpsimd
                def _(pool):
                    consts(pool)

            @block.vector
            def _(dve):
                nc.vector.tensor_tensor(MEAN[:, :], STATS[:, :, 1], STATS[:, :, 4], ALU.add)
                nc.vector.tensor_tensor(DM, STATS[:, :, 1], STATS[:, :, 4], ALU.subtract)
                nc.vector.tensor_tensor(VE, STATS[:, :, 2], STATS[:, :, 5], ALU.add)
                dve.drain()
                nc.vector.tensor_scalar(MEAN[:, :], MEAN[:, :], 0.5, None, ALU.mult)
                nc.vector.tensor_tensor(DM, DM, DM, ALU.mult)
                nc.vector.tensor_scalar(VE, VE, 1.0 / D, EPS, ALU.mult, ALU.add)
                dve.drain()
                nc.vector.scalar_tensor_tensor(out=VE, in0=DM, scalar=0.25, in1=VE,
                                               op0=ALU.mult, op1=ALU.add).then_inc(var_ready, 1)
                dve.wait_ge(sd_ready, 1)
                dve.wait_ge(var_ready, 1)
                nc.vector.reciprocal(R0, SD)
                dve.drain()
                nc.vector.tensor_tensor(R1, R0, R0, ALU.mult)
                dve.drain()
                nc.vector.tensor_tensor(R1, R1, VE, ALU.mult)
                dve.drain()
                nc.vector.tensor_scalar(R1, R1, -0.5, 1.5, ALU.mult, ALU.add)
                dve.drain()
                nc.vector.tensor_tensor(RS[:, :], R0, R1, ALU.mult)

            @block.scalar
            def _(act):
                act.wait_ge(var_ready, 1)
                nc.scalar.activation(SD, VE, ACT.Sqrt).then_inc(sd_ready, 1)


def causal_attention(nc, x, X, STATS, MEAN, RS, B, Wq, Wk, Wv, ident, identb):
    H, HS = Wq.shape[0], Wq.shape[2]
    HH = H // 2
    G = 4
    PARTS_Q = (0, 0, 1, 1, 0, 2)
    PARTS_K = (0, 1, 0, 1, 2, 0)
    K6 = len(PARTS_Q) * HS
    K9 = K6 + 3
    SCALE = 1.0 / float(np.sqrt(D))
    MAXU = sorted(((h, n, qt, kc) for qt in range(KT) for kc in range(qt // 4 + 1)
                   for n in (min(2, BANK // min(BANK, (qt + 1) * P - kc * BANK)),) for h in range(0, G, n)),
                  key=lambda u: (u[0] + u[1], u))

    SCORES = [(g, kt, j, c) for g in range(2) for kt in range(KT) for j in range(G) for c in range(kt // 4, 2)]

    def back_pieces():
        out = []
        for g in range(2):
            for kt in range(KT + 1):
                out += [("s", g, kt, j) for j in range(G) if kt < KT]
                out += [("v", g, kt - 1, c, j) for c in range((kt - 1) // 4, 2) for j in range(G) if kt > 0]
        return out

    def projections(hf):
        return [("x", t) for t in range(KT) if hf == 0] + [("p", u) for u in range(4)]

    VALUES = [("v", q) for q in range(2)]
    MAXIMA = [u for g in range(2) for u in [("m", g, *m) for m in MAXU] + [("t", g)]]

    BACK = back_pieces()
    FIRST_MAX = 24
    OUT_AT = len(BACK) // 2 + 14

    def filling(next_hf, third_hf):
        after = [[] for _ in BACK]
        if next_hf is not None:
            head = VALUES + (projections(third_hf) if third_hf is not None else [])
            for i, u in enumerate(head):
                after[i].append(u)
            cost = [100 + (u[3] * min(BANK, (u[4] + 1) * P - u[5] * BANK) if u[0] == "m" else BANK) for u in MAXIMA]
            columns = [100 + T - p[2] * P if p[0] == "s" else 100 + (p[3] + 1) * BANK - max(p[2] * P, p[3] * BANK)
                       for p in BACK]
            done, spent, at = 0, 0, FIRST_MAX
            for u, c in zip(MAXIMA, cost):
                while done * sum(cost) < spent * sum(columns[FIRST_MAX:]):
                    done += columns[at]
                    at += 1
                after[min(at, len(BACK) - 1)].append(u)
                spent += c
        after[OUT_AT].append(("o", 0))
        after[-1].append(("o", 1))
        return after

    NPT = 8

    with ExitStack() as ctx:
        def sb(name, shape, dt=F32):
            return ctx.enter_context(nc.sbuf_tensor(name, shape, dt))

        def sem(name):
            return ctx.enter_context(nc.semaphore(name))

        wq = sb("wq_sb", [P, DC, H, HS])
        wk = sb("wk_sb", [P, DC, H, HS])
        wv = sb("wv_sb", [P, DC, H, HS])
        maskq = sb("mask_query_major", [P, P], BF16)
        maskk = sb("mask_key_major", [P, P], BF16)
        XT = sb("xnT", [P, DC, T])
        V = sb("values", [P, 2, KT, HH, 32])
        QS = sb("q_stack", [P, 2, HH, T], BF16)
        KS = sb("k_stack", [P, 2, HH, T], BF16)
        PT = sb("probsT", [P, NPT, T])
        REM = sb("split_rest", [P, BANK])
        PC = sb("split_parts", [P, 2, 3, BANK], BF16)
        M2 = sb("maxima", [P, HH, KT, 2])
        NM = sb("row_max", [P, 2, G * KT])
        MREM = sb("max_rest", [G * KT, P])
        MP = sb("max_parts", [G * KT, 3, P], BF16)
        OS = sb("outT", [P, 2 * BANK])
        RZ = sb("recip_sum", [P, 4, G])
        XN = OS[:, 0:2 * D].rearrange("p (s d) -> p s d", s=2)
        ON = REM[:, 0:4 * G * HS].rearrange("p (t j d) -> p t j d", t=4, j=G)
        F = [ctx.enter_context(nc.psum_tensor(f"front{i}", [P, BANK], F32)) for i in range(3)]
        ST = [ctx.enter_context(nc.psum_tensor(f"scoresT{i}", [P, BANK], F32)) for i in range(3)]
        PV = ctx.enter_context(nc.psum_tensor("pv", [P, 2 * BANK], F32))
        part_d = nc.dram_tensor("split_scratch", [2, 2, 3, P, T], BF16).ap()
        max_d = nc.dram_tensor("max_scratch", [2, 2, 3, G * KT, P], BF16).ap()

        weights_in = sem("weights_in")
        consts_ready = sem("consts_ready")
        masks_zeroed = sem("masks_zeroed")
        xn_ready = sem("xn_ready")
        front_done = sem("front_done")
        front_free = sem("front_free")
        parts_ready = sem("parts_ready")
        parts_stored = [sem(f"parts_stored{i}") for i in range(2)]
        stacks_in = sem("stacks_in")
        maxp_ready = sem("maxp_ready")
        maxp_stored = sem("maxp_stored")
        maxrows_in = [sem(f"maxrows_in{g}") for g in range(2)]
        rowmax_ready = sem("rowmax_ready")
        scores_ready = sem("scores_ready")
        probs_ready = sem("probs_ready")
        pv_done = sem("pv_done")
        out_ready = sem("out_ready")
        outs_added = sem("outs_added")

        UPB = KT + 2 * (2 + 4 + len(MAXIMA) + 4)
        SPB = 2 * len(SCORES)
        VPB = 4 * KT

        AHEAD = 512

        def stack_released(n):
            return 2 + 2 * KT * (n - 1)

        def used_before(n):
            return not isinstance(n, int) or n >= 2

        def loads(sp):
            for w, dst in ((Wq, wq), (Wk, wk), (Wv, wv)):
                for c in range(DC):
                    sp.dma_start(dst[:, c, :, :], w[:, c * P:(c + 1) * P, :].rearrange("h p d -> p h d"))\
                      .then_inc(weights_in, 16)

        def consts(pool):
            nc.gpsimd.memset(maskq[:, :], 0.0).then_inc(masks_zeroed, 1)
            nc.gpsimd.memset(maskk[:, :], 0.0).then_inc(masks_zeroed, 1)
            nc.gpsimd.memset(V[:, :, :, :, HS:32], 0.0).then_inc(masks_zeroed, 1)
            pool.wait_ge(masks_zeroed, 3)
            nc.gpsimd.memset(KS[K6:K9, :, :, :], 1.0).then_inc(consts_ready, 1)
            pool.wait_ge(consts_ready, 1)
            nc.gpsimd.affine_select(out=maskq[:, :], in_=maskq[:, :], compare_op=ALU.is_ge, fill=FAR,
                                    base=0, pattern=[[-1, P]], channel_multiplier=1).then_inc(consts_ready, 1)
            nc.gpsimd.affine_select(out=maskk[:, :], in_=maskk[:, :], compare_op=ALU.is_ge, fill=FAR,
                                    base=0, pattern=[[1, P]], channel_multiplier=-1).then_inc(consts_ready, 1)
            nc.gpsimd.memset(V[:, :, :, :, HS:HS + 1], 1.0).then_inc(consts_ready, 1)

        load_x(nc, x, X, STATS, B, loads, consts)
        ln_scales(nc, STATS, MEAN, RS, "a0")
        block = ctx.enter_context(nc.Block())

        @block.sync
        def _(sp):
            def store_parts(b, hf):
                n = 2 * b + hf
                for side in range(2):
                    for c in range(2):
                        sp.wait_ge(parts_ready, 4 * n + 2 * side + c + 1)
                        sp.dma_start(part_d[hf, side, :, :, c * BANK:(c + 1) * BANK].rearrange("s r t -> r s t"),
                                     PC[:, c, :, :]).then_inc(parts_stored[c], 16)

            def load_stacks(b, hf):
                n = 2 * b + hf
                for c in range(2):
                    sp.wait_ge(parts_stored[c], 16 * 2 * (n + 1))
                if used_before(n):
                    sp.wait_ge(pv_done, stack_released(n))
                for side, (parts, stack) in enumerate(((PARTS_Q, QS), (PARTS_K, KS))):
                    for s, part in enumerate(parts):
                        sp.dma_start(stack[HS * s:HS * (s + 1), hf, :, :],
                                     part_d[hf, side, part].rearrange("(h d) t -> d h t", d=HS))\
                          .then_inc(stacks_in, 16)

            def maxima(b, hf):
                for g in range(2):
                    m = 2 * (2 * b + hf) + g
                    sp.wait_ge(maxp_ready, m + 1)
                    sp.dma_start(max_d[hf, g].rearrange("s r t -> r s t"), MP[:, :, :]).then_inc(maxp_stored, 16)
                    sp.wait_ge(maxp_stored, 16 * (m + 1))
                    sp.dma_start(QS[K6:K9, hf, G * g:G * (g + 1), :],
                                 max_d[hf, g].rearrange("s (h t) q -> s h (t q)", h=G)).then_inc(maxrows_in[g], 16)

            store_parts(0, 0)
            load_stacks(0, 0)
            store_parts(0, 1)
            maxima(0, 0)
            if B > 1:
                with sp.Fori(0, B - 1) as b:
                    load_stacks(b, 1)
                    store_parts(b + 1, 0)
                    maxima(b, 1)
                    load_stacks(b + 1, 0)
                    store_parts(b + 1, 1)
                    maxima(b + 1, 0)
            load_stacks(B - 1, 1)
            maxima(B - 1, 1)

        @block.tensor
        def _(pe):
            pe.sem_inc(pv_done, 2)
            pe.wait_ge(weights_in, 16 * 3 * DC)
            pe.wait_ge(consts_ready, 4)

            def fill(unit, base, k, b, hf):
                kind = unit[0]
                n = 2 * b + hf
                if kind == "o":
                    return turn_out(b, base, k, hf, unit[1])
                if kind == "x":
                    pe.wait_ge(xn_ready, KT * b + unit[1] + 1)
                elif unit == ("p", 0) and hf == 0:
                    pe.wait_ge(front_free, AHEAD + base + k + 3)
                elif unit == MAXIMA[0]:
                    pe.wait_ge(stacks_in, 16 * 12 * (n + 1))
                elif kind == "t":
                    pe.wait_ge(rowmax_ready, 2 * n + unit[1] + 1)
                pe.wait_ge(front_free, AHEAD + base + k + 1)
                bank = F[k % 3]
                if kind == "x":
                    t = unit[1]
                    for c in range(DC):
                        mm = nc.tensor.transpose(bank[:, c * P:(c + 1) * P], XN[:, t % 2, c * P:(c + 1) * P], ident[:, :])
                elif kind == "v":
                    for t in range(4):
                        for c in range(DC):
                            tok = slice((4 * unit[1] + t) * P, (4 * unit[1] + t + 1) * P)
                            mm = nc.tensor.matmul(bank[:, t * P:(t + 1) * P], XT[:, c, tok],
                                                  wv[:, c, HH * hf:HH * (hf + 1), :], start=(c == 0), stop=(c == DC - 1))
                elif kind == "p":
                    side, q = divmod(unit[1], 2)
                    for c in range(DC):
                        mm = nc.tensor.matmul(bank[:, :], (wq, wk)[side][:, c, HH * hf:HH * (hf + 1), :],
                                              XT[:, c, q * BANK:(q + 1) * BANK], start=(c == 0), stop=(c == DC - 1))
                elif kind == "m":
                    _, g, h0, heads, qt, kc = unit
                    w = min(BANK, (qt + 1) * P - kc * BANK)
                    diag = kc == qt // 4
                    for i in range(heads):
                        h = G * g + h0 + i
                        mm = nc.tensor.matmul(bank[:, i * w:(i + 1) * w], QS[0:K6, hf, h, qt * P:(qt + 1) * P],
                                              KS[0:K6, hf, h, kc * BANK:kc * BANK + w], start=True, stop=not diag)
                        if diag:
                            mm = nc.tensor.matmul(bank[:, (i + 1) * w - P:(i + 1) * w], identb[:, :], maskq[:, :],
                                                  start=False, stop=True)
                elif kind == "t":
                    mm = nc.tensor.transpose(bank[0:G * KT, 0:P], NM[:, unit[1], :], ident[:, :])
                mm.then_inc(front_done, 1)
                return k + 1

            def turn_out(b, base, k, hf, g):
                pe.wait_ge(out_ready, 4 * b + 2 * hf + g + 2)
                for c in range(2):
                    pe.wait_ge(front_free, AHEAD + base + k + 1)
                    for t in range(4):
                        mm = nc.tensor.transpose(F[k % 3][:, t * P:(t + 1) * P],
                                                 OS[:, (4 * c + t) * P:(4 * c + t + 1) * P], ident[:, :])
                    mm.then_inc(front_done, 1)
                    k += 1
                return k

            def scores(b, hf, g, kt, j):
                h = G * g + j
                if kt == 0 and j == 0:
                    pe.wait_ge(maxrows_in[g], 16 * (2 * b + hf + 1))
                for c in range(kt // 4, 2):
                    i = SCORES.index((g, kt, j, c)) + hf * len(SCORES)
                    pe.wait_ge(probs_ready, SPB * b + i + 1)
                    bank = ST[i % 3]
                    q0 = max(kt * P, c * BANK)
                    at = q0 - c * BANK
                    diag = c == kt // 4
                    mm = nc.tensor.matmul(bank[:, at:BANK], KS[0:K9, hf, h, kt * P:(kt + 1) * P],
                                          QS[0:K9, hf, h, q0:(c + 1) * BANK], start=True, stop=not diag)
                    if diag:
                        mm = nc.tensor.matmul(bank[:, at:at + P], identb[:, :], maskk[:, :], start=False, stop=True)
                    mm.then_inc(scores_ready, 1)

            def values(b, hf, g, kt, c, j):
                x = ((2 * hf + g) * KT + kt) * G
                if c == kt // 4 and j == 0:
                    pe.wait_ge(probs_ready, SPB * b + hf * len(SCORES) + SCORES.index((g, kt, G - 1, 1)) + 4)
                    if kt == 0:
                        pe.wait_ge(out_ready, 4 * b + 2 * hf + g + 1)
                q0 = max(kt * P, c * BANK)
                mm = nc.tensor.matmul(PV[32 * j:32 * (j + 1), q0:(c + 1) * BANK], V[:, hf, kt, G * g + j, :],
                                      PT[:, (x + j) % NPT, q0:(c + 1) * BANK],
                                      start=(kt == 0), stop=(kt == 4 * c + 3), tile_position=(0, 32 * j))
                if c == 1 and j == G - 1:
                    mm.then_inc(pv_done, 1)

            def step(b, hf, base, k, following, third):
                for piece, after in zip(BACK, filling(following[1], third[1])):
                    if piece[0] == "s":
                        scores(b, hf, *piece[1:])
                    else:
                        values(b, hf, *piece[1:])
                    for unit in after:
                        k = fill(unit, base, k, *((b, hf) if unit[0] == "o" else third if unit[0] in "xp" else following))
                return k

            k0 = 0
            for unit in projections(0) + VALUES:
                k0 = fill(unit, 0, k0, 0, 0)
            for unit in projections(1):
                k0 = fill(unit, 0, k0, 0, 1)
            for unit in MAXIMA:
                k0 = fill(unit, 0, k0, 0, 0)
            if B > 1:
                with pe.Fori(0, B - 1) as b:
                    k = step(b, 0, UPB * b, k0, (b, 1), (b + 1, 0))
                    k = step(b, 1, UPB * b, k, (b + 1, 0), (b + 1, 1))
                    assert k == k0 + UPB and UPB % 3 == 0 and SPB % 3 == 0
            k = step(B - 1, 0, UPB * (B - 1), k0, (B - 1, 1), (None, None))
            step(B - 1, 1, UPB * (B - 1), k, (None, None), (None, None))

        @block.scalar
        def _(act):
            act.sem_inc(probs_ready, 3)
            act.sem_inc(out_ready, 1)
            with act.Fori(0, B) as b:
                for i, (g, kt, j, c) in enumerate(SCORES + SCORES):
                    g += i // len(SCORES) * 2
                    x = (g * KT + kt) * G + j
                    act.wait_ge(scores_ready, SPB * b + i + 1)
                    if j == 0 and c == kt // 4:
                        act.wait_ge(pv_done, VPB * b + x // G + 1)
                    q0 = max(kt * P, c * BANK)
                    nc.scalar.activation(PT[:, x % NPT, q0:(c + 1) * BANK], ST[i % 3][:, q0 - c * BANK:BANK], ACT.Exp,
                                         scale=SCALE).then_inc(probs_ready, 1)
                    if (kt, j, c) != (KT - 1, G - 1, 1):
                        continue
                    act.wait_ge(pv_done, VPB * b + (g + 1) * KT + 2)
                    act.wait_ge(outs_added, 4 * b + g + 1)
                    nc.scalar.activation(OS[:, :], PV[:, :], ACT.Copy).then_inc(out_ready, 1)

        @block.vector
        def _(dve):
            dve.sem_inc(front_free, AHEAD + 3)
            dve.sem_inc(outs_added, 1)
            nc.vector.memset(M2[:, :, :, :], -3e38)

            def norm(b, t):
                nc.vector.tensor_scalar(XN[:, t % 2, :], X[:, KT * b + t, :], MEAN[:, bass.ds(KT * b + t, 1)],
                                        RS[:, bass.ds(KT * b + t, 1)], ALU.subtract, ALU.mult).then_inc(xn_ready, 1)

            def empty(unit, base, k, b, hf):
                kind = unit[0]
                n = 2 * b + hf
                if kind == "o":
                    return add_out(b, base, k, hf, unit[1])
                bank = F[k % 3]
                if kind == "x" and unit[1] == 0:
                    norm(b, 0)
                    norm(b, 1)
                if kind == "v" and unit[1] == 0 and used_before(n):
                    dve.wait_ge(pv_done, stack_released(n))
                dve.wait_ge(front_done, base + k + 1)
                if kind == "x":
                    t = unit[1]
                    nc.vector.tensor_copy(XT[:, :, t * P:(t + 1) * P], bank[:, 0:D].rearrange("p (c t) -> p c t", c=DC))\
                      .then_inc(front_free, 1)
                    if t + 2 < KT:
                        norm(b, t + 2)
                elif kind == "v":
                    nc.vector.tensor_copy(V[:, hf, 4 * unit[1]:4 * unit[1] + 4, :, 0:HS],
                                          bank[:, :].rearrange("p (t h d) -> p t h d", t=4, h=HH)).then_inc(front_free, 1)
                elif kind == "p":
                    u = unit[1]
                    pc = PC[:, u % 2, :, :]
                    wait(dve, parts_stored[u % 2], 16 * (2 * n + u // 2))
                    nc.vector.tensor_copy(pc[:, 0, :], bank[:, :])
                    dve.drain()
                    nc.vector.tensor_tensor(REM[:, :], bank[:, :], pc[:, 0, :], ALU.subtract).then_inc(front_free, 1)
                    dve.drain()
                    nc.vector.tensor_copy(pc[:, 1, :], REM[:, :])
                    dve.drain()
                    nc.vector.tensor_tensor(pc[:, 2, :], REM[:, :], pc[:, 1, :], ALU.subtract).then_inc(parts_ready, 1)
                elif kind == "m":
                    _, g, h0, heads, qt, kc = unit
                    w = min(BANK, (qt + 1) * P - kc * BANK)
                    hs = slice(G * g + h0, G * g + h0 + heads)
                    nc.vector.tensor_reduce(M2[:, hs, qt, kc], bank[:, 0:heads * w].rearrange("p (h k) -> p h k", h=heads),
                                            AX.X, ALU.max).then_inc(front_free, 1)
                    if unit[2:] == MAXU[-1]:
                        dve.drain()
                        nc.vector.tensor_tensor(NM[:, g, :].rearrange("p (h t) -> p h t", h=G),
                                                M2[:, G * g:G * (g + 1), :, 0], M2[:, G * g:G * (g + 1), :, 1],
                                                ALU.max).then_inc(rowmax_ready, 1)
                elif kind == "t":
                    wait(dve, maxp_stored, 16 * (2 * n + unit[1]))
                    turned = bank[0:G * KT, 0:P]
                    nc.vector.tensor_scalar(MP[:, 0, :], turned, -1.0, None, ALU.mult)
                    dve.drain()
                    nc.vector.scalar_tensor_tensor(out=MREM[:, :], in0=turned, scalar=-1.0, in1=MP[:, 0, :],
                                                   op0=ALU.mult, op1=ALU.subtract).then_inc(front_free, 1)
                    dve.drain()
                    nc.vector.tensor_copy(MP[:, 1, :], MREM[:, :])
                    dve.drain()
                    nc.vector.tensor_tensor(MP[:, 2, :], MREM[:, :], MP[:, 1, :], ALU.subtract).then_inc(maxp_ready, 1)
                return k + 1

            def add_out(b, base, k, hf, g):
                for c in range(2):
                    dve.wait_ge(front_done, base + k + 1)
                    o = F[k % 3][:, :].rearrange("p (t j e) -> p t j e", t=4, j=G)
                    nc.vector.reciprocal(RZ[:, :, :], o[:, :, :, HS])
                    dve.drain()
                    nc.vector.tensor_tensor(ON, o[:, :, :, 0:HS], RZ[:, :, :].unsqueeze(3).to_broadcast([P, 4, G, HS]),
                                            ALU.mult).then_inc(front_free, 1)
                    dve.drain()
                    cols = slice((hf * HH + g * G) * HS, (hf * HH + (g + 1) * G) * HS)
                    xs = X[:, bass.ds(KT * b + 4 * c, 4), cols]
                    add = nc.vector.tensor_tensor(xs, xs, ON.rearrange("p t j d -> p t (j d)"), ALU.add)
                    k += 1
                add.then_inc(outs_added, 1)
                return k

            def step(b, hf, base, k, following, third):
                for after in filling(following[1], third[1]):
                    for unit in after:
                        k = empty(unit, base, k, *((b, hf) if unit[0] == "o" else third if unit[0] in "xp" else following))
                if hf == 1:
                    dve.drain()
                    for t in range(KT):
                        tile_stats(nc, X, STATS, KT * b + t)
                return k

            k0 = 0
            for unit in projections(0) + VALUES:
                k0 = empty(unit, 0, k0, 0, 0)
            for unit in projections(1):
                k0 = empty(unit, 0, k0, 0, 1)
            for unit in MAXIMA:
                k0 = empty(unit, 0, k0, 0, 0)
            if B > 1:
                with dve.Fori(0, B - 1) as b:
                    k = step(b, 0, UPB * b, k0, (b, 1), (b + 1, 0))
                    k = step(b, 1, UPB * b, k, (b + 1, 0), (b + 1, 1))
            k = step(B - 1, 0, UPB * (B - 1), k0, (B - 1, 1), (None, None))
            step(B - 1, 1, UPB * (B - 1), k, (None, None), (None, None))


def expert_weights(nc, WQ, KY, DN, loaded, MT, DT, WQT, KB, ident):
    NK, _, H, KD = KY.shape
    NB = DN.shape[1]
    with ExitStack() as ctx:
        PS = [ctx.enter_context(nc.psum_tensor(f"prep{i}", [P, BANK], F32)) for i in range(2)]
        filled = ctx.enter_context(nc.semaphore("prep_filled"))
        copied = ctx.enter_context(nc.semaphore("prep_copied"))
        zeroed = ctx.enter_context(nc.semaphore("prep_zeroed"))
        PAIRS = [(p, r) for p in range(2) for r in range(H // 2)]
        with nc.Block() as block:
            @block.tensor
            def _(pe):
                pe.wait_ge(loaded, 16 * (DC + 3))
                n = 0
                for s, r in PAIRS:
                    wait(pe, copied, n - 1)
                    for c in range(DC):
                        mm = nc.tensor.transpose(PS[n % 2][:, c * P:(c + 1) * P],
                                                 WQ[:, c, s, 2 * r * KD:2 * (r + 1) * KD], ident[:, :])
                    mm.then_inc(filled, 1)
                    n += 1
                for s, r in PAIRS:
                    wait(pe, copied, n - 1)
                    nc.tensor.transpose(PS[n % 2][:, 0:NK],
                                        KY[:, s, 2 * r:2 * (r + 1), :].rearrange("k h n -> k (h n)"),
                                        ident[0:NK, 0:NK]).then_inc(filled, 1)
                    n += 1
                for c in range(DC):
                    wait(pe, copied, n)
                    for i, (s, r) in enumerate(PAIRS):
                        mm = nc.tensor.matmul(PS[n % 2][:, i * P:(i + 1) * P], WQT[:, s, r, c * P:(c + 1) * P],
                                              KB[:, s, r, :], start=True, stop=True)
                    mm.then_inc(filled, 1)
                    n += 1
                for b in range(NB):
                    wait(pe, copied, n - 1)
                    for c in range(DC):
                        mm = nc.tensor.transpose(PS[n % 2][:, c * P:(c + 1) * P],
                                                 DN[:, b, c * P:(c + 1) * P], ident[:, :])
                    mm.then_inc(filled, 1)
                    n += 1

            @block.vector
            def _(dve):
                nc.vector.memset(KB[:, :, :, :], 0.0)
                dve.drain()
                n = 0
                for s, r in PAIRS:
                    dve.wait_ge(filled, n + 1)
                    nc.vector.tensor_copy(WQT[:, s, r, :], PS[n % 2][:, 0:D]).then_inc(copied, 1)
                    n += 1
                for s, r in PAIRS:
                    dve.wait_ge(filled, n + 1)
                    nc.vector.tensor_copy(KB[0:KD, s, r, 0:NK], PS[n % 2][0:KD, 0:NK])
                    nc.vector.tensor_copy(KB[KD:P, s, r, NK:P], PS[n % 2][KD:P, 0:NK]).then_inc(copied, 1)
                    n += 1
                for c in range(DC):
                    dve.wait_ge(filled, n + 1)
                    nc.vector.tensor_copy(MT[:, c, :], PS[n % 2][:, :]).then_inc(copied, 1)
                    n += 1
                for b in range(NB):
                    dve.wait_ge(filled, n + 1)
                    nc.vector.tensor_copy(DT[:, :, b * P:(b + 1) * P],
                                          PS[n % 2][:, 0:D].rearrange("p (c e) -> p c e", c=DC)).then_inc(copied, 1)
                    n += 1


def expert_ffn(nc, X, STATS, MEAN, RS, B, Wg, bg, Wu, bu, Wd, bd, Wq, keys, down, up, ident):
    H, NK, _, KD = keys.shape
    NE = down.shape[0]
    NB = NE // P
    NR = NE // NK
    FF = Wg.shape[1]
    FB = FF // P
    TT = 4
    TM = TT * P
    NM = B * KT // TT
    TOPK = 8
    with ExitStack() as ctx:
        def sb(name, shape, dt=F32):
            return ctx.enter_context(nc.sbuf_tensor(name, shape, dt))

        def sem(name):
            return ctx.enter_context(nc.semaphore(name))

        MT = sb("sim_weights", [P, DC, 2 * H * NK])
        DT = sb("downT", [P, DC, NE])
        UP = sb("up_sb", [P, NB, D])
        wg = sb("wg_sb", [P, DC, FF])
        wu = sb("wu_sb", [P, DC, FF])
        wd = sb("wd_sb", [P, FB, D])
        bgc = sb("bg_col", [P, FB])
        buc = sb("bu_col", [P, FB])
        bdr = sb("bd_rows", [P, D])
        XN = sb("xn0", [P, TT, D])
        XT = sb("xnT0", [P, DC, TM])
        SM = sb("sims", [P, TT, 2, H, NK])
        A = sb("pair_sums", [P, H, NE])
        E = sb("pair_exp", [P, 2, NE])
        S = sb("expert_weight", [P, TT, NE])
        SD = sb("silu_down", [P, NB, TM])
        GS = sb("silu_gate", [P, 2, TM])
        HT = sb("hiddenT", [P, FB, TM])
        TOP = sb("top_sims", [P, 2, H, TOPK])
        C = sb("candidates", [P, H, TOPK, TOPK])
        T8 = sb("top_pairs", [P, 2, H, TOPK])
        TD = sb("top_less_max", [P, H, TOPK])
        E8 = sb("top_exp", [P, H, TOPK])
        NMX = sb("neg_max", [P, 2, H])
        RZ = sb("recip_z", [P, H])
        SUM = sb("weight_sum", [P, 1])
        early, early2 = HT[:, :, :].rearrange("p f t -> p (f t)"), S[:, :, :].rearrange("p t e -> p (t e)")
        sizes = np.cumsum([0, DC * 2 * H * KD, 2 * H * KD, NB * D])
        WQ = early[:, sizes[0]:sizes[1]].rearrange("p (c s n) -> p c s n", c=DC, s=2)
        KY = early[0:NK, sizes[1]:sizes[2]].rearrange("p (s h n) -> p s h n", s=2, h=H)
        DN = early[:, sizes[2]:sizes[3]].rearrange("p (b d) -> p b d", b=NB)
        WQT = early2[:, 0:H * D].rearrange("p (s r d) -> p s r d", s=2, r=H // 2)
        KB = early2[:, H * D:H * (D + P)].rearrange("p (s r k) -> p s r k", s=2, r=H // 2)
        prep_in = sem("prep_in")

        def loads(sp):
            for c in range(DC):
                sp.dma_start(WQ[:, c, :, :], Wq[c * P:(c + 1) * P, :].rearrange("p (s n) -> p s n", s=2))\
                  .then_inc(prep_in, 16)
            for s in range(2):
                sp.dma_start(KY[:, s, :, :], keys[:, :, s, :].rearrange("h k n -> k h n")).then_inc(prep_in, 16)
            sp.dma_start(DN[:, :, :], down.rearrange("(b p) d -> p b d", p=P)).then_inc(prep_in, 16)
            for dst, src in moves:
                sp.dma_start(dst, src).then_inc(weights_in, 16)

        moves = [(UP[:, :, :], up.rearrange("(b p) d -> p b d", p=P)),
                 (wg[:, :, :], Wg.rearrange("(c p) f -> p c f", p=P)),
                 (wu[:, :, :], Wu.rearrange("(c p) f -> p c f", p=P)),
                 (wd[:, :, :], Wd.rearrange("(b p) d -> p b d", p=P)),
                 (bdr[:, :], bd.rearrange("(a d) -> a d", a=1).to_broadcast([P, D]))]
        for b in range(FB):
            moves.append((bgc[:, b:b + 1], bg[b * P:(b + 1) * P].rearrange("(p a) -> p a", a=1)))
            moves.append((buc[:, b:b + 1], bu[b * P:(b + 1) * P].rearrange("(p a) -> p a", a=1)))
        ALL_IN = 16 * len(moves)
        weights_in = sem("weights0_in")
        ln_scales(nc, STATS, MEAN, RS, "f0", loads)
        expert_weights(nc, WQ, KY, DN, prep_in, MT, DT, WQT, KB, ident)

        F = [ctx.enter_context(nc.psum_tensor(f"front0_{i}", [P, BANK], F32)) for i in range(2)]
        R = [ctx.enter_context(nc.psum_tensor(f"dense{i}", [P, BANK], F32)) for i in range(4)]
        UB = OB = R[2:4]
        SP = ctx.enter_context(nc.psum_tensor("weightT", [P, NB, P], F32))

        biased = sem("biased")
        xn_ready = sem("xn0_ready")
        front_done = sem("front0_done")
        front_free = sem("front0_free")
        dg_done = sem("dg_done")
        dg_free = sem("dg_free")
        u_done = sem("u_done")
        h_done = sem("h_done")
        t8_ready = sem("t8_ready")
        e8_ready = sem("e8_ready")
        a_ready = sem("a_ready")
        a_free = sem("a_free")
        e_ready = sem("e_ready")
        e_free = sem("e_free")
        tiles_begun = sem("tiles_begun")
        s_ready = sem("s_ready")
        st_done = sem("st_done")
        w_ready = sem("w_ready")
        out_done = sem("out_done")
        out_free = sem("out_free")

        block = ctx.enter_context(nc.Block())

        EXPS_AT = {5: (2, range(0, 2)), 9: (2, range(2, 4)), 11: (3, range(0, 2)), 13: (3, range(2, 4))}

        @block.tensor
        def _(pe):
            pe.wait_ge(weights_in, ALL_IN)

            def turn_xn(m, t):
                k = 2 * TT * m + t
                pe.wait_ge(xn_ready, TT * m + t + 1)
                pe.wait_ge(front_free, k + 1)
                for c in range(DC):
                    mm = nc.tensor.transpose(F[t % 2][:, c * P:(c + 1) * P], XN[:, t, c * P:(c + 1) * P], ident[:, :])
                mm.then_inc(front_done, 1)

            def similarities(m, t):
                k = 2 * TT * m + TT + t
                pe.wait_ge(front_free, 2 * TT * m + t + 3)
                pe.wait_ge(front_free, k + 1)
                for c in range(DC):
                    mm = nc.tensor.matmul(F[t % 2][:, :], XT[:, c, t * P:(t + 1) * P], MT[:, c, :],
                                          start=(c == 0), stop=(c == DC - 1))
                mm.then_inc(front_done, 1)

            def dense(m):
                pe.wait_ge(front_free, 2 * TT * m + TT + 2)
                for e in range(NB):
                    if e < 2:
                        pe.wait_ge(dg_free, (NB + FB) * m + e + 1)
                    elif e < 4:
                        pe.wait_ge(out_free, TT * m + e - 1)
                    else:
                        pe.wait_ge(dg_free, (NB + FB) * m + e - 1)
                    for c in range(DC):
                        mm = nc.tensor.matmul(R[e % 4][:, :], DT[:, c, e * P:(e + 1) * P], XT[:, c, :],
                                              start=(c == 0), stop=(c == DC - 1))
                    mm.then_inc(dg_done, 1)
                for f in range(FB):
                    pe.wait_ge(dg_free, (NB + FB) * m + NB + (f - 1 if f < 2 else f + 1))
                    for c in range(DC):
                        mm = nc.tensor.matmul(R[f % 2][:, :], wg[:, c, f * P:(f + 1) * P], XT[:, c, :],
                                              start=(c == 0), stop=(c == DC - 1))
                    mm.then_inc(dg_done, 1)
                    if f < 2:
                        pe.wait_ge(dg_free, (NB + FB) * m + NB + f + 1)
                    pe.wait_ge(h_done, FB * m + f + 1)
                    for c in range(DC):
                        mm = nc.tensor.matmul(UB[f % 2][:, :], wu[:, c, f * P:(f + 1) * P], XT[:, c, :],
                                              start=(c == 0), stop=(c == DC - 1))
                    mm.then_inc(u_done, 1)

            def turn_weights(m, t):
                pe.wait_ge(s_ready, TT * m + t + 1)
                pe.wait_ge(w_ready, TT * m + t + 1)
                for e in range(NB):
                    mm = nc.tensor.transpose(SP[:, e, :], S[:, t, e * P:(e + 1) * P], ident[:, :])
                mm.then_inc(st_done, 1)

            def mlp_out(m, t):
                if t == 0:
                    pe.wait_ge(h_done, FB * (m + 1) + 2)
                pe.wait_ge(out_free, TT * m + t + 1)
                for f in range(FB):
                    nc.tensor.matmul(OB[t % 2][:, 0:D], HT[:, f, t * P:(t + 1) * P], wd[:, f, :],
                                     start=(f == 0), stop=False)

            def experts_out(m, t):
                pe.wait_ge(w_ready, TT * m + t + 2)
                for e in range(NB):
                    mm = nc.tensor.matmul(OB[t % 2][:, 0:D], SD[:, e, t * P:(t + 1) * P], UP[:, e, :],
                                          start=False, stop=(e == NB - 1))
                mm.then_inc(out_done, 1)

            def outputs(m, following):
                front = {(turn_weights, 0): [(turn_xn, 0), (turn_xn, 1)], (mlp_out, 0): [(turn_xn, 2), (turn_xn, 3)],
                         (experts_out, 0): [(similarities, 0), (similarities, 1)],
                         (mlp_out, 1): [(similarities, 2), (similarities, 3)]}
                steps = [(turn_weights, 0)]
                for t in range(TT):
                    steps += [(mlp_out, t)] + ([(turn_weights, t + 1)] if t + 1 < TT else []) + [(experts_out, t)]
                for step, t in steps:
                    for part, tile in front.get((step, t), ()) if following is not None else ():
                        part(following, tile)
                    step(m, t)

            for t in range(TT):
                turn_xn(0, t)
            for t in range(TT):
                similarities(0, t)
            if NM > 1:
                with pe.Fori(0, NM - 1) as m:
                    dense(m)
                    outputs(m, m + 1)
            dense(NM - 1)
            outputs(NM - 1, None)

        @block.gpsimd
        def _(pool):
            pool.wait_ge(weights_in, ALL_IN)
            with pool.Fori(0, NM) as m:
                pool.wait_ge(xn_ready, TT * (m + 1))
                xs = X[:, bass.ds(TT * m, TT), :]
                nc.gpsimd.tensor_tensor(xs, xs, bdr[:, :].unsqueeze(1).to_broadcast([P, TT, D]), ALU.add).then_inc(biased, 1)
                for t in range(TT):
                    pool.wait_ge(front_free, 2 * TT * m + TT + t + 3)
                    for h in range(H):
                        pool.wait_ge(a_free, H * TT * m + H * t + h + 1)
                        nc.gpsimd.tensor_tensor(A[:, h, :].rearrange("p (i j) -> p i j", i=NR),
                                                SM[:, t, 0, h, 0:NR].unsqueeze(2).to_broadcast([P, NR, NK]),
                                                SM[:, t, 1, h, :].unsqueeze(1).to_broadcast([P, NR, NK]),
                                                ALU.add).then_inc(a_ready, 1)

        @block.scalar
        def _(act):
            act.wait_ge(weights_in, ALL_IN)
            act.sem_inc(front_free, 2)
            act.sem_inc(dg_free, 2)

            def front(m):
                for t in range(TT):
                    act.wait_ge(front_done, 2 * TT * m + t + 1)
                    nc.scalar.activation(XT[:, :, t * P:(t + 1) * P],
                                         F[t % 2][:, 0:D].rearrange("p (c t) -> p c t", c=DC), ACT.Copy)\
                      .then_inc(front_free, 1)
                for t in range(TT):
                    act.wait_ge(front_done, 2 * TT * m + TT + t + 1)
                    if not isinstance(m, int):
                        act.wait_ge(a_ready, H * TT * (m - 1) + H * (t + 1))
                    nc.scalar.activation(SM[:, t, :, :, :], F[t % 2][:, :], ACT.Copy).then_inc(front_free, 1)

            def silu_block(m, n):
                act.wait_ge(dg_done, (NB + FB) * m + n + 1)
                if n < NB:
                    nc.scalar.activation(SD[:, n, :], R[n % 4][:, :], ACT.Silu).then_inc(dg_free, 1)
                else:
                    f = n - NB
                    act.wait_ge(h_done, FB * m + f + 1)
                    nc.scalar.activation(GS[:, f % 2, :], R[f % 2][:, :], ACT.Silu, bias=bgc[:, f:f + 1])\
                       .then_inc(dg_free, 1)

            def exps(m, t, heads):
                if heads[0] == 0:
                    act.wait_ge(t8_ready, TT * m + t + 1)
                    nc.scalar.activation(E8[:, :, :], TD[:, :, :], ACT.Exp).then_inc(e8_ready, 1)
                for h in heads:
                    k = H * (TT * m + t) + h
                    act.wait_ge(a_ready, k + 1)
                    act.wait_ge(e_free, k + 1)
                    nc.scalar.activation(E[:, h % 2, :], A[:, h, :], ACT.Exp, bias=NMX[:, t % 2, h:h + 1])\
                       .then_inc(e_ready, 1)

            def first_half(m):
                for n in range(NB + FB):
                    silu_block(m, n)
                    if n in EXPS_AT:
                        exps(m, *EXPS_AT[n])

            def second_half(m):
                front(m)
                for t in range(2):
                    exps(m, t, range(H))

            second_half(0)
            if NM > 1:
                with act.Fori(0, NM - 1) as m:
                    first_half(m)
                    second_half(m + 1)
            first_half(NM - 1)

        @block.vector
        def _(dve):
            dve.wait_ge(weights_in, ALL_IN)
            dve.sem_inc(h_done, 2)
            dve.sem_inc(a_free, H)
            dve.sem_inc(e_free, 2)
            dve.sem_inc(w_ready, 1)
            dve.sem_inc(out_free, 2)

            def norm(m):
                for t in range(TT):
                    nc.vector.tensor_scalar(XN[:, t, :], X[:, TT * m + t, :], MEAN[:, bass.ds(TT * m + t, 1)],
                                            RS[:, bass.ds(TT * m + t, 1)], ALU.subtract, ALU.mult)\
                      .then_inc(xn_ready, 1)

            def tops(m, t):
                dve.wait_ge(front_free, 2 * TT * m + TT + t + 3)
                dve.sem_inc(tiles_begun, 1)
                for s in range(2):
                    for h in range(H):
                        nc.vector.max(TOP[:, s, h, :], SM[:, t, s, h, :])
                dve.drain()
                nc.vector.tensor_tensor(C[:, :, :, :], TOP[:, 0, :, :].unsqueeze(3).to_broadcast([P, H, TOPK, TOPK]),
                                        TOP[:, 1, :, :].unsqueeze(2).to_broadcast([P, H, TOPK, TOPK]), ALU.add)
                dve.drain()
                top = T8[:, t % 2, :, :]
                for h in range(H):
                    nc.vector.max(top[:, h, :], C[:, h, :, :].rearrange("p a b -> p (a b)"))
                dve.drain()
                nc.vector.tensor_scalar(NMX[:, t % 2, :], top[:, :, 0], -1.0, None, ALU.mult)
                nc.vector.tensor_tensor(TD[:, :, :], top, top[:, :, 0:1].to_broadcast([P, H, TOPK]), ALU.subtract)
                dve.drain()
                dve.sem_inc(t8_ready, 1)

            def top_sum(m, t):
                dve.wait_ge(e8_ready, TT * m + t + 1)
                nc.vector.tensor_reduce(RZ[:, :], E8[:, :, :], AX.X, ALU.add)
                dve.drain()
                nc.vector.reciprocal(RZ[:, :], RZ[:, :])
                dve.drain()

            def choose(m, t, h):
                top = T8[:, t % 2, :, :]
                dve.wait_ge(e_ready, H * (TT * m + t) + h + 1)
                nc.vector.scalar_tensor_tensor(out=E[:, h % 2, :], in0=A[:, h, :], scalar=top[:, h, TOPK - 1:TOPK],
                                               in1=E[:, h % 2, :], op0=ALU.is_ge, op1=ALU.mult).then_inc(a_free, 1)
                dve.drain()
                if h == 0:
                    nc.vector.tensor_scalar(S[:, t, :], E[:, 0, :], RZ[:, 0:1], None, ALU.mult).then_inc(e_free, 1)
                else:
                    nc.vector.scalar_tensor_tensor(out=S[:, t, :], in0=E[:, h % 2, :], scalar=RZ[:, h:h + 1],
                                                   in1=S[:, t, :], op0=ALU.mult, op1=ALU.add,
                                                   accum_out=SUM[:, :] if h == H - 1 else None)\
                      .then_inc(e_free, 1)
                if h < H - 1:
                    return
                dve.drain()
                nc.vector.tensor_scalar(SUM[:, :], SUM[:, :], -1.0, float(H), ALU.mult, ALU.add)
                dve.drain()
                nc.vector.tensor_tensor(S[:, t, NE - 1:NE], S[:, t, NE - 1:NE], SUM[:, :], ALU.add).then_inc(s_ready, 1)

            def hidden(m, f):
                dve.wait_ge(u_done, FB * m + f + 1)
                dve.wait_ge(dg_free, (NB + FB) * m + NB + f + 3)
                nc.vector.scalar_tensor_tensor(out=HT[:, f, :], in0=UB[f % 2][:, :], scalar=buc[:, f:f + 1],
                                               in1=GS[:, f % 2, :], op0=ALU.add, op1=ALU.mult).then_inc(h_done, 1)

            def weigh(m, t):
                tok = slice(t * P, (t + 1) * P)
                dve.wait_ge(st_done, TT * m + t + 1)
                nc.vector.tensor_tensor(SD[:, :, tok], SP[:, :, :], SD[:, :, tok], ALU.mult).then_inc(w_ready, 1)

            def add(m, t):
                if t == 0:
                    dve.wait_ge(biased, m + 1)
                dve.wait_ge(out_done, TT * m + t + 1)
                nc.vector.tensor_tensor(X[:, TT * m + t, :], X[:, TT * m + t, :], OB[t % 2][:, 0:D], ALU.add)\
                  .then_inc(out_free, 1)

            def first_half(m, last):
                if not last:
                    norm(m + 1)
                tops(m, 2)
                top_sum(m, 2)
                choose(m, 2, 0)
                choose(m, 2, 1)
                tops(m, 3)
                for f in range(0, FB, 2):
                    hidden(m, f)
                    hidden(m, f + 1)
                    if f == 2:
                        top_sum(m, 3)
                    if f < FB - 2:
                        for h in ((2, 3), (0, 1), (2, 3))[f // 2]:
                            choose(m, 2 if f == 0 else 3, h)

            def second_half(m, following):
                route = [[] for _ in range(2 * TT)]
                if following is not None:
                    route = [[(tops, 0), (top_sum, 0)], [(choose, 0, 0)], [(choose, 0, 1)], [(choose, 0, 2), (choose, 0, 3)],
                             [(tops, 1), (top_sum, 1)], [(choose, 1, 0)], [(choose, 1, 1)], [(choose, 1, 2), (choose, 1, 3)]]
                steps = [(weigh, 0), (weigh, 1), (add, 0), (weigh, 2), (add, 1), (weigh, 3), (add, 2), (add, 3)]
                for (step, t), parts in zip(steps, route):
                    step(m, t)
                    for part, *which in parts:
                        part(following, *which)
                dve.drain()
                for t in range(TT):
                    tile_stats(nc, X, STATS, TT * m + t)

            norm(0)
            for t in range(2):
                tops(0, t)
                top_sum(0, t)
                for h in range(H):
                    choose(0, t, h)
            if NM > 1:
                with dve.Fori(0, NM - 1) as m:
                    first_half(m, False)
                    second_half(m, m + 1)
            first_half(NM - 1, True)
            second_half(NM - 1, None)


def rotation_tables(T, hd):
    inv_freq = (1.0 / np.float32(10000.0) ** (np.arange(0, hd, 2, dtype=np.float32) / np.float32(hd))).astype(np.float32)
    ang = np.maximum(np.arange(T, dtype=np.float32) - 1, 0)[None, :] * inv_freq[:, None]
    cos, sin = np.cos(ang), np.sin(ang)
    return (np.concatenate([cos, cos]).astype(np.float32), np.concatenate([-sin, sin]).astype(np.float32))


def rotary_attention(nc, X, STATS, MEAN, RS, B, Wq, Wk, Wv, Wo, cos_d, sin_d, ident):
    HD = Wq.shape[0]
    SCALE = 1.0 / float(np.sqrt(HD))
    UNITS = [("x", t) for t in range(KT)] + [("v", 0), ("r", 0, 0, 0), ("v", 1)] + \
            [("r", side, q, swapped) for side in range(2) for q in range(2) for swapped in range(2)][1:]
    UPB = len(UNITS)
    UNITS_AT = [range(0, 4), range(4, 8), range(8, 9), range(9, 11), range(11, 13), range(13, 14),
                range(14, 16), range(16, 17), range(17, 18), range(0), range(0)]
    with ExitStack() as ctx:
        def sb(name, shape, dt=F32):
            return ctx.enter_context(nc.sbuf_tensor(name, shape, dt))

        def sem(name):
            return ctx.enter_context(nc.semaphore(name))

        RAW = sb("w_raw", [P, 4, D])
        WT = sb("w_turned", [P, 5, DC, HD])
        WOT = sb("woT", [HD, D])
        COS = sb("cos_sb", [HD, T])
        SIN = sb("sin_sb", [HD, T])
        XN = sb("xn1", [P, KT, D])
        XT = sb("xnT1", [P, DC, T])
        QR = sb("q_turned", [HD, 2, T])
        KR = sb("k_turned", [HD, 2, T])
        RC = sb("rot_cos_part", [HD, BANK])
        RSN = sb("rot_sin_part", [HD, BANK])
        V = sb("values1", [P, 2, KT, HD])
        PQ = sb("probs", [P, 2, T])
        PT = sb("probsT1", [P, 2, KT, P])
        OT = sb("outT1", [HD, 2, P])
        MX = sb("row_max1", [P, 2, 2])
        NB = sb("neg_max1", [P, 2])
        ZS = sb("row_sum", [P, 4])
        RZ = sb("recip_sum1", [P, 4])
        F = [ctx.enter_context(nc.psum_tensor(f"front1_{i}", [P, BANK], F32)) for i in range(2)]
        SC = ctx.enter_context(nc.psum_tensor("scores1", [P, T], F32))
        TP = ctx.enter_context(nc.psum_tensor("turned1", [P, KT, P], F32))
        OP = ctx.enter_context(nc.psum_tensor("pv1", [P, BANK], F32))
        YP = ctx.enter_context(nc.psum_tensor("proj1", [P, BANK], F32))

        weights_in = sem("weights1_in")
        front_done = sem("front1_done")
        front_free = sem("front1_free")
        xn_ready = sem("xn1_ready")
        scores_done = sem("scores1_done")
        max_ready = sem("max1_ready")
        exp_done = sem("exp1_done")
        turned_done = sem("turned1_done")
        turned_act = sem("turned1_act")
        turned_dve = sem("turned1_dve")
        pv_done = sem("pv1_done")
        ot_ready = sem("ot1_ready")
        out_done = sem("out1_done")
        x_added = sem("x1_added")

        def loads(sp):
            for i, w in enumerate((Wq, Wk, Wv)):
                sp.dma_start(RAW[0:HD, i, :], w).then_inc(weights_in, 16)
            sp.dma_start(RAW[:, 3, :].rearrange("p (a h) -> p a h", a=2), Wo.rearrange("(a p) h -> p a h", p=P))\
              .then_inc(weights_in, 16)
            sp.dma_start(COS[:, :], cos_d).then_inc(weights_in, 16)
            sp.dma_start(SIN[:, :], sin_d).then_inc(weights_in, 16)

        ln_scales(nc, STATS, MEAN, RS, "a1", loads)
        block = ctx.enter_context(nc.Block())

        @block.tensor
        def _(pe):
            pe.sem_inc(turned_done, 2)
            pe.sem_inc(pv_done, 2)
            pe.sem_inc(out_done, 2)
            pe.wait_ge(weights_in, 16 * 6)
            for i in range(4):
                pe.wait_ge(front_free, i + 1)
                for c in range(DC):
                    mm = nc.tensor.transpose(F[i % 2][:, c * P:(c + 1) * P], RAW[:, i, c * P:(c + 1) * P], ident[:, :])
                mm.then_inc(front_done, 1)
            pe.wait_ge(front_free, 4 + 2)

            def fill(b, u):
                k = 4 + UPB * b + u
                kind = UNITS[u][0]
                bank = F[u % 2]
                if kind == "x":
                    pe.wait_ge(xn_ready, KT * b + UNITS[u][1] + 1)
                if u == KT:
                    pe.wait_ge(front_free, k + 2)
                pe.wait_ge(front_free, k + 1)
                if kind == "x":
                    t = UNITS[u][1]
                    for c in range(DC):
                        mm = nc.tensor.transpose(bank[:, c * P:(c + 1) * P], XN[:, t, c * P:(c + 1) * P], ident[:, :])
                elif kind == "v":
                    i = UNITS[u][1]
                    for t in range(4):
                        for c in range(DC):
                            mm = nc.tensor.matmul(bank[:, t * P:(t + 1) * P],
                                                  XT[:, c, (4 * i + t) * P:(4 * i + t + 1) * P], WT[:, 4, c, :],
                                                  start=(c == 0), stop=(c == DC - 1))
                else:
                    _, side, q, swapped = UNITS[u]
                    for c in range(DC):
                        mm = nc.tensor.matmul(bank[:, :], WT[:, 2 * side + swapped, c, :],
                                              XT[:, c, q * BANK:(q + 1) * BANK], start=(c == 0), stop=(c == DC - 1))
                mm.then_inc(front_done, 1)

            def tiles(b, par, last):
                pe.wait_ge(front_free, 4 + UPB * (b + 1) + 2)
                for t in range(KT + 2):
                    n = KT * b + t
                    if t < KT:
                        pe.wait_ge(exp_done, n + 1)
                        for q in range(2):
                            nc.tensor.matmul(SC[:, q * BANK:(q + 1) * BANK], QR[:, par, t * P:(t + 1) * P],
                                             KR[:, par, q * BANK:(q + 1) * BANK], start=True, stop=True)\
                              .then_inc(scores_done, 1)
                    if 1 <= t <= KT:
                        pe.wait_ge(exp_done, n + 1)
                        pe.wait_ge(turned_act, n)
                        pe.wait_ge(turned_dve, n)
                        for k in range(KT):
                            mm = nc.tensor.transpose(TP[:, k, :], PQ[:, (t - 1) % 2, k * P:(k + 1) * P], ident[:, :])
                        mm.then_inc(turned_done, 1)
                    if t >= 2:
                        pe.wait_ge(ot_ready, n)
                        pe.wait_ge(x_added, n - 1)
                        nc.tensor.matmul(YP[:, 0:D], OT[:, t % 2, :], WOT[:, :], start=True, stop=True)\
                          .then_inc(out_done, 1)
                    if 1 <= t <= KT:
                        pe.wait_ge(turned_act, n + 1)
                        pe.wait_ge(turned_dve, n + 1)
                        pe.wait_ge(ot_ready, n)
                        for k in range(KT):
                            mm = nc.tensor.matmul(OP[:, 0:P], V[:, par, k, :], PT[:, (t - 1) % 2, k, :],
                                                  start=(k == 0), stop=(k == KT - 1))
                        mm.then_inc(pv_done, 1)
                    if not last:
                        for u in UNITS_AT[t]:
                            fill(b + 1, u)

            for u in range(UPB):
                fill(0, u)
            if B > 2:
                with pe.Fori(0, B // 2 - 1) as i:
                    tiles(2 * i, 0, False)
                    tiles(2 * i + 1, 1, False)
            tiles(B - 2, 0, False)
            tiles(B - 1, 1, True)

        @block.scalar
        def _(act):
            act.sem_inc(exp_done, 1)
            act.sem_inc(turned_act, 1)
            act.sem_inc(ot_ready, 1)
            with act.Fori(0, B) as b:
                for t in range(KT + 1):
                    n = KT * b + t
                    if t >= 1:
                        act.wait_ge(turned_done, n + 2)
                        act.wait_ge(pv_done, n)
                        nc.scalar.activation(PT[:, (t - 1) % 2, 0:KT // 2, :], TP[:, 0:KT // 2, :], ACT.Copy)\
                           .then_inc(turned_act, 1)
                    if t < KT:
                        act.wait_ge(max_ready, n + 1)
                        act.wait_ge(turned_done, n + 1)
                        nc.scalar.activation(PQ[:, t % 2, :], SC[:, :], ACT.Exp, bias=NB[:, t % 2:t % 2 + 1],
                                             scale=SCALE, accum_out=ZS[:, t % 4:t % 4 + 1]).then_inc(exp_done, 1)
                    if t >= 1:
                        act.wait_ge(pv_done, n + 2)
                        act.wait_ge(out_done, n)
                        nc.scalar.activation(OT[:, (t - 1) % 2, :], OP[:, 0:P], ACT.Copy).then_inc(ot_ready, 1)

        @block.vector
        def _(dve):
            dve.sem_inc(front_free, 2)
            dve.sem_inc(turned_dve, 1)
            dve.sem_inc(x_added, 1)
            dve.wait_ge(weights_in, 16 * 6)
            half = HD // 2
            for i in range(4):
                dve.wait_ge(front_done, i + 1)
                if i < 2:
                    src = F[i % 2][:, 0:D].rearrange("p (c h two) -> p c h two", c=DC, two=2)
                    nc.vector.tensor_copy(WT[:, 2 * i, :, 0:half], src[:, :, :, 0])
                    nc.vector.tensor_copy(WT[:, 2 * i, :, half:HD], src[:, :, :, 1])
                    nc.vector.tensor_copy(WT[:, 2 * i + 1, :, 0:half], src[:, :, :, 1])
                    nc.vector.tensor_copy(WT[:, 2 * i + 1, :, half:HD], src[:, :, :, 0]).then_inc(front_free, 1)
                else:
                    dst = WT[:, 4, :, :] if i == 2 else WOT[:, :].rearrange("p (c h) -> p c h", c=2)
                    nc.vector.tensor_copy(dst, F[i % 2][:, 0:D].rearrange("p (c h) -> p c h", c=DC)).then_inc(front_free, 1)

            def norm(b, t):
                nc.vector.tensor_scalar(XN[:, t, :], X[:, KT * b + t, :], MEAN[:, bass.ds(KT * b + t, 1)],
                                        RS[:, bass.ds(KT * b + t, 1)], ALU.subtract, ALU.mult).then_inc(xn_ready, 1)

            def empty(b, par, u):
                dve.wait_ge(front_done, 4 + UPB * b + u + 1)
                kind = UNITS[u][0]
                bank = F[u % 2]
                if kind == "x":
                    t = UNITS[u][1]
                    nc.vector.tensor_copy(XT[:, :, t * P:(t + 1) * P],
                                          bank[:, 0:D].rearrange("p (c t) -> p c t", c=DC)).then_inc(front_free, 1)
                elif kind == "v":
                    i = UNITS[u][1]
                    nc.vector.tensor_copy(V[:, par, 4 * i:4 * i + 4, :], bank[:, :].rearrange("p (t h) -> p t h", t=4))\
                      .then_inc(front_free, 1)
                else:
                    _, side, q, swapped = UNITS[u]
                    tok = slice(q * BANK, (q + 1) * BANK)
                    if not swapped:
                        nc.vector.tensor_tensor(RC[:, :], bank[:, :], COS[:, tok], ALU.mult).then_inc(front_free, 1)
                    else:
                        nc.vector.tensor_tensor(RSN[:, :], bank[:, :], SIN[:, tok], ALU.mult)
                        dve.drain()
                        nc.vector.tensor_tensor((QR, KR)[side][:, par, tok], RC[:, :], RSN[:, :], ALU.add)\
                          .then_inc(front_free, 1)
                        dve.drain()

            def tiles(b, par, last):
                for t in range(KT + 2):
                    n = KT * b + t
                    if not last:
                        for u in UNITS_AT[t]:
                            if u < KT:
                                norm(b + 1, u)
                    if t < KT:
                        for q in range(2):
                            dve.wait_ge(scores_done, 2 * n + q + 1)
                            nc.vector.tensor_reduce(MX[:, t % 2, q:q + 1], SC[:, q * BANK:(q + 1) * BANK], AX.X, ALU.max)
                        dve.drain()
                        nc.vector.tensor_scalar(NB[:, t % 2:t % 2 + 1], MX[:, t % 2, 0:1], MX[:, t % 2, 1:2], -SCALE,
                                                ALU.max, ALU.mult).then_inc(max_ready, 1)
                    if 1 <= t <= KT:
                        dve.wait_ge(turned_done, n + 2)
                        dve.wait_ge(pv_done, n)
                        nc.vector.tensor_copy(PT[:, (t - 1) % 2, KT // 2:KT, :], TP[:, KT // 2:KT, :])\
                          .then_inc(turned_dve, 1)
                    if t >= 2:
                        z = slice((t - 2) % 4, (t - 2) % 4 + 1)
                        dve.wait_ge(out_done, n + 1)
                        dve.wait_ge(exp_done, n)
                        nc.vector.reciprocal(RZ[:, z], ZS[:, z])
                        dve.drain()
                        nc.vector.scalar_tensor_tensor(out=X[:, KT * b + (t - 2), :], in0=YP[:, 0:D], scalar=RZ[:, z],
                                                       in1=X[:, KT * b + (t - 2), :], op0=ALU.mult, op1=ALU.add)\
                          .then_inc(x_added, 1)
                        dve.drain()
                        tile_stats(nc, X, STATS, KT * b + (t - 2))
                    if not last:
                        for u in UNITS_AT[t]:
                            empty(b + 1, 1 - par, u)

            for t in range(KT):
                norm(0, t)
            for u in range(UPB):
                empty(0, 0, u)
            if B > 2:
                with dve.Fori(0, B // 2 - 1) as i:
                    tiles(2 * i, 0, False)
                    tiles(2 * i + 1, 1, False)
            tiles(B - 2, 0, False)
            tiles(B - 1, 1, True)


def mixture_ffn(nc, X, STATS, MEAN, RS, B, Wm, bm, emb, W1, b1, W2, b2, Wo, bo, out, ident):
    HD, E = emb.shape
    I = W1.shape[2]
    G = P // HD
    HC = D // P
    H = G * HC
    TT = 4
    TM = TT * P
    NM = B * KT // TT
    NU = HC * E
    with ExitStack() as ctx:
        def sb(name, shape, dt=F32):
            return ctx.enter_context(nc.sbuf_tensor(name, shape, dt))

        def sem(name):
            return ctx.enter_context(nc.semaphore(name))

        wm = sb("wm_sb", [P, DC, D])
        wo = sb("wo_sb", [P, HC, D])
        w1 = sb("w1_sb", [P, E, I])
        w1s = sb("w1_stack", [P, 2, E, I], BF16)
        wpart = sb("w1_part", [P, 2, E, I], BF16)
        w2 = sb("w2_sb", [I, E, HD])
        embd = sb("emb_diag", [P, G, E])
        bmc = sb("bm_col", [P, HC])
        b1c = sb("b1_col", [I, E])
        b2c = sb("b2_col", [P, E])
        bor = sb("bo_rows", [P, D])
        SEL = sb("gate_spread", [3 * HD, E // 2, G, HD], BF16)
        XN = sb("xn2", [P, TT, D])
        XT = sb("xnT2", [P, DC, TM])
        HX = sb("slices", [P, HC, TM])
        REM = sb("split_rest2", [P, TM])
        PCH = sb("slice_parts", [P, HC, 3, TM], BF16)
        PCG = sb("gate_parts", [P, 3, TM], BF16)
        HS = sb("slice_stack", [P, 2, H, TM], BF16)
        GT = sb("gate_stack", [3 * HD, 2, 2 * HC, TM], BF16)
        EXP = sb("gates", [P, TT, P])
        LS = sb("logits", [P, TT, H, E])
        LM = sb("logits_less_max", [P, TT, H, E])
        EX = sb("gate_exp", [P, TT, H, E])
        MK = sb("gate_mask", [P, TT, H, E])
        M8 = sb("top_logits", [P, TT, H, 8])
        RZ = sb("gate_recip", [P, TT, H])
        GH = sb("gelu_out", [I, 4, 2, TM])
        GS = sb("gates_spread", [P, 2, TM])
        Y = sb("gated", [P, 2, TM])
        CM = sb("combined", [P, 2, HC, TM])
        HP = [ctx.enter_context(nc.psum_tensor(f"hidden{i}", [P, 2, TM], F32)) for i in range(2)]
        OP = [ctx.enter_context(nc.psum_tensor(f"expert_out{i}", [P, TM], F32)) for i in range(2)]
        GP = ctx.enter_context(nc.psum_tensor("gate_bank", [P, TM], F32))
        MB = ctx.enter_context(nc.psum_tensor("misc_bank", [P, TM], F32))

        slice_d = nc.dram_tensor("slice_scratch", [2, 3, D, TM], BF16).ap()
        gate_d = nc.dram_tensor("gate_scratch", [2, 3, P, TM], BF16).ap()

        stored = sem("x_stored")
        slices_ready = sem("slices_ready")
        slices_stored = [sem(f"slices_stored{c}") for c in range(HC)]
        slices_in = sem("slices_in")
        gparts_ready = sem("gparts_ready")
        gates_stored = sem("gates_stored")
        gates_in = sem("gates_in")
        wpart_ready = sem("wpart_ready")
        w1_ready = sem("w1_ready")
        weights_in = sem("weights2_in")
        zeroed = sem("zeroed2")
        consts_ready = sem("consts2_ready")
        xn_ready = sem("xn2_ready")
        biased = sem("biased2")
        misc_done = sem("misc_done")
        misc_free = sem("misc_free")
        lm_ready = sem("lm_ready")
        ex_ready = sem("ex_ready")
        gates_ready = sem("gates_ready")
        a_done = sem("a_done")
        gelu_done = sem("gelu_done")
        o_done = sem("o_done")
        g_done = sem("g_done")
        gs_ready = sem("gs_ready")
        y_ready = sem("y_ready")
        y_added = sem("y_added")

        moves = [(wm[:, :, :], Wm.rearrange("(c p) n -> p c n", p=P)),
                 (wo[:, :, :], Wo.rearrange("(c p) n -> p c n", p=P)),
                 (w2[:, :, :], W2.rearrange("e i o -> i e o")),
                 (bmc[:, :], bm.rearrange("(c p) -> p c", p=P)),
                 (b1c[:, :], b1.rearrange("e i -> i e")),
                 (bor[:, :], bo.rearrange("(a d) -> a d", a=1).to_broadcast([P, D]))]
        for j in range(G):
            row = slice(HD * j, HD * (j + 1))
            moves += [(w1[row, :, :], W1.rearrange("e d i -> d e i")), (b2c[row, :], b2.rearrange("e o -> o e")),
                      (embd[row, j, :], emb)]
        ALL_IN = 16 * len(moves)

        def loads(sp):
            sp.wait_ge(zeroed, 1)
            for dst, src in moves:
                sp.dma_start(dst, src, allow_slow_non_contiguous=True).then_inc(weights_in, 16)

        def consts(pool):
            nc.gpsimd.memset(embd[:, :, :], 0.0).then_inc(zeroed, 1)
            pool.wait_ge(zeroed, 1)
            nc.gpsimd.memset(SEL[:, :, :, :], 0.0).then_inc(consts_ready, 1)
            pool.wait_ge(consts_ready, 1)
            for s in range(3):
                nc.gpsimd.affine_select(out=SEL[:, :, :, :], in_=SEL[:, :, :, :], compare_op=ALU.not_equal, fill=1.0,
                                        base=-HD * s, pattern=[[-1, E // 2], [-(E // 2), G], [0, HD]],
                                        channel_multiplier=1).then_inc(consts_ready, 1)
                pool.wait_ge(consts_ready, s + 2)

        ln_scales(nc, STATS, MEAN, RS, "f1", loads, consts)
        block = ctx.enter_context(nc.Block())

        FRONT = [("x", 0), ("x", 1), ("x", 2), ("x", 3), ("h", 0), ("h", 1), ("l", 0), ("w", 0), ("g", 0)]
        OUTPUT_AT = dict(zip(range(2, 2 + TT), range(TT)))
        FRONT_AT = dict(zip((6, 7, 8, 9, 11, 13, 16, 20, 24), FRONT))
        EXP_AT = 18
        FPB = TT + HC + 2

        def before(m):
            return FPB if isinstance(m, int) and m == 0 else (FPB + TT) * m + FPB - TT

        @block.sync
        def _(sp):
            def front_io(m, par):
                for c in range(HC):
                    sp.wait_ge(slices_ready, HC * m + c + 1)
                    sp.dma_start(slice_d[par, :, c * P:(c + 1) * P, :].rearrange("s r t -> r s t"), PCH[:, c, :, :])\
                      .then_inc(slices_stored[c], 16)
                for c in range(HC):
                    sp.wait_ge(slices_stored[c], 16 * (m + 1))
                for s, part in enumerate((0, 1, 2, 0)):
                    sp.dma_start(HS[HD * s:HD * (s + 1), par, :, :],
                                 slice_d[par, part].rearrange("(h d) t -> d h t", d=HD)).then_inc(slices_in, 16)
                sp.wait_ge(gparts_ready, m + 1)
                sp.dma_start(gate_d[par].rearrange("s r t -> r s t"), PCG[:, :, :]).then_inc(gates_stored, 16)
                sp.wait_ge(gates_stored, 16 * (m + 1))
                for s in range(3):
                    sp.dma_start(GT[HD * s:HD * (s + 1), par, :, :],
                                 gate_d[par, s].rearrange("(g r) t -> r g t", r=HD)).then_inc(gates_in, 16)

            with sp.Fori(0, NM // 2) as i:
                front_io(2 * i, 0)
                front_io(2 * i + 1, 1)
            for b in range(B):
                sp.wait_ge(misc_free, (before(2 * b + 2) if b < B - 1 else before(NM - 1) + TT) + TT + 1)
                sp.dma_start(out[b].rearrange("(t p) d -> p t d", p=P), X[:, KT * b:KT * (b + 1), :])\
                  .then_inc(stored, 16)
            sp.wait_ge(stored, 16 * B)

        @block.tensor
        def _(pe):
            pe.sem_inc(o_done, 2)
            pe.wait_ge(weights_in, ALL_IN)
            pe.wait_ge(consts_ready, 4)

            def turn_x(m, t, k):
                pe.wait_ge(xn_ready, TT * m + t + 1)
                pe.wait_ge(misc_free, k + 1)
                for c in range(DC):
                    mm = nc.tensor.transpose(MB[:, c * P:(c + 1) * P], XN[:, t, c * P:(c + 1) * P], ident[:, :])
                mm.then_inc(misc_done, 1)

            def project(m, h, k):
                pe.wait_ge(misc_free, k + 1)
                for c in range(DC):
                    mm = nc.tensor.matmul(MB[:, :], wm[:, c, h * P:(h + 1) * P], XT[:, c, :],
                                          start=(c == 0), stop=(c == DC - 1))
                mm.then_inc(misc_done, 1)

            def logits(m, _, k):
                pe.wait_ge(misc_free, k + 1)
                for t in range(TT):
                    for h in range(HC):
                        mm = nc.tensor.matmul(MB[:, t * P + h * G * E:t * P + (h + 1) * G * E],
                                              HX[:, h, t * P:(t + 1) * P], embd[:, :, :], start=True, stop=True)
                mm.then_inc(misc_done, 1)

            def turn_gates(m, _, k):
                pe.wait_ge(gates_ready, m + 1)
                pe.wait_ge(misc_free, k + 1)
                for t in range(TT):
                    mm = nc.tensor.transpose(MB[:, t * P:(t + 1) * P], EXP[:, t, :], ident[:, :])
                mm.then_inc(misc_done, 1)

            def output(m, par, t, k):
                if t == 0:
                    pe.wait_ge(y_added, NU * m + NU + 3)
                pe.wait_ge(misc_free, k + 1)
                for h in range(HC):
                    mm = nc.tensor.matmul(MB[:, 0:D], CM[:, par, h, t * P:(t + 1) * P], wo[:, h, :],
                                          start=(h == 0), stop=(h == HC - 1))
                mm.then_inc(misc_done, 1)

            def hidden(m, par, u):
                hc, e = divmod(u, E)
                for p in range(2):
                    pe.wait_ge(gelu_done, 2 * (NU * m + u) + p + 1)
                    for j in range(2):
                        h = G * hc + 2 * p + j
                        nc.tensor.matmul(HP[p][:, j, :], w1s[:, 0, e, :], HS[:, par, h, :], start=True, stop=False)
                        mm = nc.tensor.matmul(HP[p][:, j, :], w1s[0:3 * HD, 1, e, :], HS[0:3 * HD, par, h, :],
                                              start=False, stop=True)
                    mm.then_inc(a_done, 1)

            def expert_out(m, par, u):
                hc, e = divmod(u, E)
                n = NU * m + u
                pe.wait_ge(gs_ready, n + 1)
                nc.tensor.matmul(GP[:, :], SEL[:, e % (E // 2), :, :], GT[:, par, 2 * hc + e // (E // 2), :],
                                 start=True, stop=True).then_inc(g_done, 1)
                pe.wait_ge(gelu_done, 2 * n + 4)
                pe.wait_ge(y_ready, n + 1)
                for j in range(G):
                    mm = nc.tensor.matmul(OP[u % 2][HD * j:HD * (j + 1), :], w2[:, e, :],
                                          GH[:, (2 * u + j // 2) % 4, j % 2, :], start=True, stop=True,
                                          tile_position=(0, HD * j))
                mm.then_inc(o_done, 1)

            front = {"x": turn_x, "h": project, "l": logits, "g": turn_gates}

            def one_block(m, par, first, last):
                k = before(m)
                pe.wait_ge(slices_in, 16 * 4 * (m + 1))
                pe.wait_ge(gates_in, 16 * 3 * (m + 1))
                for u in range(NU + 1):
                    if u < NU:
                        hidden(m, par, u)
                    if u >= 1:
                        expert_out(m, par, u - 1)
                    if u in OUTPUT_AT and not first:
                        output(m - 1, 1 - par, OUTPUT_AT[u], k)
                        k += 1
                    if u in FRONT_AT and FRONT_AT[u][0] != "w" and not last:
                        part, t = FRONT_AT[u]
                        front[part](m + 1, t, k)
                        k += 1
                return k

            k = 0
            for part, t in FRONT:
                if part != "w":
                    front[part](0, t, k)
                    k += 1
            pe.wait_ge(misc_free, FPB + 1)
            pe.wait_ge(w1_ready, 2)
            one_block(0, 0, True, False)
            if NM > 2:
                with pe.Fori(0, NM // 2 - 1) as i:
                    one_block(2 * i + 1, 1, False, False)
                    one_block(2 * i + 2, 0, False, False)
            k = one_block(NM - 1, 1, False, True)
            for t in range(TT):
                output(NM - 1, 1, t, k + t)

        @block.gpsimd
        def _(pool):
            pool.sem_inc(y_added, 3)

            pool.wait_ge(weights_in, ALL_IN)

            def sum_up(m, par):
                pool.wait_ge(xn_ready, TT * (m + 1))
                xs = X[:, bass.ds(TT * m, TT), :]
                nc.gpsimd.tensor_tensor(xs, xs, bor[:, :].unsqueeze(1).to_broadcast([P, TT, D]), ALU.add)\
                  .then_inc(biased, 1)
                for u in range(NU):
                    hc, e = divmod(u, E)
                    n = NU * m + u
                    pool.wait_ge(y_ready, n + 3)
                    pool.wait_ge(y_added, n + 3)
                    if e == 0:
                        pool.sem_inc(y_added, 1)
                    else:
                        nc.gpsimd.tensor_tensor(CM[:, par, hc, :], CM[:, par, hc, :], Y[:, u % 2, :], ALU.add)\
                          .then_inc(y_added, 1)

            with pool.Fori(0, NM // 2) as i:
                sum_up(2 * i, 0)
                sum_up(2 * i + 1, 1)

        @block.scalar
        def _(act):
            act.wait_ge(weights_in, ALL_IN)
            act.sem_inc(gelu_done, 2)

            def gate_exp(m):
                act.wait_ge(lm_ready, m + 1)
                nc.scalar.activation(EX[:, :, :, :], LM[:, :, :, :], ACT.Exp).then_inc(ex_ready, 1)

            def one_block(m, last):
                for u in range(NU):
                    for p in range(2):
                        k = 2 * u + p
                        act.wait_ge(a_done, 2 * NU * m + k + 1)
                        act.wait_ge(o_done, NU * m + u + 1)
                        nc.scalar.activation(GH[:, k % 4, :, :], HP[p][:, :, :], ACT.Gelu, bias=b1c[:, u % E:u % E + 1])\
                           .then_inc(gelu_done, 1)
                    if u == EXP_AT and not last:
                        gate_exp(m + 1)

            gate_exp(0)
            act.wait_ge(wpart_ready, 1)
            nc.scalar.activation(w1s[0:3 * HD, 0, :, :], wpart[0:3 * HD, 0, :, :], ACT.Copy)
            act.wait_ge(wpart_ready, 2)
            for row, i in ((3, 0), (1, 1), (2, 1)):
                rows = slice(HD * row, HD * (row + 1))
                place = nc.scalar.activation(w1s[rows, i, :, :], wpart[rows, 1, :, :], ACT.Copy)
            place.then_inc(w1_ready, 1)
            if NM > 1:
                with act.Fori(0, NM - 1) as m:
                    one_block(m, False)
            one_block(NM - 1, True)

        @block.vector
        def _(dve):
            dve.wait_ge(weights_in, ALL_IN)
            dve.sem_inc(misc_free, 1)
            dve.sem_inc(gs_ready, 1)
            dve.sem_inc(y_ready, 2)

            def norm(m):
                for t in range(TT):
                    nc.vector.tensor_scalar(XN[:, t, :], X[:, TT * m + t, :], MEAN[:, bass.ds(TT * m + t, 1)],
                                            RS[:, bass.ds(TT * m + t, 1)], ALU.subtract, ALU.mult).then_inc(xn_ready, 1)

            def turn_x(m, t, k):
                dve.wait_ge(misc_done, k + 1)
                nc.vector.tensor_copy(XT[:, :, t * P:(t + 1) * P], MB[:, 0:D].rearrange("p (c t) -> p c t", c=DC))\
                  .then_inc(misc_free, 1)

            def project(m, h, k):
                dve.wait_ge(misc_done, k + 1)
                nc.vector.tensor_scalar(HX[:, h, :], MB[:, :], bmc[:, h:h + 1], None, ALU.add)\
                  .then_inc(misc_free, 1)
                dve.drain()
                wait(dve, slices_stored[h], 16 * m)
                nc.vector.tensor_copy(PCH[:, h, 0, :], HX[:, h, :])
                dve.drain()
                nc.vector.tensor_tensor(REM[:, :], HX[:, h, :], PCH[:, h, 0, :], ALU.subtract)
                dve.drain()
                nc.vector.tensor_copy(PCH[:, h, 1, :], REM[:, :])
                dve.drain()
                nc.vector.tensor_tensor(PCH[:, h, 2, :], REM[:, :], PCH[:, h, 1, :], ALU.subtract)\
                  .then_inc(slices_ready, 1)
                dve.drain()

            def logits(m, _, k):
                dve.wait_ge(misc_done, k + 1)
                nc.vector.tensor_copy(LS[:, :, :, :], MB[:, :]).then_inc(misc_free, 1)
                dve.drain()
                for t in range(TT):
                    for h in range(H):
                        nc.vector.max(M8[:, t, h, :], LS[:, t, h, :])
                dve.drain()
                flat = lambda a: a.rearrange("p t h e -> p (t h) e")
                ls, m8 = flat(LS[:, :, :, :]), flat(M8[:, :, :, :])
                nc.vector.tensor_tensor(flat(LM[:, :, :, :]), ls, m8[:, :, 0:1].to_broadcast([P, TT * H, E]), ALU.subtract)\
                  .then_inc(lm_ready, 1)
                nc.vector.tensor_tensor(flat(MK[:, :, :, :]), ls, m8[:, :, 1:2].to_broadcast([P, TT * H, E]), ALU.is_ge)

            def weigh(m, _, k):
                flat = lambda a: a.rearrange("p t h e -> p (t h) e")
                dve.wait_ge(ex_ready, m + 1)
                nc.vector.tensor_reduce(RZ[:, :, :], EX[:, :, :, :], AX.X, ALU.add)
                dve.drain()
                nc.vector.reciprocal(RZ[:, :, :], RZ[:, :, :])
                nc.vector.tensor_tensor(EX[:, :, :, :], EX[:, :, :, :], MK[:, :, :, :], ALU.mult)
                dve.drain()
                for g in range(2):
                    src = EX[:, :, :, :].rearrange("p t (c j) (g e) -> p g (t c) j e", c=HC, g=2)
                    dst = EXP[:, :, :].rearrange("p t (c g j e) -> p g (t c) j e", c=HC, g=2, j=G)
                    rz = RZ[:, :, :].rearrange("p t (c j) -> p (t c) j", c=HC).unsqueeze(3)
                    mult = nc.vector.tensor_tensor(dst[:, g], src[:, g], rz.to_broadcast([P, TT * HC, G, E // 2]), ALU.mult)
                mult.then_inc(gates_ready, 1)

            def turn_gates(m, _, k):
                dve.wait_ge(misc_done, k + 1)
                wait(dve, gates_stored, 16 * m)
                nc.vector.tensor_copy(PCG[:, 0, :], MB[:, :])
                dve.drain()
                nc.vector.tensor_tensor(REM[:, :], MB[:, :], PCG[:, 0, :], ALU.subtract).then_inc(misc_free, 1)
                dve.drain()
                nc.vector.tensor_copy(PCG[:, 1, :], REM[:, :])
                dve.drain()
                nc.vector.tensor_tensor(PCG[:, 2, :], REM[:, :], PCG[:, 1, :], ALU.subtract).then_inc(gparts_ready, 1)

            def output(m, t, k):
                if t == 0:
                    dve.wait_ge(biased, m + 1)
                dve.wait_ge(misc_done, k + 1)
                nc.vector.tensor_tensor(X[:, TT * m + t, :], X[:, TT * m + t, :], MB[:, 0:D], ALU.add)\
                  .then_inc(misc_free, 1)

            def gate_unit(m, par, u):
                n = NU * m + u
                dve.wait_ge(g_done, n + 1)
                nc.vector.tensor_copy(GS[:, u % 2, :], GP[:, :]).then_inc(gs_ready, 1)
                dve.drain()
                dve.wait_ge(o_done, n + 3)
                dve.wait_ge(y_added, n + 2)
                hc, e = divmod(u, E)
                nc.vector.scalar_tensor_tensor(out=Y[:, u % 2, :] if e else CM[:, par, hc, :], in0=OP[u % 2][:, :],
                                               scalar=b2c[:, e:e + 1], in1=GS[:, u % 2, :], op0=ALU.add, op1=ALU.mult).then_inc(y_ready, 1)

            front = {"x": turn_x, "h": project, "l": logits, "w": weigh, "g": turn_gates}

            def one_block(m, par, first, last):
                k = before(m)
                for u in range(NU + 1):
                    if u >= 1:
                        gate_unit(m, par, u - 1)
                    if u == 1 and not last:
                        norm(m + 1)
                    if u in OUTPUT_AT and not first:
                        output(m - 1, OUTPUT_AT[u], k)
                        k += 1
                    if u in FRONT_AT and not last:
                        part, t = FRONT_AT[u]
                        front[part](m + 1, t, k)
                        k += part != "w"
                return k

            def split_w1():
                for part in range(2):
                    nc.vector.tensor_copy(wpart[:, part, :, :], w1[:, :, :])
                    dve.drain()
                    dve.sem_inc(wpart_ready, 1)
                    nc.vector.tensor_tensor(w1[:, :, :], w1[:, :, :], wpart[:, part, :, :], ALU.subtract)
                    dve.drain()
                nc.vector.tensor_copy(w1s[0:HD, 1, :, :], w1[0:HD, :, :]).then_inc(w1_ready, 1)

            norm(0)
            k = 0
            for part, t in FRONT:
                front[part](0, t, k)
                k += part != "w"
            split_w1()
            one_block(0, 0, True, False)
            if NM > 2:
                with dve.Fori(0, NM // 2 - 1) as i:
                    one_block(2 * i + 1, 1, False, False)
                    one_block(2 * i + 2, 0, False, False)
            k = one_block(NM - 1, 1, False, True)
            for t in range(TT):
                output(NM - 1, t, k + t)

def make_idents(nc, ident, identb):
    with ExitStack() as ctx:
        zeroed = ctx.enter_context(nc.semaphore("ident_zeroed"))
        made = ctx.enter_context(nc.semaphore("ident_made"))
        with nc.Block() as block:
            @block.gpsimd
            def _(pool):
                for m in (ident, identb):
                    nc.gpsimd.memset(m[:, :], 0.0).then_inc(zeroed, 1)
                pool.wait_ge(zeroed, 2)
                for m in (ident, identb):
                    nc.gpsimd.affine_select(out=m[:, :], in_=m[:, :], compare_op=ALU.not_equal, fill=1.0,
                                            base=0, pattern=[[-1, P]], channel_multiplier=1).then_inc(made, 1)
                pool.wait_ge(made, 2)


def program(nc, a, out):
    B = a["L0_attn_x"].shape[0]
    NT = B * KT
    with ExitStack() as ctx:
        X = ctx.enter_context(nc.sbuf_tensor("x_tiles", [P, NT, D], F32))
        MEAN = ctx.enter_context(nc.sbuf_tensor("ln_mean", [P, NT], F32))
        RS = ctx.enter_context(nc.sbuf_tensor("ln_rstd", [P, NT], F32))
        STATS = ctx.enter_context(nc.sbuf_tensor("ln_stats", [P, NT, 6], F32))
        ident = ctx.enter_context(nc.sbuf_tensor("ident", [P, P], F32))
        identb = ctx.enter_context(nc.sbuf_tensor("ident_bf16", [P, P], BF16))
        make_idents(nc, ident, identb)
        causal_attention(nc, a["L0_attn_x"], X, STATS, MEAN, RS, B, a["L0_attn_Wq"], a["L0_attn_Wk"],
                         a["L0_attn_Wv"], ident, identb)
        expert_ffn(nc, X, STATS, MEAN, RS, B, *(a["L0_ffn_" + n] for n in (
            "Wg", "bg", "Wu", "bu", "Wd", "bd", "Wq", "keys", "down_embed", "up_embed")), ident)
        rotary_attention(nc, X, STATS, MEAN, RS, B, *(a["L1_attn_" + n] for n in ("wq", "wk", "wv", "wo")),
                         a["rotation_cos"], a["rotation_sin"], ident)
        mixture_ffn(nc, X, STATS, MEAN, RS, B, *(a["L1_ffn_" + n] for n in (
            "Wm", "bm", "expert_emb", "W1", "b1", "W2", "b2", "Wo", "bo")), out, ident)


_INS = ["L0_attn_x", "L0_attn_Wq", "L0_attn_Wk", "L0_attn_Wv",
        "L0_ffn_Wg", "L0_ffn_bg", "L0_ffn_Wu", "L0_ffn_bu",
        "L0_ffn_Wd", "L0_ffn_bd", "L0_ffn_Wq", "L0_ffn_keys",
        "L0_ffn_down_embed", "L0_ffn_up_embed", "L1_attn_wq", "L1_attn_wk",
        "L1_attn_wv", "L1_attn_wo", "L1_ffn_Wm", "L1_ffn_bm",
        "L1_ffn_expert_emb", "L1_ffn_W1", "L1_ffn_b1", "L1_ffn_W2",
        "L1_ffn_b2", "L1_ffn_Wo", "L1_ffn_bo"]


def kernel(**inputs):
    import numpy as _np
    import concourse.bacc as _bacc
    from concourse import mybir as _mybir
    from concourse.bass_utils import run_bass_kernel_spmd as _run

    nc = _bacc.Bacc("TRN2", target_bir_lowering=False, num_devices=1)
    arrays, args = {}, {}
    for name in _INS:
        x = _np.ascontiguousarray(inputs[name])
        arrays[f"in_{name}"] = x
        args[name] = nc.dram_tensor(f"in_{name}", x.shape, _mybir.dt.from_np(x.dtype), kind="ExternalInput").ap()
    shape = inputs["L0_attn_x"].shape
    for name, x in zip(("rotation_cos", "rotation_sin"), rotation_tables(shape[1], inputs["L1_attn_wq"].shape[0])):
        arrays[name] = x
        args[name] = nc.dram_tensor(name, x.shape, _mybir.dt.float32, kind="ExternalInput").ap()
    out = nc.dram_tensor("out_x", shape, _mybir.dt.float32, kind="ExternalOutput").ap()
    program(nc, args, out)
    r = _run(nc, [arrays], core_ids=[0])
    return r.results[0]["out_x"]
```
